# Optimizing a Trainium2 kernel written in Bass

```python
import numpy as np
import jax
import jax.numpy as jnp

def _softmax(x, axis=-1):
    return jax.nn.softmax(x, axis=axis)

def _gelu(x):
    return jax.nn.gelu(x, approximate=True)

def _silu(x):
    return jax.nn.silu(x)

def _sigmoid(x):
    return jax.nn.sigmoid(x)

def _layernorm(x, axis=-1, eps=1e-05):
    m = jnp.mean(x, axis=axis, keepdims=True)
    v = jnp.var(x, axis=axis, keepdims=True)
    return (x - m) / jnp.sqrt(v + eps)

def _scatter_add(tgt, idx, src, axis=0):
    return tgt.at[idx].add(src)

def _segment_sum(src, seg, n):
    return jax.ops.segment_sum(src, seg, n)
kernel_name = 'mk_recurrent_d1_jaxref_r8_bba3f3'

def setup_inputs(seed: int=0):
    np.random.seed(seed)
    _w = jnp.asarray

    def _L0_attn_setup():
        import jax, jax.numpy as jnp
        import numpy as np
        HEADS = 16
        DIM_HEAD = 128
        SCALE = 16.0
        EPS = 1e-05

        def _layernorm(x, g):
            mu = jnp.mean(x, axis=-1, keepdims=True)
            var = jnp.mean((x - mu) ** 2, axis=-1, keepdims=True)
            return (x - mu) * jax.lax.rsqrt(var + EPS) * g

        def _l2norm(t):
            return t * jax.lax.rsqrt(jnp.sum(t * t, axis=-1, keepdims=True) + 1e-12)
        key = jax.random.key(seed)
        ks = jax.random.split(key, 5)
        B, N, dim = (2, 256, 256)
        hidden = HEADS * DIM_HEAD
        x = jax.random.normal(ks[0], (B, N, dim), dtype=jnp.float32)
        g_norm = jnp.ones((dim,), dtype=jnp.float32)
        Wq = jax.random.normal(ks[1], (dim, hidden), dtype=jnp.float32) * dim ** (-0.5)
        Wkv = jax.random.normal(ks[2], (dim, 2 * DIM_HEAD), dtype=jnp.float32) * dim ** (-0.5)
        Wout = jax.random.normal(ks[3], (hidden, dim), dtype=jnp.float32) * hidden ** (-0.5)
        g_out = jnp.ones((dim,), dtype=jnp.float32)
        return {'x': x, 'g_norm': g_norm, 'Wq': Wq, 'Wkv': Wkv, 'Wout': Wout, 'g_out': g_out}
    _L0_attn_in = _L0_attn_setup()

    def _L0_ffn_setup():
        import jax, jax.numpy as jnp
        import numpy as np
        B, T, D, E, F, K, ND = (2, 32, 256, 64, 64, 4, 4)
        H = F * K
        N_SHARED = 2
        key = jax.random.key(seed)
        ks = jax.random.split(key, 12)
        s = lambda k, shape: jax.random.normal(k, shape, jnp.float32) * 0.02
        x = jax.random.normal(ks[0], (B, T, D), jnp.float32)
        Wr = s(ks[1], (E, D))
        router_bias = jnp.zeros((E,), jnp.float32)
        affinity = s(ks[2], (E, ND))
        te_W1 = s(ks[3], (D // 2, D))
        te_b1 = jnp.zeros((D // 2,), jnp.float32)
        te_W2 = s(ks[4], (ND, D // 2))
        te_b2 = jnp.zeros((ND,), jnp.float32)
        Wg = s(ks[5], (E, D, F))
        Wu = s(ks[6], (E, D, F))
        Wd = s(ks[7], (E, F, D))
        Sg = s(ks[8], (N_SHARED, D, H))
        Su = s(ks[9], (N_SHARED, D, H))
        Sd = s(ks[10], (N_SHARED, H, D))
        return dict(x=x, Wr=Wr, router_bias=router_bias, affinity=affinity, te_W1=te_W1, te_b1=te_b1, te_W2=te_W2, te_b2=te_b2, Wg=Wg, Wu=Wu, Wd=Wd, Sg=Sg, Su=Su, Sd=Sd)
    _L0_ffn_in = _L0_ffn_setup()
    _d = {'L0_attn_x': _L0_attn_in['x'], 'L0_attn_g_norm': _L0_attn_in['g_norm'], 'L0_attn_Wq': _L0_attn_in['Wq'], 'L0_attn_Wkv': _L0_attn_in['Wkv'], 'L0_attn_Wout': _L0_attn_in['Wout'], 'L0_attn_g_out': _L0_attn_in['g_out'], 'L0_ffn_Wr': _L0_ffn_in['Wr'], 'L0_ffn_router_bias': _L0_ffn_in['router_bias'], 'L0_ffn_affinity': _L0_ffn_in['affinity'], 'L0_ffn_te_W1': _L0_ffn_in['te_W1'], 'L0_ffn_te_b1': _L0_ffn_in['te_b1'], 'L0_ffn_te_W2': _L0_ffn_in['te_W2'], 'L0_ffn_te_b2': _L0_ffn_in['te_b2'], 'L0_ffn_Wg': _L0_ffn_in['Wg'], 'L0_ffn_Wu': _L0_ffn_in['Wu'], 'L0_ffn_Wd': _L0_ffn_in['Wd'], 'L0_ffn_Sg': _L0_ffn_in['Sg'], 'L0_ffn_Su': _L0_ffn_in['Su'], 'L0_ffn_Sd': _L0_ffn_in['Sd']}
    _x0 = _d['L0_attn_x']
    _d['L0_attn_x'] = jax.random.normal(jax.random.fold_in(jax.random.key(seed), 1), (8, 256, 256), dtype=_x0.dtype)
    del _x0
    return _d

def reference(L0_attn_x, L0_attn_g_norm, L0_attn_Wq, L0_attn_Wkv, L0_attn_Wout, L0_attn_g_out, L0_ffn_Wr, L0_ffn_router_bias, L0_ffn_affinity, L0_ffn_te_W1, L0_ffn_te_b1, L0_ffn_te_W2, L0_ffn_te_b2, L0_ffn_Wg, L0_ffn_Wu, L0_ffn_Wd, L0_ffn_Sg, L0_ffn_Su, L0_ffn_Sd):

    def _L0_attn_ref(x, g_norm, Wq, Wkv, Wout, g_out):
        import jax, jax.numpy as jnp
        import numpy as np
        HEADS = 16
        DIM_HEAD = 128
        SCALE = 16.0
        EPS = 1e-05

        def _layernorm(x, g):
            mu = jnp.mean(x, axis=-1, keepdims=True)
            var = jnp.mean((x - mu) ** 2, axis=-1, keepdims=True)
            return (x - mu) * jax.lax.rsqrt(var + EPS) * g

        def _l2norm(t):
            return t * jax.lax.rsqrt(jnp.sum(t * t, axis=-1, keepdims=True) + 1e-12)
        B, N, dim = x.shape
        xn = _layernorm(x, g_norm)
        q = xn @ Wq
        kv = xn @ Wkv
        k, v = (kv[..., :DIM_HEAD], kv[..., DIM_HEAD:])
        q = q.reshape(B, N, HEADS, DIM_HEAD).transpose(0, 2, 1, 3)
        q = q * SCALE
        q = _l2norm(q)
        k = _l2norm(k)
        s = jnp.sqrt(SCALE).astype(x.dtype)
        q = q * s
        k = k * s
        sim = jnp.einsum('bhid,bjd->bhij', q, k)
        attn = jax.nn.softmax(sim.astype(jnp.float32), axis=-1).astype(sim.dtype)
        out = jnp.einsum('bhij,bjd->bhid', attn, v)
        out = out.transpose(0, 2, 1, 3).reshape(B, N, HEADS * DIM_HEAD)
        out = out @ Wout
        return _layernorm(out, g_out)

    def _L0_ffn_ref(x, Wr, router_bias, affinity, te_W1, te_b1, te_W2, te_b2, Wg, Wu, Wd, Sg, Su, Sd):
        import jax, jax.numpy as jnp
        import numpy as np
        B, T, D, E, F, K, ND = (2, 32, 256, 64, 64, 4, 4)
        H = F * K
        N_SHARED = 2
        b, t, d = x.shape
        n = b * t
        flat = x.reshape(n, d)
        xm = x.mean(axis=1)
        h1 = jax.nn.gelu(xm @ te_W1.T + te_b1, approximate=False)
        task_dist = jax.nn.softmax(h1 @ te_W2.T + te_b2, axis=-1)
        dom = task_dist @ affinity.T
        logits = (flat @ Wr.T).reshape(b, t, E) + 0.5 * dom[:, None, :]
        logits = logits.reshape(n, E)
        scores = jax.nn.softmax(logits, axis=-1)
        _, topk_idx = jax.lax.top_k(logits + router_bias, K)
        topk_scores = jnp.take_along_axis(scores, topk_idx, axis=-1)
        topk_scores = topk_scores / (topk_scores.sum(-1, keepdims=True) + 1e-08)
        combine = jnp.zeros((n, E), x.dtype).at[jnp.arange(n)[:, None], topk_idx].add(topk_scores)
        g = jnp.einsum('nd,edf->enf', flat, Wg)
        u = jnp.einsum('nd,edf->enf', flat, Wu)
        h = jax.nn.silu(g) * u
        hw = h * combine.T[:, :, None]
        out = jnp.einsum('enf,efd->nd', hw, Wd)
        for i in range(Sg.shape[0]):
            sh = jax.nn.silu(flat @ Sg[i]) * (flat @ Su[i])
            out = out + sh @ Sd[i]
        return out.reshape(b, t, d)
    x = L0_attn_x
    xn = _layernorm(x, axis=-1)
    s = _L0_attn_ref(xn, L0_attn_g_norm, L0_attn_Wq, L0_attn_Wkv, L0_attn_Wout, L0_attn_g_out)
    g = _silu(_L0_ffn_ref(xn, L0_ffn_Wr, L0_ffn_router_bias, L0_ffn_affinity, L0_ffn_te_W1, L0_ffn_te_b1, L0_ffn_te_W2, L0_ffn_te_b2, L0_ffn_Wg, L0_ffn_Wu, L0_ffn_Wd, L0_ffn_Sg, L0_ffn_Su, L0_ffn_Sd))
    x = x + s * g
    return x

_drawn_inputs = setup_inputs


def setup_inputs(seed=0):
    import zlib

    import numpy as np

    out = dict(_drawn_inputs(seed))
    spreads = {'L0_attn_g_norm': (1.0, 0.6),
     'L0_attn_g_out': (1.0, 0.6),
     'L0_ffn_router_bias': (0.0, 0.8),
     'L0_ffn_te_b1': (0.0, 0.8),
     'L0_ffn_te_b2': (0.0, 0.8)}
    factors = {'L0_attn_Wq': 4.836,
     'L0_attn_Wkv': 4.546,
     'L0_attn_Wout': 4.531,
     'L0_ffn_Wr': 8.0,
     'L0_ffn_affinity': 8.0,
     'L0_ffn_te_W1': 54.404,
     'L0_ffn_te_W2': 8.0,
     'L0_ffn_Wg': 8.0,
     'L0_ffn_Wu': 8.0,
     'L0_ffn_Wd': 8.0,
     'L0_ffn_Sg': 4.652,
     'L0_ffn_Su': 4.585,
     'L0_ffn_Sd': 4.598}
    for name, (base, spread) in spreads.items():
        noise = np.random.default_rng([zlib.crc32(name.encode()), seed]).standard_normal(out[name].shape)
        drawn = base * np.exp(spread * noise) if base else spread * noise
        out[name] = jnp.asarray(drawn.astype(out[name].dtype))
    for name, factor in factors.items():
        out[name] = (out[name] * factor).astype(out[name].dtype)
    return out
```

```python
from contextlib import ExitStack

import concourse.bass as bass
from concourse import mybir

F32 = mybir.dt.float32
F32R = mybir.dt.float32r
U32 = mybir.dt.uint32
ALU = mybir.AluOpType
ACT = mybir.ActivationFunctionType
AX_X = mybir.AxisListType.X

P = 128
EPS = 1e-5
L2_EPS = 1e-12
SCALE = 16.0
TOPK = 4


def build(nc, x, wq, wkv, wout, g_norm, g_out, wr_t, r_bias, aff_t, w1_t, b1, w2_t, b2, w_units, ident_in, iota_in, out):
    B, N, D = x.shape
    HID = wq.shape[1]
    DH = P
    HEADS = HID // DH
    E = wr_t.shape[1]
    ND = w2_t.shape[1]
    UNITS = w_units.shape[0]
    TOK = B * N
    TT = N // P
    KC = D // P
    TILES = TOK // P
    HP = HEADS // 2
    PAIR = 2 * N
    TG = 512
    NTG = TOK // TG
    WCOLS = w_units.shape[2]
    assert TT == 2 and KC == 2 and HP == 8 and PAIR == 512

    x_rows = x.rearrange("b (t p) d -> p (b t) d", p=P)
    out_rows = out.rearrange("b (t p) d -> p (b t) d", p=P)
    combine_dram = nc.dram_tensor("combine_rows", (2 * UNITS, TOK), F32, kind="Internal").ap()

    with ExitStack() as whole:
        def sem(name):
            return whole.enter_context(nc.semaphore(name))

        def sbuf(ctx, name, shape, dt=F32):
            return ctx.enter_context(nc.sbuf_tensor(name, shape, dt))

        def psum(ctx, name, shape, dt=F32):
            return ctx.enter_context(nc.psum_tensor(name, shape, dt))

        def bcast(a, shape):
            return a.to_broadcast(shape)

        x_sb = sbuf(whole, "x_sb", [P, TILES, D])
        xn_t = sbuf(whole, "xn_t", [P, KC, TOK])
        attn_out = sbuf(whole, "attn_out", [P, TILES, D])
        ident = sbuf(whole, "ident", [P, P])
        minus_half = sbuf(whole, "minus_half", [P, 8])
        spare = sbuf(whole, "spare", [P, 8])

        attention = ExitStack()
        xa_t = sbuf(attention, "xa_t", [P, KC, TOK])
        wq_hi = sbuf(attention, "wq_hi", [P, KC, HID], F32R)
        wq_lo = sbuf(attention, "wq_lo", [P, KC, HID], F32R)
        wkv_hi = sbuf(attention, "wkv_hi", [P, KC, 2 * DH], F32R)
        wkv_lo = sbuf(attention, "wkv_lo", [P, KC, 2 * DH], F32R)
        wo_hi = sbuf(attention, "wo_hi", [P, HEADS, D], F32R)
        wo_lo = sbuf(attention, "wo_lo", [P, HEADS, D], F32R)
        g_out_b = sbuf(attention, "g_out_b", [P, D])

        prep = ExitStack()
        wo_raw = sbuf(prep, "wo_raw", [P, HEADS, D])
        wkv_raw = sbuf(prep, "wkv_raw", [P, KC, 2 * DH])
        xn = sbuf(prep, "xn", [P, TT, D])
        xa = sbuf(prep, "xa", [P, TT, D])
        xn_stat = sbuf(prep, "xn_stat", [P, KC, N])
        g_col = sbuf(prep, "g_col", [P, KC])
        wr_sb = sbuf(prep, "wr_sb", [P, KC, E])
        w1_sb = sbuf(prep, "w1_sb", [P, KC, P])
        b1_sb = sbuf(prep, "b1_sb", [P, 1])
        w2_sb = sbuf(prep, "w2_sb", [P, ND])
        b2_b = sbuf(prep, "b2_b", [P, ND])
        aff_b = sbuf(prep, "aff_b", [P, ND, E])
        rbias_b = sbuf(prep, "rbias_b", [P, E])
        iota_b = sbuf(prep, "iota_b", [P, E])
        stats = sbuf(prep, "stats", [P, TT, 6])
        meanvar = sbuf(prep, "meanvar", [P, TT, 2])
        var_eps = sbuf(prep, "var_eps", [P, TT])
        rstd = sbuf(prep, "rstd", [P, TT])
        x_sum = sbuf(prep, "x_sum", [P, KC, B])
        raw_logits = sbuf(prep, "raw_logits", [P, TILES, E])
        h1_rep = sbuf(prep, "h1_rep", [P, B, P])
        task = sbuf(prep, "task", [P, B, ND])
        task_s = sbuf(prep, "task_s", [P, B])
        dom = sbuf(prep, "dom", [P, B, E])
        dom_part = sbuf(prep, "dom_part", [P, B, E])
        choice = sbuf(prep, "choice", [P, TILES, E])
        top = sbuf(prep, "top", [P, TILES, 8])
        top_at = sbuf(prep, "top_at", [P, TILES, 8], U32)
        top_f = sbuf(prep, "top_f", [P, TILES, 8])
        mask = sbuf(prep, "mask", [P, TILES, E])
        hit = sbuf(prep, "hit", [P, TILES, E])
        row = sbuf(prep, "row", [P, 3, TILES])
        ones_rows = sbuf(prep, "ones_rows", [8, TOK])
        combine_t = sbuf(prep, "combine_t", [E, TOK])
        wq_raw = attn_out[:, :, :].rearrange("p t d -> p (t d)").rearrange("p (c n) -> p c n", c=KC)

        prep_ps = ExitStack()
        ps_xn = psum(prep_ps, "ps_xn", [P, KC, N])
        ps_xa = psum(prep_ps, "ps_xa", [P, KC, N])
        ps_logits = psum(prep_ps, "ps_logits", [P, TT, E])
        ps_h1 = psum(prep_ps, "ps_h1", [P, B])
        ps_task = psum(prep_ps, "ps_task", [P, B, ND])
        ps_comb = psum(prep_ps, "ps_comb", [E, 512])

        x_loaded = sem("x_loaded")
        const_loaded = sem("const_loaded")
        wq_loaded = sem("wq_loaded")
        wkv_loaded = sem("wkv_loaded")
        wo_loaded = sem("wo_loaded")
        half_set = sem("half_set")
        ones_set = sem("ones_set")
        ln_step = sem("ln_step")
        var_ready = sem("var_ready")
        rstd_ready = sem("rstd_ready")
        xn_ready = sem("xn_ready")
        xa_ready = sem("xa_ready")
        xn_turned = sem("xn_turned")
        xa_turned = sem("xa_turned")
        xn_copied = sem("xn_copied")
        xn_summed = sem("xn_summed")
        xa_copied = sem("xa_copied")
        logits_done = sem("logits_done")
        logits_copied = sem("logits_copied")
        h1_done = sem("h1_done")
        h1_ready = sem("h1_ready")
        task_done = sem("task_done")
        task_max = sem("task_max")
        task_exp = sem("task_exp")
        choice_sub = sem("choice_sub")
        choice_exp = sem("choice_exp")
        comb_ready = sem("comb_ready")
        comb_turned = sem("comb_turned")
        comb_copied = sem("comb_copied")
        comb_stored = sem("comb_stored")
        hi_split = sem("hi_split")
        lo_split = sem("lo_split")

        LN_LINKS = 8
        with nc.Block() as block:
            @block.sync
            def _(sp):
                for b in range(B):
                    sp.dma_start(x_sb[:, b * TT:(b + 1) * TT, :], x_rows[:, b * TT:(b + 1) * TT, :]).then_inc(x_loaded, 16)
                sp.dma_start(wq_raw, wq.rearrange("(c p) n -> p c n", p=P)).then_inc(wq_loaded, 16)
                sp.dma_start(wkv_raw[:, :, :], wkv.rearrange("(c p) n -> p c n", p=P)).then_inc(wkv_loaded, 16)
                sp.dma_start(wo_raw[:, :, :], wout.rearrange("(h p) n -> p h n", p=P)).then_inc(wo_loaded, 16)
                sp.wait_ge(ones_set, 1)
                for r in range(E, 2 * UNITS, 8):
                    n = min(8, 2 * UNITS - r)
                    sp.dma_start(combine_dram[r:r + n, :], ones_rows[0:n, :]).then_inc(comb_stored, 16)
                sp.wait_ge(comb_copied, 4)
                sp.dma_start(combine_dram[0:E, :], combine_t[:, :]).then_inc(comb_stored, 16)
                sp.wait_ge(comb_stored, 32)

            @block.scalar
            def _(act):
                def row_b(a, n):
                    return a.unsqueeze(0).to_broadcast([P, n])
                act.dma_start(ident[:, :], ident_in).then_inc(const_loaded, 16)
                act.dma_start(g_col[:, :], g_norm).then_inc(const_loaded, 16)
                act.dma_start(wr_sb[:, :, :], wr_t.rearrange("(c p) e -> p c e", p=P)).then_inc(const_loaded, 16)
                act.dma_start(w1_sb[:, :, :], w1_t.rearrange("(c p) e -> p c e", p=P)).then_inc(const_loaded, 16)
                act.dma_start(b1_sb[:, :], b1).then_inc(const_loaded, 16)
                act.dma_start(w2_sb[:, :], w2_t).then_inc(const_loaded, 16)
                act.dma_start(b2_b[:, :], row_b(b2, ND)).then_inc(const_loaded, 16)
                act.dma_start(rbias_b[:, :], row_b(r_bias, E)).then_inc(const_loaded, 16)
                act.dma_start(iota_b[:, :], row_b(iota_in, E)).then_inc(const_loaded, 16)
                act.dma_start(g_out_b[:, :], row_b(g_out, D)).then_inc(const_loaded, 16)
                act.dma_start(aff_b[:, :, :].rearrange("p a e -> p (a e)"), row_b(aff_t.rearrange("a e -> (a e)"), ND * E)).then_inc(const_loaded, 16)
                act.wait_ge(const_loaded, 16 * 11)
                with act.Fori(0, B) as b:
                    act.wait_ge(xn_turned, b + 1)
                    nc.scalar.activation(xn_t[:, :, bass.ds(b * N, N)], ps_xn[:, :, :], ACT.Copy)
                    act.wait_ge(logits_done, b + 1)
                    act.wait_ge(xn_summed, b + 1)
                    nc.scalar.activation(xn_stat[:, :, :], ps_xn[:, :, :], ACT.Copy).then_inc(xn_copied, 1)
                    act.wait_ge(xa_turned, b + 1)
                    for c in range(KC):
                        last = nc.scalar.activation(xa_t[:, c, bass.ds(b * N, N)], ps_xa[:, c, :], ACT.Copy, scale=g_col[:, c:c + 1])
                    last.then_inc(xa_copied, 1)
                    act.wait_ge(logits_done, b + 2)
                    nc.scalar.activation(raw_logits[:, bass.ds(b * TT, TT), :], ps_logits[:, :, :], ACT.Copy).then_inc(logits_copied, 1)
                act.wait_ge(h1_done, 1)
                nc.scalar.activation(h1_rep[:, :, :], bcast(ps_h1[:, :].unsqueeze(2), [P, B, P]), ACT.Gelu,
                                     bias=b1_sb[:, 0:1], scale=1.0 / N).then_inc(h1_ready, 1)
                act.wait_ge(wq_loaded, 16)
                nc.scalar.activation(wq_hi[:, :, :], wq_raw, ACT.Copy).then_inc(hi_split, 1)
                act.wait_ge(wkv_loaded, 16)
                nc.scalar.activation(wkv_hi[:, :, :], wkv_raw[:, :, :], ACT.Copy).then_inc(hi_split, 1)
                act.wait_ge(wo_loaded, 16)
                nc.scalar.activation(wo_hi[:, :, :], wo_raw[:, :, :], ACT.Copy).then_inc(hi_split, 1)
                act.wait_ge(task_max, 1)
                nc.scalar.activation(task[:, :, :], task[:, :, :], ACT.Exp).then_inc(task_exp, 1)
                act.wait_ge(choice_sub, 1)
                nc.scalar.activation(raw_logits[:, :, :], raw_logits[:, :, :], ACT.Exp).then_inc(choice_exp, 1)
                for q in range(4):
                    act.wait_ge(comb_turned, q + 1)
                    nc.scalar.activation(combine_t[:, q * 512:(q + 1) * 512], ps_comb[:, :], ACT.Copy).then_inc(comb_copied, 1)

            @block.gpsimd
            def _(pool):
                nc.gpsimd.memset(minus_half[:, :], -0.5).then_inc(half_set, 1)
                nc.gpsimd.memset(ones_rows[:, :], 1.0).then_inc(ones_set, 1)
                pool.wait_ge(half_set, 1)
                with pool.Fori(0, B) as b:
                    for k in range(2):
                        pool.wait_ge(var_ready, 2 * b + k + 1)
                        nc.gpsimd.tensor_tensor(rstd[:, :], var_eps[:, :], minus_half[:, 0:TT], ALU.pow).then_inc(rstd_ready, 1)
                pool.wait_ge(hi_split, 3)
                nc.gpsimd.tensor_tensor(wo_lo[:, :, :], wo_raw[:, :, :], wo_hi[:, :, :].bitcast(F32), ALU.subtract).then_inc(lo_split, 1)

            @block.tensor
            def _(pe):
                pe.wait_ge(const_loaded, 16 * 11)
                with pe.Fori(0, B) as b:
                    pe.wait_ge(xn_ready, b + 1)
                    pe.wait_ge(xn_copied, b + 1)
                    for c in range(KC):
                        for t in range(TT):
                            last = nc.tensor.transpose(ps_xn[:, c, t * P:(t + 1) * P], xn[:, t, c * P:(c + 1) * P], ident[:, :])
                    last.then_inc(xn_turned, 1)
                    pe.wait_ge(xa_ready, b + 1)
                    pe.wait_ge(xa_copied, b + 1)
                    for c in range(KC):
                        for t in range(TT):
                            last = nc.tensor.transpose(ps_xa[:, c, t * P:(t + 1) * P], xa[:, t, c * P:(c + 1) * P], ident[:, :])
                    last.then_inc(xa_turned, 1)
                    pe.wait_ge(xn_copied, b + 2)
                    pe.wait_ge(logits_copied, b + 1)
                    for t in range(TT):
                        for c in range(KC):
                            last = nc.tensor.matmul(ps_logits[:, t, :], xn_stat[:, c, t * P:(t + 1) * P], wr_sb[:, c, :],
                                                    start=(c == 0), stop=(c == KC - 1))
                    last.then_inc(logits_done, 1)
                pe.wait_ge(xn_summed, B + 1)
                for c in range(KC):
                    last = nc.tensor.matmul(ps_h1[:, :], w1_sb[:, c, :], x_sum[:, c, :], start=(c == 0), stop=(c == KC - 1))
                last.then_inc(h1_done, 1)
                pe.wait_ge(h1_ready, 1)
                for b in range(B):
                    last = nc.tensor.matmul(ps_task[:, b, :], h1_rep[:, b, :], w2_sb[:, :], start=True, stop=True)
                last.then_inc(task_done, 1)
                pe.wait_ge(comb_ready, 1)
                for q in range(4):
                    if q:
                        pe.wait_ge(comb_copied, q)
                    for t in range(4):
                        last = nc.tensor.transpose(ps_comb[:, t * P:(t + 1) * P], choice[:, 4 * q + t, :], ident[:, :])
                    last.then_inc(comb_turned, 1)

            @block.vector
            def _(dve):
                for k, s in enumerate((xn_summed, xn_copied, xa_copied, logits_done, logits_copied)):
                    nc.vector.memset(spare[:, k:k + 1], 0.0).then_inc(s, 1)
                dve.wait_ge(x_loaded, 16 * B)
                with dve.Fori(0, B) as b:
                    links = [0]

                    def link(ins):
                        links[0] += 1
                        ins.then_inc(ln_step, 1)
                        dve.wait_ge(ln_step, b * LN_LINKS + links[0])

                    for k, (dst, ready) in enumerate(((xn, xn_ready), (xa, xa_ready))):
                        for t in range(TT):
                            src = x_sb[:, bass.ds(b * TT + t, 1), :].rearrange("p a d -> p (a d)") if k == 0 else xn[:, t, :]
                            last = nc.vector.bn_stats(stats[:, t, :], src)
                        link(last)
                        nc.vector.memset(spare[:, 7:8], 0.0)
                        for t in range(TT):
                            last = nc.vector.bn_aggr(meanvar[:, t, :], stats[:, t, :])
                        link(last)
                        nc.vector.tensor_scalar(var_eps[:, :], meanvar[:, :, 1], EPS, None, ALU.add).then_inc(var_ready, 1)
                        dve.wait_ge(rstd_ready, 2 * b + k + 1)
                        for t in range(TT):
                            src = x_sb[:, bass.ds(b * TT + t, 1), :].rearrange("p a d -> p (a d)") if k == 0 else xn[:, t, :]
                            last = nc.vector.tensor_scalar(dst[:, t, :], src, meanvar[:, t, 0:1], rstd[:, t:t + 1], ALU.subtract, ALU.mult)
                            if t == 0:
                                link(last)
                        last.then_inc(ready, 1)
                        dve.wait_ge(ready, b + 1)
                        if k == 0:
                            dve.wait_ge(xn_copied, b + 2)
                            red = nc.vector.tensor_reduce(x_sum[:, :, bass.ds(b, 1)].rearrange("p c o -> p (c o)"), xn_stat[:, :, :], AX_X, ALU.add)
                            red.then_inc(xn_summed, 1)
                            link(nc.vector.memset(spare[:, 5:6], 0.0))
                    dve.wait_ge(xa_turned, b + 1)
                    link(nc.vector.memset(spare[:, 6:7], 0.0))
                    assert links[0] == LN_LINKS, links

                chain = [0]
                route_step = sem("route_step")

                def then(ins):
                    chain[0] += 1
                    ins.then_inc(route_step, 1)
                    dve.wait_ge(route_step, chain[0])

                dve.wait_ge(hi_split, 2)
                nc.vector.tensor_tensor(wq_lo[:, :, :], wq_raw, wq_hi[:, :, :].bitcast(F32), ALU.subtract)
                nc.vector.tensor_tensor(wkv_lo[:, :, :], wkv_raw[:, :, :], wkv_hi[:, :, :].bitcast(F32), ALU.subtract)
                dve.wait_ge(task_done, 1)
                then(nc.vector.tensor_tensor(task[:, :, :], ps_task[:, :, :], bcast(b2_b[:, :].unsqueeze(1), [P, B, ND]), ALU.add))
                then(nc.vector.tensor_reduce(task_s[:, :], task[:, :, :], AX_X, ALU.max))
                nc.vector.tensor_tensor(task[:, :, :], task[:, :, :], bcast(task_s[:, :].unsqueeze(2), [P, B, ND]), ALU.subtract).then_inc(task_max, 1)
                dve.wait_ge(task_exp, 1)
                then(nc.vector.tensor_reduce(task_s[:, :], task[:, :, :], AX_X, ALU.add))
                then(nc.vector.reciprocal(task_s[:, :], task_s[:, :]))
                then(nc.vector.scalar_tensor_tensor(task[:, :, :], task[:, :, :], 0.5, bcast(task_s[:, :].unsqueeze(2), [P, B, ND]), ALU.mult, ALU.mult))
                for a in range(ND):
                    dst = dom if a == 0 else dom_part
                    then(nc.vector.tensor_tensor(dst[:, :, :], bcast(task[:, :, a].unsqueeze(2), [P, B, E]),
                                                 bcast(aff_b[:, a, :].unsqueeze(1), [P, B, E]), ALU.mult))
                    if a:
                        then(nc.vector.tensor_tensor(dom[:, :, :], dom[:, :, :], dom_part[:, :, :], ALU.add))
                dve.wait_ge(logits_copied, B + 1)
                logits4 = raw_logits[:, :, :].rearrange("p (b t) e -> p b t e", t=TT)
                for t in range(TT):
                    then(nc.vector.tensor_tensor(logits4[:, :, t, :], logits4[:, :, t, :], dom[:, :, :], ALU.add))
                then(nc.vector.tensor_tensor(choice[:, :, :], raw_logits[:, :, :], bcast(rbias_b[:, :].unsqueeze(1), [P, TILES, E]), ALU.add))
                then(nc.vector.tensor_reduce(row[:, 0, :], raw_logits[:, :, :], AX_X, ALU.max))
                nc.vector.tensor_tensor(raw_logits[:, :, :], raw_logits[:, :, :], bcast(row[:, 0, :].unsqueeze(2), [P, TILES, E]), ALU.subtract).then_inc(choice_sub, 1)
                for t in range(TILES):
                    then(nc.vector.max(top[:, t, :], choice[:, t, :]))
                    last = nc.vector.max_index(top_at[:, t, :], top[:, t, :], choice[:, t, :])
                then(last)
                then(nc.vector.tensor_copy(top_f[:, :, :], top_at[:, :, :]))
                for k in range(TOPK):
                    dst = mask if k == 0 else hit
                    then(nc.vector.tensor_tensor(dst[:, :, :], bcast(iota_b[:, :].unsqueeze(1), [P, TILES, E]),
                                                 bcast(top_f[:, :, k].unsqueeze(2), [P, TILES, E]), ALU.is_equal))
                    if k:
                        then(nc.vector.tensor_tensor(mask[:, :, :], mask[:, :, :], hit[:, :, :], ALU.add))
                dve.wait_ge(choice_exp, 1)
                then(nc.vector.tensor_reduce(row[:, 1, :], raw_logits[:, :, :], AX_X, ALU.add))
                then(nc.vector.tensor_tensor(mask[:, :, :], mask[:, :, :], raw_logits[:, :, :], ALU.mult))
                then(nc.vector.tensor_reduce(row[:, 0, :], mask[:, :, :], AX_X, ALU.add))
                then(nc.vector.scalar_tensor_tensor(row[:, 2, :], row[:, 1, :], 1e-8, row[:, 0, :], ALU.mult, ALU.add))
                then(nc.vector.reciprocal(row[:, 1, :], row[:, 2, :]))
                nc.vector.tensor_tensor(choice[:, :, :], mask[:, :, :], bcast(row[:, 1, :].unsqueeze(2), [P, TILES, E]), ALU.mult).then_inc(comb_ready, 1)
        prep_ps.close()
        prep.close()

        work = ExitStack()
        xs_hi = sbuf(work, "xs_hi", [P, KC, N], F32R)
        xs_lo = sbuf(work, "xs_lo", [P, KC, N], F32R)
        kv_rows = sbuf(work, "kv_rows", [P, TT, 2 * DH])
        k_sq = sbuf(work, "k_sq", [P, TT, DH])
        k_norm = sbuf(work, "k_norm", [P, TT, DH])
        kt_hi = sbuf(work, "kt_hi", [P, N], F32R)
        kt_lo = sbuf(work, "kt_lo", [P, N], F32R)
        VW = DH + 2
        v_hi = sbuf(work, "v_hi", [P, TT, VW], F32R)
        v_lo = sbuf(work, "v_lo", [P, TT, DH], F32R)
        ones2 = sbuf(work, "ones2", [P, TT, 2])
        q_sq = sbuf(work, "q_sq", [P, 4, DH])
        q_sum = sbuf(work, "q_sum", [P, 4])
        q_var = sbuf(work, "q_var", [P, 4])
        q_scale = sbuf(work, "q_scale", [P, 4])
        k_sum = sbuf(work, "k_sum", [P, 2])
        k_var = sbuf(work, "k_var", [P, 2])
        k_scale = sbuf(work, "k_scale", [P, 2])
        q_norm = sbuf(work, "q_norm", [P, TT, 2, DH])
        qt_hi = sbuf(work, "qt_hi", [P, 2, PAIR], F32R)
        qt_lo = sbuf(work, "qt_lo", [P, 2, PAIR], F32R)
        w_f = sbuf(work, "w_f", [P, TT, PAIR])
        w_hi = sbuf(work, "w_hi", [P, 2, TT, PAIR], F32R)
        w_lo = sbuf(work, "w_lo", [P, 2, TT, PAIR], F32R)
        w_rec = sbuf(work, "w_rec", [P, 4])
        o_norm = sbuf(work, "o_norm", [P, 4, DH])
        ot_hi = sbuf(work, "ot_hi", [P, 2, PAIR], F32R)
        ot_lo = sbuf(work, "ot_lo", [P, 2, PAIR], F32R)
        rows_out = sbuf(work, "rows_out", [P, TT, D])
        o_stats = sbuf(work, "o_stats", [P, TT, 6])
        o_mv = sbuf(work, "o_mv", [P, TT, 2])
        o_var = sbuf(work, "o_var", [P, TT])
        o_rstd = sbuf(work, "o_rstd", [P, TT])

        work_ps = ExitStack()
        ps_q = psum(work_ps, "ps_q", [P, TT, 2, DH])
        ps_t = psum(work_ps, "ps_t", [P, PAIR])
        ps_s = psum(work_ps, "ps_s", [P, TT, PAIR])
        ps_o = psum(work_ps, "ps_o", [P, 2, 512])
        ps_ot = psum(work_ps, "ps_ot", [P, PAIR])
        ps_acc = psum(work_ps, "ps_acc", [P, TT, D])
        o_at = ps_o[:, :, 0:2 * VW].rearrange("p h (t w) -> p h t w", t=2)

        v_ones = sem("v_ones")
        xs_ready = sem("xs_ready")
        xs_hi_ready = sem("xs_hi_ready")
        kv_done = sem("kv_done")
        kv_copied = sem("kv_copied")
        ksq_ready = sem("ksq_ready")
        ksum_ready = sem("ksum_ready")
        kscale_ready = sem("kscale_ready")
        knorm_ready = sem("knorm_ready")
        k_turned = sem("k_turned")
        kt_hi_ready = sem("kt_hi_ready")
        kt_lo_ready = sem("kt_lo_ready")
        v_ready = sem("v_ready")
        q_done = sem("q_done")
        qsq_ready = sem("qsq_ready")
        qsum_ready = sem("qsum_ready")
        qscale_ready = sem("qscale_ready")
        qnorm_ready = sem("qnorm_ready")
        q_turned = sem("q_turned")
        qt_hi_ready = sem("qt_hi_ready")
        qt_lo_ready = sem("qt_lo_ready")
        s_done = sem("s_done")
        w_ready = sem("w_ready")
        w_hi_ready = sem("w_hi_ready")
        w_lo_ready = sem("w_lo_ready")
        av_done = sem("av_done")
        rec_ready = sem("rec_ready")
        onorm_ready = sem("onorm_ready")
        o_turned = sem("o_turned")
        ot_hi_ready = sem("ot_hi_ready")
        ot_lo_ready = sem("ot_lo_ready")
        proj_done = sem("proj_done")
        acc_copied = sem("acc_copied")
        ln_out = sem("ln_out")
        ovar_ready = sem("ovar_ready")
        orstd_ready = sem("orstd_ready")
        k_link = sem("k_link")
        q_link = sem("q_link")
        v_hi_ready = sem("v_hi_ready")

        UNITS_A = B * HP

        def steps(eng, step):
            for hp in range(HP):
                step(0, hp)
            with eng.Fori(1, B) as b:
                for hp in range(HP):
                    step(b, hp)
            for hp in range(5):
                step(B, hp)

        def live(b, hp, lag):
            if not isinstance(b, int):
                return True
            return 0 <= HP * b + hp - lag < UNITS_A

        def started(b):
            return not isinstance(b, int) or b < B

        def first(b):
            return isinstance(b, int) and b == 0

        with nc.Block() as block:
            @block.tensor
            def _(pe):
                def mm3(dst, l_hi, l_lo, r_hi, r_lo, start, stop, **kw):
                    nc.tensor.matmul(dst, l_hi, r_hi, start=start, stop=False, **kw)
                    nc.tensor.matmul(dst, l_hi, r_lo, start=False, stop=False, **kw)
                    return nc.tensor.matmul(dst, l_lo, r_hi, start=False, stop=stop, **kw)

                def step(b, hp):
                    u = HP * b + hp
                    if hp == 0 and started(b):
                        pe.wait_ge(xs_ready, b + 1)
                        if not first(b):
                            pe.wait_ge(qnorm_ready, u)
                        for t in range(TT):
                            for c in range(KC):
                                cols = slice(t * P, (t + 1) * P)
                                last = mm3(ps_q[:, t, :, :], xs_hi[:, c, cols], xs_lo[:, c, cols],
                                           wkv_hi[:, c, :], wkv_lo[:, c, :], c == 0, c == KC - 1)
                        last.then_inc(kv_done, 1)
                    if live(b, hp, 2):
                        pe.wait_ge(qt_lo_ready, u - 1)
                        pe.wait_ge(qt_hi_ready, u - 1)
                        if hp == 2:
                            pe.wait_ge(kt_hi_ready, b + 1)
                            pe.wait_ge(kt_lo_ready, b + 1)
                        if live(b, hp, 3):
                            pe.wait_ge(w_ready, u - 2)
                        i = hp % 2
                        for t in range(TT):
                            cols = slice(t * P, (t + 1) * P)
                            last = mm3(ps_s[:, t, :], kt_hi[:, cols], kt_lo[:, cols], qt_hi[:, i, :], qt_lo[:, i, :], True, True)
                        last.then_inc(s_done, 1)
                    if hp == 1 and started(b):
                        pe.wait_ge(knorm_ready, b + 1)
                        if not first(b):
                            pe.wait_ge(qt_lo_ready, u - 1)
                            pe.wait_ge(qt_hi_ready, u - 1)
                        for t in range(TT):
                            last = nc.tensor.transpose(ps_t[:, t * P:(t + 1) * P], k_norm[:, t, :], ident[:, :])
                        last.then_inc(k_turned, 1)
                    if live(b, hp, 3):
                        pe.wait_ge(w_lo_ready, u - 2)
                        pe.wait_ge(w_hi_ready, u - 2)
                        if hp == 3:
                            pe.wait_ge(v_ready, b + 1)
                        if live(b, hp, 4):
                            pe.wait_ge(onorm_ready, u - 3)
                        i = (hp + 1) % 2
                        for h in range(2):
                            for t in range(TT):
                                cols = slice(h * N + t * P, h * N + (t + 1) * P)
                                for j in range(TT):
                                    nc.tensor.matmul(o_at[:, h, t, :], w_hi[:, i, j, cols], v_hi[:, j, :], start=(j == 0), stop=False)
                                    nc.tensor.matmul(o_at[:, h, t, 0:DH], w_hi[:, i, j, cols], v_lo[:, j, :], start=False, stop=False)
                                    last = nc.tensor.matmul(o_at[:, h, t, :], w_lo[:, i, j, cols], v_hi[:, j, :], start=False, stop=(j == TT - 1))
                        last.then_inc(av_done, 1)
                    if live(b, hp, 1):
                        pe.wait_ge(qnorm_ready, u)
                        if hp == 1 and started(b):
                            pe.wait_ge(kt_hi_ready, b + 1)
                            pe.wait_ge(kt_lo_ready, b + 1)
                        elif live(b, hp, 2):
                            pe.wait_ge(qt_hi_ready, u - 1)
                            pe.wait_ge(qt_lo_ready, u - 1)
                        for h in range(2):
                            for t in range(TT):
                                last = nc.tensor.transpose(ps_t[:, h * N + t * P:h * N + (t + 1) * P], q_norm[:, t, h, :], ident[:, :])
                        last.then_inc(q_turned, 1)
                    if started(b):
                        if hp == 0:
                            pe.wait_ge(kv_copied, b + 1)
                        else:
                            pe.wait_ge(qnorm_ready, u)
                        for t in range(TT):
                            for c in range(KC):
                                cols = slice(t * P, (t + 1) * P)
                                heads = slice(hp * 2 * DH, (hp + 1) * 2 * DH)
                                last = mm3(ps_q[:, t, :, :], xs_hi[:, c, cols], xs_lo[:, c, cols],
                                           wq_hi[:, c, heads], wq_lo[:, c, heads], c == 0, c == KC - 1)
                        last.then_inc(q_done, 1)
                    if live(b, hp, 4):
                        pe.wait_ge(onorm_ready, u - 3)
                        if live(b, hp, 5):
                            pe.wait_ge(ot_hi_ready, u - 4)
                            pe.wait_ge(ot_lo_ready, u - 4)
                        for k in range(4):
                            last = nc.tensor.transpose(ps_ot[:, k * P:(k + 1) * P], o_norm[:, k, :], ident[:, :])
                        last.then_inc(o_turned, 1)
                    if live(b, hp, 5):
                        pe.wait_ge(ot_hi_ready, u - 4)
                        pe.wait_ge(ot_lo_ready, u - 4)
                        unit = (hp - 5) % HP
                        if unit == 0 and not first(b):
                            pe.wait_ge(acc_copied, b)
                        i = unit % 2
                        for h in range(2):
                            for t in range(TT):
                                cols = slice(h * N + t * P, h * N + (t + 1) * P)
                                last = mm3(ps_acc[:, t, :], ot_hi[:, i, cols], ot_lo[:, i, cols], wo_hi[:, 2 * unit + h, :], wo_lo[:, 2 * unit + h, :],
                                           unit == 0 and h == 0 and t == 0, unit == HP - 1 and h == 1 and t == TT - 1, skip_group_check=True)
                        last.then_inc(proj_done, 1)

                steps(pe, step)

            @block.scalar
            def _(act):
                def step(b, hp):
                    u = HP * b + hp
                    if hp == 0 and started(b):
                        act.wait_ge(kv_done, b + 1)
                        if not first(b):
                            act.wait_ge(v_ready, b)
                            act.wait_ge(knorm_ready, b)
                        nc.scalar.activation(kv_rows[:, :, :], ps_q[:, :, :, :].rearrange("p t h d -> p t (h d)"), ACT.Copy).then_inc(kv_copied, 1)
                        act.wait_ge(kv_copied, b + 1)
                        nc.scalar.activation(k_sq[:, :, :], kv_rows[:, :, 0:DH], ACT.Square).then_inc(ksq_ready, 1)
                    if live(b, hp, 2):
                        act.wait_ge(s_done, u - 1)
                        if live(b, hp, 3):
                            act.wait_ge(w_lo_ready, u - 2)
                            act.wait_ge(w_hi_ready, u - 2)
                        nc.scalar.activation(w_f[:, :, :], ps_s[:, :, :], ACT.Exp).then_inc(w_ready, 1)
                        act.wait_ge(w_ready, u - 1)
                        if live(b, hp, 4):
                            act.wait_ge(av_done, u - 3)
                        nc.scalar.activation(w_hi[:, hp % 2, :, :], w_f[:, :, :], ACT.Copy).then_inc(w_hi_ready, 1)
                    if hp == 1 and started(b):
                        act.wait_ge(k_turned, b + 1)
                        nc.scalar.activation(kt_hi[:, :], ps_t[:, 0:N], ACT.Copy).then_inc(kt_hi_ready, 1)
                    if live(b, hp, 1):
                        act.wait_ge(q_turned, u)
                        if live(b, hp, 3):
                            act.wait_ge(s_done, u - 2)
                        nc.scalar.activation(qt_hi[:, (hp + 1) % 2, :], ps_t[:, :], ACT.Copy).then_inc(qt_hi_ready, 1)
                    if started(b):
                        act.wait_ge(q_done, u + 1)
                        if live(b, hp, 1):
                            act.wait_ge(qsum_ready, u)
                        nc.scalar.activation(q_sq[:, :, :], ps_q[:, :, :, :].rearrange("p t h d -> p (t h) d"), ACT.Square).then_inc(qsq_ready, 1)
                    if live(b, hp, 4):
                        act.wait_ge(o_turned, u - 3)
                        if live(b, hp, 6):
                            act.wait_ge(proj_done, u - 5)
                        nc.scalar.activation(ot_hi[:, hp % 2, :], ps_ot[:, :], ACT.Copy).then_inc(ot_hi_ready, 1)
                    if hp == 2 and started(b):
                        if not first(b):
                            act.wait_ge(av_done, HP * b)
                        nc.scalar.activation(v_hi[:, :, 0:DH], kv_rows[:, :, DH:2 * DH], ACT.Copy).then_inc(v_hi_ready, 1)
                    if hp == 4 and not first(b):
                        act.wait_ge(proj_done, HP * b)
                        act.wait_ge(ln_out, b)
                        nc.scalar.activation(rows_out[:, :, :], ps_acc[:, :, :], ACT.Copy).then_inc(acc_copied, 1)

                steps(act, step)

            @block.vector
            def _(dve):
                nc.vector.memset(ones2[:, :, :], 1.0).then_inc(v_ones, 1)
                nc.vector.memset(o_rstd[:, :], 0.0).then_inc(ln_out, 1)
                dve.wait_ge(v_ones, 1)
                nc.vector.tensor_copy(v_hi[:, :, DH:VW], ones2[:, :, :]).then_inc(v_ones, 1)

                def split_x(b):
                    cols = slice(b * N, (b + 1) * N) if isinstance(b, int) else bass.ds(b * N, N)
                    nc.vector.tensor_copy(xs_hi[:, :, :], xa_t[:, :, cols]).then_inc(xs_hi_ready, 1)
                    dve.wait_ge(xs_hi_ready, b + 1)
                    nc.vector.tensor_tensor(xs_lo[:, :, :], xa_t[:, :, cols], xs_hi[:, :, :].bitcast(F32), ALU.subtract).then_inc(xs_ready, 1)

                def step(b, hp):
                    u = HP * b + hp
                    if hp == 0 and started(b):
                        if not first(b):
                            dve.wait_ge(q_done, u)
                        split_x(b)
                        dve.wait_ge(ksq_ready, b + 1)
                        nc.vector.tensor_reduce(k_sum[:, :], k_sq[:, :, :], AX_X, ALU.add).then_inc(k_link, 1)
                        dve.wait_ge(k_link, b + 1)
                        nc.vector.tensor_scalar(k_var[:, :], k_sum[:, :], 1.0 / SCALE, L2_EPS / SCALE, ALU.mult, ALU.add).then_inc(ksum_ready, 1)
                    if hp == 1 and started(b):
                        dve.wait_ge(kscale_ready, b + 1)
                        if not first(b):
                            dve.wait_ge(k_turned, b)
                        nc.vector.tensor_tensor(k_norm[:, :, :], kv_rows[:, :, 0:DH], bcast(k_scale[:, :].unsqueeze(2), [P, TT, DH]),
                                                ALU.mult).then_inc(knorm_ready, 1)
                        dve.wait_ge(kt_hi_ready, b + 1)
                        nc.vector.tensor_tensor(kt_lo[:, :], ps_t[:, 0:N], kt_hi[:, :].bitcast(F32), ALU.subtract).then_inc(kt_lo_ready, 1)
                    if live(b, hp, 2):
                        dve.wait_ge(w_hi_ready, u - 1)
                        i = hp % 2
                        nc.vector.tensor_tensor(w_lo[:, i, :, :], w_f[:, :, :], w_hi[:, i, :, :].bitcast(F32), ALU.subtract).then_inc(w_lo_ready, 1)
                    if live(b, hp, 3):
                        dve.wait_ge(av_done, u - 2)
                        nc.vector.reciprocal(w_rec[:, :].rearrange("p (h t) -> p h t", h=2), o_at[:, :, :, DH]).then_inc(rec_ready, 1)
                        dve.wait_ge(rec_ready, u - 2)
                        if live(b, hp, 4):
                            dve.wait_ge(o_turned, u - 3)
                        nc.vector.tensor_tensor(o_norm[:, :, :].rearrange("p (h t) d -> p h t d", h=2), o_at[:, :, :, 0:DH],
                                                bcast(w_rec[:, :].rearrange("p (h t) -> p h t", h=2).unsqueeze(3), [P, 2, TT, DH]),
                                                ALU.mult).then_inc(onorm_ready, 1)
                    if live(b, hp, 1):
                        i = (hp + 1) % 2
                        dve.wait_ge(qt_hi_ready, u)
                        nc.vector.tensor_tensor(qt_lo[:, i, :], ps_t[:, :], qt_hi[:, i, :].bitcast(F32), ALU.subtract).then_inc(qt_lo_ready, 1)
                    if started(b):
                        dve.wait_ge(qsq_ready, u + 1)
                        nc.vector.tensor_reduce(q_sum[:, :], q_sq[:, :, :], AX_X, ALU.add).then_inc(q_link, 1)
                        dve.wait_ge(q_link, u + 1)
                        nc.vector.tensor_scalar(q_var[:, :], q_sum[:, :], 1.0 / SCALE, L2_EPS / (SCALE * SCALE * SCALE), ALU.mult, ALU.add).then_inc(qsum_ready, 1)
                    if live(b, hp, 4):
                        i = hp % 2
                        dve.wait_ge(ot_hi_ready, u - 3)
                        nc.vector.tensor_tensor(ot_lo[:, i, :], ps_ot[:, :], ot_hi[:, i, :].bitcast(F32), ALU.subtract).then_inc(ot_lo_ready, 1)
                    if started(b):
                        dve.wait_ge(qscale_ready, u + 1)
                        if live(b, hp, 1):
                            dve.wait_ge(q_turned, u)
                        nc.vector.tensor_tensor(q_norm[:, :, :, :].rearrange("p t h d -> p (t h) d"),
                                                ps_q[:, :, :, :].rearrange("p t h d -> p (t h) d"),
                                                bcast(q_scale[:, :].unsqueeze(2), [P, 4, DH]), ALU.mult).then_inc(qnorm_ready, 1)
                    if hp == 4 and not first(b):
                        dve.wait_ge(acc_copied, b)
                        for t in range(TT):
                            last = nc.vector.bn_stats(o_stats[:, t, :], rows_out[:, t, :])
                        last.then_inc(k_link2, 1)
                        dve.wait_ge(k_link2, 4 * b - 3)
                        nc.vector.memset(spare[:, 7:8], 0.0)
                        for t in range(TT):
                            last = nc.vector.bn_aggr(o_mv[:, t, :], o_stats[:, t, :])
                        last.then_inc(k_link2, 1)
                        dve.wait_ge(k_link2, 4 * b - 2)
                        nc.vector.tensor_scalar(o_var[:, :], o_mv[:, :, 1], EPS, None, ALU.add).then_inc(ovar_ready, 1)
                        dve.wait_ge(orstd_ready, b)
                        for t in range(TT):
                            last = nc.vector.tensor_scalar(rows_out[:, t, :], rows_out[:, t, :], o_mv[:, t, 0:1], o_rstd[:, t:t + 1], ALU.subtract, ALU.mult)
                            last.then_inc(k_link2, 1)
                        dve.wait_ge(k_link2, 4 * b)
                        if isinstance(b, int):
                            dst = attn_out[:, (b - 1) * TT:b * TT, :]
                        else:
                            dst = attn_out[:, bass.ds(b * TT - TT, TT), :]
                        nc.vector.tensor_tensor(dst, rows_out[:, :, :], bcast(g_out_b[:, :].unsqueeze(1), [P, TT, D]), ALU.mult).then_inc(ln_out, 1)

                k_link2 = sem("out_link")
                steps(dve, step)

            @block.gpsimd
            def _(pool):
                pool.wait_ge(v_ones, 2)

                def step(b, hp):
                    u = HP * b + hp
                    if hp == 0 and started(b):
                        pool.wait_ge(ksum_ready, b + 1)
                        nc.gpsimd.tensor_tensor(k_scale[:, :], k_var[:, :], minus_half[:, 0:2], ALU.pow).then_inc(kscale_ready, 1)
                    if started(b):
                        pool.wait_ge(qsum_ready, u + 1)
                        nc.gpsimd.tensor_tensor(q_scale[:, :], q_var[:, :], minus_half[:, 0:4], ALU.pow).then_inc(qscale_ready, 1)
                    if hp == 2 and started(b):
                        pool.wait_ge(v_hi_ready, b + 1)
                        nc.gpsimd.tensor_tensor(v_lo[:, :, :], kv_rows[:, :, DH:2 * DH], v_hi[:, :, 0:DH].bitcast(F32), ALU.subtract).then_inc(v_ready, 1)
                    if hp == 4 and not first(b):
                        pool.wait_ge(ovar_ready, b)
                        nc.gpsimd.tensor_tensor(o_rstd[:, :], o_var[:, :], minus_half[:, 0:TT], ALU.pow).then_inc(orstd_ready, 1)

                steps(pool, step)
        work_ps.close()
        work.close()
        attention.close()

        ffn = ExitStack()
        y_t = sbuf(ffn, "y_t", [P, KC, TOK])
        xh = sbuf(ffn, "xh", [P, KC, TOK], F32R)
        xl = sbuf(ffn, "xl", [P, KC, TOK], F32R)
        w_raw = sbuf(ffn, "w_raw", [P, 2, 2, WCOLS])
        wu_hi = sbuf(ffn, "wu_hi", [P, 2, 2, WCOLS], F32R)
        wu_lo = sbuf(ffn, "wu_lo", [P, 2, 2, WCOLS], F32R)
        comb = sbuf(ffn, "comb", [P, 2, 2, TOK])
        gate = sbuf(ffn, "gate", [P, 2, TG])
        hid = sbuf(ffn, "hid", [P, 2, TG])
        hid_c = sbuf(ffn, "hid_c", [P, 2, TG])
        hid_hi = sbuf(ffn, "hid_hi", [P, 2, TG], F32R)
        hid_lo = sbuf(ffn, "hid_lo", [P, 2, TG], F32R)
        ffn_ps = ExitStack()
        ps_g = psum(ffn_ps, "ps_g", [P, 2, TG])
        ps_u = psum(ffn_ps, "ps_u", [P, 2, TG])
        ps_y = psum(ffn_ps, "ps_y", [P, 2, KC, TG])

        GROUPS = UNITS // 2
        PER = 2 * NTG
        assert GROUPS % 2 == 0
        f_xh = sem("f_xh")
        f_xl = sem("f_xl")
        y_zero = sem("y_zero")
        wu_loaded = [sem(f"wu_loaded{i}") for i in range(2)]
        wu_hi_done = sem("wu_hi_done")
        wu_split = sem("wu_split")
        comb_loaded = [sem(f"comb_loaded{i}") for i in range(2)]
        comb_used = sem("comb_used")
        gu_done = sem("gu_done")
        gate_ready = sem("gate_ready")
        hid_ready = sem("hid_ready")
        hidc_ready = sem("hidc_ready")
        hid_hi_ready = sem("hid_hi_ready")
        hid_lo_ready = sem("hid_lo_ready")
        down_done = sem("down_done")
        y_added = sem("y_added")

        with nc.Block() as block:
            @block.sync
            def _(sp):
                def load(G, buf):
                    first_two = isinstance(G, int)
                    if not first_two:
                        sp.wait_ge(wu_split, G - 1)
                    src = w_units[2 * G:2 * G + 2] if first_two else w_units[bass.ds(2 * G, 2)]
                    sp.dma_start(w_raw[:, buf, :, :], src.rearrange("u p n -> p u n")).then_inc(wu_loaded[buf], 16)
                    if not first_two:
                        sp.wait_ge(hidc_ready, PER * (G - 1))
                    for p in range(2):
                        for e in range(2):
                            r = 4 * G + 2 * p + e
                            srow = combine_dram[r:r + 1, :] if first_two else combine_dram[bass.ds(r, 1), :]
                            sp.dma_start(comb[64 * e:64 * e + 64, buf, p, :], srow.to_broadcast([64, TOK])).then_inc(comb_loaded[buf], 16)
                load(0, 0)
                load(1, 1)
                with sp.Fori(1, GROUPS // 2) as g:
                    for buf in range(2):
                        load(2 * g + buf, buf)

            @block.gpsimd
            def _(pool):
                def split(G, buf):
                    pool.wait_ge(wu_hi_done, G + 1)
                    nc.gpsimd.tensor_tensor(wu_lo[:, buf, :, :], w_raw[:, buf, :, :], wu_hi[:, buf, :, :].bitcast(F32), ALU.subtract).then_inc(wu_split, 1)
                split(0, 0)
                split(1, 1)
                with pool.Fori(1, GROUPS // 2) as g:
                    for buf in range(2):
                        split(2 * g + buf, buf)

            @block.tensor
            def _(pe):
                def mm3(dst, l_hi, l_lo, r_hi, r_lo, start, stop):
                    nc.tensor.matmul(dst, l_hi, r_hi, start=start, stop=False)
                    nc.tensor.matmul(dst, l_hi, r_lo, start=False, stop=False)
                    return nc.tensor.matmul(dst, l_lo, r_hi, start=False, stop=stop)

                def up(G, buf, t, p, early):
                    n = PER * G + 2 * t + p
                    if t == 0 and p == 0:
                        pe.wait_ge(wu_split, G + 1)
                    if not (early and n < 2):
                        pe.wait_ge(gate_ready, n - 1)
                        pe.wait_ge(hid_ready, n - 1)
                    cols = slice(t * TG, (t + 1) * TG)
                    for dst, at in ((ps_g, 0), (ps_u, KC * P)):
                        for c in range(KC):
                            w = slice(at + c * P, at + (c + 1) * P)
                            last = mm3(dst[:, p, :], wu_hi[:, buf, p, w], wu_lo[:, buf, p, w], xh[:, c, cols], xl[:, c, cols], c == 0, c == KC - 1)
                    last.then_inc(gu_done, 1)

                def down(G, buf, t, p, early):
                    n = PER * G + 2 * t + p
                    pe.wait_ge(hid_lo_ready, n + 1)
                    pe.wait_ge(hid_hi_ready, n + 1)
                    if p == 0 and not (early and n < 4):
                        pe.wait_ge(y_added, NTG * G + t - 1)
                    for c in range(KC):
                        w = slice(2 * KC * P + c * P, 2 * KC * P + (c + 1) * P)
                        last = mm3(ps_y[:, t % 2, c, :], wu_hi[:, buf, p, w], wu_lo[:, buf, p, w], hid_hi[:, p, :], hid_lo[:, p, :], p == 0, p == 1)
                    last.then_inc(down_done, 1)

                def pair(g, early):
                    for buf in range(2):
                        for t in range(NTG):
                            for p in range(2):
                                up(2 * g + buf, buf, t, p, early)
                                k = (buf * NTG + t) * 2 + p - 1
                                if k >= 0:
                                    down(2 * g + k // PER, k // PER, k % PER // 2, k % 2, early)
                                elif not early:
                                    down(2 * g - 1, 1, NTG - 1, 1, False)

                pe.wait_ge(f_xl, 4)
                pair(0, True)
                with pe.Fori(1, GROUPS // 2) as g:
                    pair(g, False)
                down(GROUPS - 1, 1, NTG - 1, 1, True)

            @block.scalar
            def _(act):
                for q in range(4):
                    cols = slice(q * TG, (q + 1) * TG)
                    nc.scalar.activation(xh[:, :, cols], xn_t[:, :, cols], ACT.Copy).then_inc(f_xh, 1)

                def silu(n, p, early):
                    act.wait_ge(gu_done, n + 1)
                    if not (early and n < 2):
                        act.wait_ge(hid_ready, n - 1)
                    nc.scalar.activation(gate[:, p, :], ps_g[:, p, :], ACT.Silu).then_inc(gate_ready, 1)

                def high(n, p, early):
                    act.wait_ge(hidc_ready, n + 1)
                    if not (early and n < 2):
                        act.wait_ge(down_done, n - 1)
                    nc.scalar.activation(hid_hi[:, p, :], hid_c[:, p, :], ACT.Copy).then_inc(hid_hi_ready, 1)

                def split(g, buf):
                    G = 2 * g + buf
                    if not isinstance(G, int) or G >= 2:
                        act.wait_ge(down_done, PER * (G - 1))
                    act.wait_ge(wu_loaded[buf], 16 * (g + 1))
                    nc.scalar.activation(wu_hi[:, buf, :, :], w_raw[:, buf, :, :], ACT.Copy).then_inc(wu_hi_done, 1)

                def body(g, early, more=True):
                    for k in range(2 * PER):
                        n = 2 * PER * g + k
                        if not early and k == 3:
                            split(g, 1)
                        if more and k == PER + 3:
                            split(g + 1, 0)
                        silu(n, k % 2, early)
                        high(n, k % 2, early)
                split(0, 0)
                split(0, 1)
                body(0, True)
                with act.Fori(1, GROUPS // 2 - 1) as g:
                    body(g, False)
                body(GROUPS // 2 - 1, False, more=False)

            @block.vector
            def _(dve):
                nc.vector.memset(y_t[:, :, :], 0.0).then_inc(y_zero, 1)
                for q in range(4):
                    cols = slice(q * TG, (q + 1) * TG)
                    dve.wait_ge(f_xh, q + 1)
                    nc.vector.tensor_tensor(xl[:, :, cols], xn_t[:, :, cols], xh[:, :, cols].bitcast(F32), ALU.subtract).then_inc(f_xl, 1)
                dve.wait_ge(y_zero, 1)

                def low(n, p, early):
                    dve.wait_ge(hid_hi_ready, n + 1)
                    nc.vector.tensor_tensor(hid_lo[:, p, :], hid_c[:, p, :], hid_hi[:, p, :].bitcast(F32), ALU.subtract).then_inc(hid_lo_ready, 1)

                def add(m, t):
                    dve.wait_ge(down_done, 2 * (m + 1))
                    cols = slice(t * TG, (t + 1) * TG)
                    nc.vector.tensor_tensor(y_t[:, :, cols], ps_y[:, t % 2, :, :], y_t[:, :, cols], ALU.add).then_inc(y_added, 1)

                def body(g, early):
                    for k in range(2 * PER):
                        n = 2 * PER * g + k
                        t, p = k % PER // 2, k % 2
                        dve.wait_ge(gate_ready, n + 1)
                        if not (early and n < 2):
                            dve.wait_ge(hidc_ready, n - 1)
                        nc.vector.tensor_tensor(hid[:, p, :], ps_u[:, p, :], gate[:, p, :], ALU.mult).then_inc(hid_ready, 1)
                        dve.wait_ge(hid_ready, n + 1)
                        if t == 0 and p == 0:
                            dve.wait_ge(comb_loaded[k // PER], 64 * (g + 1))
                        if not (early and n < 2):
                            dve.wait_ge(hid_lo_ready, n - 1)
                            dve.wait_ge(hid_hi_ready, n - 1)
                        nc.vector.tensor_tensor(hid_c[:, p, :], hid[:, p, :], comb[:, k // PER, p, t * TG:(t + 1) * TG], ALU.mult).then_inc(hidc_ready, 1)
                        if not (early and n == 0):
                            if not (early and n - 1 < 2):
                                dve.wait_ge(down_done, n - 2)
                            low(n - 1, 1 - p, early)
                        if p == 1 and not (early and k == 1):
                            m = NTG * 2 * g + k // 2 - 1
                            add(m, (k // 2 - 1) % NTG)
                body(0, True)
                with dve.Fori(1, GROUPS // 2) as g:
                    body(g, False)
                last = GROUPS * PER - 1
                dve.wait_ge(down_done, last - 1)
                low(last, 1, False)
                add(GROUPS * NTG - 1, NTG - 1)
        ffn_ps.close()

        fin_ps = ExitStack()
        ps_f = psum(fin_ps, "ps_f", [P, 2, TT, D])
        silu_done = sem("silu_done")
        f_turned = sem("f_turned")
        f_gated = sem("f_gated")
        f_added = sem("f_added")
        stored = sem("stored")
        with nc.Block() as block:
            @block.scalar
            def _(act):
                for q in range(4):
                    cols = slice(q * TG, (q + 1) * TG)
                    nc.scalar.activation(y_t[:, :, cols], y_t[:, :, cols], ACT.Silu).then_inc(silu_done, 1)

            @block.tensor
            def _(pe):
                for b in range(B):
                    pe.wait_ge(silu_done, b // 2 + 1)
                    if b >= 2:
                        pe.wait_ge(f_gated, b - 1)
                    for t in range(TT):
                        for c in range(KC):
                            at = (b * TT + t) * P
                            last = nc.tensor.transpose(ps_f[:, b % 2, t, c * P:(c + 1) * P], y_t[:, c, at:at + P], ident[:, :])
                    last.then_inc(f_turned, 1)

            @block.vector
            def _(dve):
                for b in range(B):
                    rows = slice(b * TT, (b + 1) * TT)
                    dve.wait_ge(f_turned, b + 1)
                    nc.vector.tensor_tensor(attn_out[:, rows, :], ps_f[:, b % 2, :, :], attn_out[:, rows, :], ALU.mult).then_inc(f_gated, 1)
                    dve.wait_ge(f_gated, b + 1)
                    nc.vector.tensor_tensor(x_sb[:, rows, :], x_sb[:, rows, :], attn_out[:, rows, :], ALU.add).then_inc(f_added, 1)

            @block.sync
            def _(sp):
                for b in range(B):
                    rows = slice(b * TT, (b + 1) * TT)
                    sp.wait_ge(f_added, b + 1)
                    sp.dma_start(out_rows[:, rows, :], x_sb[:, rows, :]).then_inc(stored, 16)
                sp.wait_ge(stored, 16 * B)
        fin_ps.close()
        ffn.close()


def kernel(L0_attn_x, L0_attn_g_norm, L0_attn_Wq, L0_attn_Wkv, L0_attn_Wout, L0_attn_g_out, L0_ffn_Wr,
           L0_ffn_router_bias, L0_ffn_affinity, L0_ffn_te_W1, L0_ffn_te_b1, L0_ffn_te_W2, L0_ffn_te_b2,
           L0_ffn_Wg, L0_ffn_Wu, L0_ffn_Wd, L0_ffn_Sg, L0_ffn_Su, L0_ffn_Sd):
    import numpy as np
    import concourse.bacc as bacc
    from concourse import mybir as mb
    from concourse.bass_utils import run_bass_kernel_spmd as run

    E, D, F = L0_ffn_Wg.shape
    NS, _, H = L0_ffn_Sg.shape
    per = 128 // F

    def up_blocks(routed, shared):
        a = routed.reshape(E // per, per, D // 128, 128, F).transpose(0, 3, 2, 1, 4).reshape(E // per, 128, D)
        s = shared.reshape(NS, D // 128, 128, H // 128, 128).transpose(0, 3, 2, 1, 4).reshape(-1, 128, D)
        return np.concatenate([a, s])

    up_g = up_blocks(L0_ffn_Wg, L0_ffn_Sg)
    up_u = up_blocks(L0_ffn_Wu, L0_ffn_Su)
    down = np.concatenate([L0_ffn_Wd.reshape(-1, 128, D), L0_ffn_Sd.reshape(-1, 128, D)])
    arrays = {
        "x": L0_attn_x, "wq": L0_attn_Wq, "wkv": L0_attn_Wkv, "wout": L0_attn_Wout,
        "g_norm": L0_attn_g_norm.reshape(D // 128, 128).T, "g_out": L0_attn_g_out,
        "wr_t": L0_ffn_Wr.T, "r_bias": L0_ffn_router_bias, "aff_t": L0_ffn_affinity.T,
        "w1_t": L0_ffn_te_W1.T, "b1": L0_ffn_te_b1[:, None], "w2_t": L0_ffn_te_W2.T, "b2": L0_ffn_te_b2,
        "w_units": np.concatenate([up_g, up_u, down], axis=2),
        "ident_in": np.eye(128, dtype=np.float32), "iota_in": np.arange(E, dtype=np.float32),
    }
    arrays = {k: np.ascontiguousarray(v) for k, v in arrays.items()}
    nc = bacc.Bacc("TRN2", target_bir_lowering=False, num_devices=1)
    args = [nc.dram_tensor(k, v.shape, mb.dt.from_np(v.dtype), kind="ExternalInput").ap() for k, v in arrays.items()]
    out = nc.dram_tensor("out", L0_attn_x.shape, mb.dt.float32, kind="ExternalOutput").ap()
    build(nc, *args, out)
    r = run(nc, [arrays], core_ids=[0])
    return r.results[0]["out"]
```

```python
from contextlib import ExitStack

import concourse.bass as bass
from concourse import mybir

F32 = mybir.dt.float32
F32R = mybir.dt.float32r
U32 = mybir.dt.uint32
I32 = mybir.dt.int32
BF16 = mybir.dt.bfloat16
ALU = mybir.AluOpType
ACT = mybir.ActivationFunctionType
AX_X = mybir.AxisListType.X

P = 128
EPS = 1e-5
L2_EPS = 1e-12
SCALE = 16.0
TOPK = 4


def build(nc, x, wq, wkv, wout, g_norm, g_out, wr_t, r_bias, aff_t, w1_t, b1, w2_t, b2, w_expert, w_shared, ident_in, tri_in, iota_in, out):
    B, N, D = x.shape
    HID = wq.shape[1]
    DH = P
    HEADS = HID // DH
    E = wr_t.shape[1]
    ND = w2_t.shape[1]
    F = P // 2
    WE = w_expert.shape[2]
    SH = w_shared.shape[1]
    TOK = B * N
    TT = N // P
    KC = D // P
    TILES = TOK // P
    HP = HEADS // 2
    PAIR = 2 * N
    TG = 512
    NTG = TOK // TG
    GT = TG // P
    NB = TOK * TOPK // P + E
    SLOTS = NB * P
    DUOS = NB // 2
    assert TT == 2 and KC == 2 and HP == 8 and PAIR == 512

    x_rows = x.rearrange("b (t p) d -> p (b t) d", p=P)
    out_rows = out.rearrange("b (t p) d -> p (b t) d", p=P)
    slot_x = nc.dram_tensor("slot_x", (SLOTS, D), F32, kind="Internal").ap()
    slot_y = nc.dram_tensor("slot_y", (SLOTS, D), F32, kind="Internal").ap()
    block_expert = nc.dram_tensor("block_expert", (NB, 1), U32, kind="Internal").ap()

    with ExitStack() as whole:
        def sem(name):
            return whole.enter_context(nc.semaphore(name))

        def sbuf(ctx, name, shape, dt=F32):
            return ctx.enter_context(nc.sbuf_tensor(name, shape, dt))

        def psum(ctx, name, shape, dt=F32):
            return ctx.enter_context(nc.psum_tensor(name, shape, dt))

        def bcast(a, shape):
            return a.to_broadcast(shape)

        x_sb = sbuf(whole, "x_sb", [P, TILES, D])
        xn_t = sbuf(whole, "xn_t", [P, KC, TOK])
        attn_out = sbuf(whole, "attn_out", [P, TILES, D])
        ident = sbuf(whole, "ident", [P, P])
        slots = sbuf(whole, "slots", [P, TILES, TOPK], U32)
        gates = sbuf(whole, "gates", [P, TILES, TOPK])
        minus_half = sbuf(whole, "minus_half", [P, 8])
        spare = sbuf(whole, "spare", [P, 8])

        attention = ExitStack()
        xa_t = sbuf(attention, "xa_t", [P, KC, TOK])
        wq_hi = sbuf(attention, "wq_hi", [P, KC, HID], F32R)
        wq_lo = sbuf(attention, "wq_lo", [P, KC, HID], F32R)
        wkv_hi = sbuf(attention, "wkv_hi", [P, KC, 2 * DH], F32R)
        wkv_lo = sbuf(attention, "wkv_lo", [P, KC, 2 * DH], F32R)
        wo_hi = sbuf(attention, "wo_hi", [P, HEADS, D], F32R)
        wo_lo = sbuf(attention, "wo_lo", [P, HEADS, D], F32R)
        g_out_b = sbuf(attention, "g_out_b", [P, D])

        prep = ExitStack()
        wo_raw = sbuf(prep, "wo_raw", [P, HEADS, D])
        wkv_raw = sbuf(prep, "wkv_raw", [P, KC, 2 * DH])
        xn = sbuf(prep, "xn", [P, TT, D])
        xa = sbuf(prep, "xa", [P, TT, D])
        xn_stat = sbuf(prep, "xn_stat", [P, KC, N])
        g_col = sbuf(prep, "g_col", [P, KC])
        wr_sb = sbuf(prep, "wr_sb", [P, KC, E])
        w1_sb = sbuf(prep, "w1_sb", [P, KC, P])
        b1_sb = sbuf(prep, "b1_sb", [P, 1])
        w2_sb = sbuf(prep, "w2_sb", [P, ND])
        b2_b = sbuf(prep, "b2_b", [P, ND])
        aff_b = sbuf(prep, "aff_b", [P, ND, E])
        rbias_b = sbuf(prep, "rbias_b", [P, E])
        iota_b = sbuf(prep, "iota_b", [P, E])
        stats = sbuf(prep, "stats", [P, TT, 6])
        meanvar = sbuf(prep, "meanvar", [P, TT, 2])
        var_eps = sbuf(prep, "var_eps", [P, TT])
        rstd = sbuf(prep, "rstd", [P, TT])
        x_sum = sbuf(prep, "x_sum", [P, KC, B])
        raw_logits = sbuf(prep, "raw_logits", [P, TILES, E])
        h1_rep = sbuf(prep, "h1_rep", [P, B, P])
        task = sbuf(prep, "task", [P, B, ND])
        task_s = sbuf(prep, "task_s", [P, B])
        dom = sbuf(prep, "dom", [P, B, E])
        dom_part = sbuf(prep, "dom_part", [P, B, E])
        choice = sbuf(prep, "choice", [P, TILES, E])
        top = sbuf(prep, "top", [P, TILES, 8])
        top_at = sbuf(prep, "top_at", [P, TILES, 8], U32)
        top_f = sbuf(prep, "top_f", [P, TILES, 8])
        part = [sbuf(prep, f"part{k}", [P, TILES, E]) for k in range(2)]
        mask_b = sbuf(prep, "mask_b", [P, TILES, E], BF16)
        before_b = sbuf(prep, "before_b", [P, TILES + 1, E], BF16)
        tri_sb = sbuf(prep, "tri_sb", [P, P])
        tri_b = sbuf(prep, "tri_b", [P, P], BF16)
        ones_b = sbuf(prep, "ones_b", [P, P], BF16)
        count_i = sbuf(prep, "count_i", [P, E], I32)
        blocks_i = sbuf(prep, "blocks_i", [P, E], I32)
        blocks = sbuf(prep, "blocks", [P, E])
        ends = [sbuf(prep, f"ends{k}", [P, E]) for k in range(2)]
        slot_f = sbuf(prep, "slot_f", [P, TILES, TOPK])
        picked = sbuf(prep, "picked", [P, TILES, TOPK])
        row = sbuf(prep, "row", [P, 3, TILES])
        block_no = sbuf(prep, "block_no", [P, 1])
        owner = sbuf(prep, "owner", [P, 1])
        owner_i = sbuf(prep, "owner_i", [P, 1], U32)
        zeros = sbuf(prep, "zeros", [P, D])
        wq_raw = attn_out[:, :, :].rearrange("p t d -> p (t d)").rearrange("p (c n) -> p c n", c=KC)
        hit = [attn_out[:, 4 * k:4 * k + 4, :].rearrange("p a (t e) -> p (a t) e", e=E) for k in range(TOPK)]

        prep_ps = ExitStack()
        ps_xn = psum(prep_ps, "ps_xn", [P, KC, N])
        ps_xa = psum(prep_ps, "ps_xa", [P, KC, N])
        ps_logits = psum(prep_ps, "ps_logits", [P, TT, E])
        ps_h1 = psum(prep_ps, "ps_h1", [P, B])
        ps_task = psum(prep_ps, "ps_task", [P, B, ND])
        ps_rank = psum(prep_ps, "ps_rank", [P, TILES, E])
        ps_count = psum(prep_ps, "ps_count", [P, E])

        x_loaded = sem("x_loaded")
        const_loaded = sem("const_loaded")
        wq_loaded = sem("wq_loaded")
        wkv_loaded = sem("wkv_loaded")
        wo_loaded = sem("wo_loaded")
        half_set = sem("half_set")
        ln_step = sem("ln_step")
        var_ready = sem("var_ready")
        rstd_ready = sem("rstd_ready")
        xn_ready = sem("xn_ready")
        xa_ready = sem("xa_ready")
        xn_turned = sem("xn_turned")
        xa_turned = sem("xa_turned")
        xn_copied = sem("xn_copied")
        xn_summed = sem("xn_summed")
        xa_copied = sem("xa_copied")
        logits_done = sem("logits_done")
        logits_copied = sem("logits_copied")
        h1_done = sem("h1_done")
        h1_ready = sem("h1_ready")
        task_done = sem("task_done")
        task_max = sem("task_max")
        task_exp = sem("task_exp")
        choice_sub = sem("choice_sub")
        choice_exp = sem("choice_exp")
        zeros_set = sem("zeros_set")
        slots_cleared = sem("slots_cleared")
        row_kept = sem("row_kept")
        tri_ready = sem("tri_ready")
        mask_ready = sem("mask_ready")
        ranked = sem("ranked")
        owner_ready = sem("owner_ready")
        owner_stored = sem("owner_stored")
        hi_split = sem("hi_split")
        lo_split = sem("lo_split")

        LN_LINKS = 8
        CONSTS = 13
        with nc.Block() as block:
            @block.sync
            def _(sp):
                for b in range(B):
                    sp.dma_start(x_sb[:, b * TT:(b + 1) * TT, :], x_rows[:, b * TT:(b + 1) * TT, :]).then_inc(x_loaded, 16)
                sp.dma_start(wq_raw, wq.rearrange("(c p) n -> p c n", p=P)).then_inc(wq_loaded, 16)
                sp.dma_start(wkv_raw[:, :, :], wkv.rearrange("(c p) n -> p c n", p=P)).then_inc(wkv_loaded, 16)
                sp.dma_start(wo_raw[:, :, :], wout.rearrange("(h p) n -> p h n", p=P)).then_inc(wo_loaded, 16)
                sp.wait_ge(zeros_set, 1)
                for a in range(SLOTS // (8 * P)):
                    sp.dma_start(slot_x.rearrange("(a p r) d -> a p r d", p=P, r=8)[a], bcast(zeros[:, :].unsqueeze(1), [P, 8, D])).then_inc(slots_cleared, 16)
                sp.wait_ge(owner_ready, 1)
                sp.dma_start(block_expert, owner_i[:, :]).then_inc(owner_stored, 16)
                sp.wait_ge(owner_stored, 16)
                sp.wait_ge(slots_cleared, 16 * (SLOTS // (8 * P)))

            @block.scalar
            def _(act):
                def row_b(a, n):
                    return a.unsqueeze(0).to_broadcast([P, n])
                act.dma_start(ident[:, :], ident_in).then_inc(const_loaded, 16)
                act.dma_start(g_col[:, :], g_norm).then_inc(const_loaded, 16)
                act.dma_start(wr_sb[:, :, :], wr_t.rearrange("(c p) e -> p c e", p=P)).then_inc(const_loaded, 16)
                act.dma_start(w1_sb[:, :, :], w1_t.rearrange("(c p) e -> p c e", p=P)).then_inc(const_loaded, 16)
                act.dma_start(b1_sb[:, :], b1).then_inc(const_loaded, 16)
                act.dma_start(w2_sb[:, :], w2_t).then_inc(const_loaded, 16)
                act.dma_start(b2_b[:, :], row_b(b2, ND)).then_inc(const_loaded, 16)
                act.dma_start(rbias_b[:, :], row_b(r_bias, E)).then_inc(const_loaded, 16)
                act.dma_start(iota_b[:, :], row_b(iota_in[0:E], E)).then_inc(const_loaded, 16)
                act.dma_start(g_out_b[:, :], row_b(g_out, D)).then_inc(const_loaded, 16)
                act.dma_start(aff_b[:, :, :].rearrange("p a e -> p (a e)"), row_b(aff_t.rearrange("a e -> (a e)"), ND * E)).then_inc(const_loaded, 16)
                act.dma_start(tri_sb[:, :], tri_in).then_inc(const_loaded, 16)
                act.dma_start(block_no[:, :], iota_in.unsqueeze(1)).then_inc(const_loaded, 16)
                act.wait_ge(const_loaded, 16 * CONSTS)
                nc.scalar.activation(tri_b[:, :], tri_sb[:, :], ACT.Copy).then_inc(tri_ready, 1)
                with act.Fori(0, B) as b:
                    act.wait_ge(xn_ready, b + 1)
                    nc.scalar.activation(x_sb[:, bass.ds(b * TT, TT), :], xn[:, :, :], ACT.Copy).then_inc(row_kept, 1)
                    act.wait_ge(xn_turned, b + 1)
                    nc.scalar.activation(xn_t[:, :, bass.ds(b * N, N)], ps_xn[:, :, :], ACT.Copy)
                    act.wait_ge(logits_done, b + 1)
                    act.wait_ge(xn_summed, b + 1)
                    nc.scalar.activation(xn_stat[:, :, :], ps_xn[:, :, :], ACT.Copy).then_inc(xn_copied, 1)
                    act.wait_ge(xa_turned, b + 1)
                    for c in range(KC):
                        last = nc.scalar.activation(xa_t[:, c, bass.ds(b * N, N)], ps_xa[:, c, :], ACT.Copy, scale=g_col[:, c:c + 1])
                    last.then_inc(xa_copied, 1)
                    act.wait_ge(logits_done, b + 2)
                    nc.scalar.activation(raw_logits[:, bass.ds(b * TT, TT), :], ps_logits[:, :, :], ACT.Copy).then_inc(logits_copied, 1)
                act.wait_ge(h1_done, 1)
                nc.scalar.activation(h1_rep[:, :, :], bcast(ps_h1[:, :].unsqueeze(2), [P, B, P]), ACT.Gelu,
                                     bias=b1_sb[:, 0:1], scale=1.0 / N).then_inc(h1_ready, 1)
                act.wait_ge(wq_loaded, 16)
                nc.scalar.activation(wq_hi[:, :, :], wq_raw, ACT.Copy).then_inc(hi_split, 1)
                act.wait_ge(wkv_loaded, 16)
                nc.scalar.activation(wkv_hi[:, :, :], wkv_raw[:, :, :], ACT.Copy).then_inc(hi_split, 1)
                act.wait_ge(wo_loaded, 16)
                nc.scalar.activation(wo_hi[:, :, :], wo_raw[:, :, :], ACT.Copy).then_inc(hi_split, 1)
                act.wait_ge(task_max, 1)
                nc.scalar.activation(task[:, :, :], task[:, :, :], ACT.Exp).then_inc(task_exp, 1)
                act.wait_ge(choice_sub, 1)
                nc.scalar.activation(raw_logits[:, :, :], raw_logits[:, :, :], ACT.Exp).then_inc(choice_exp, 1)

            @block.gpsimd
            def _(pool):
                nc.gpsimd.memset(minus_half[:, :], -0.5).then_inc(half_set, 1)
                nc.gpsimd.memset(zeros[:, :], 0.0).then_inc(zeros_set, 1)
                pool.wait_ge(half_set, 1)
                with pool.Fori(0, B) as b:
                    for k in range(2):
                        pool.wait_ge(var_ready, 2 * b + k + 1)
                        nc.gpsimd.tensor_tensor(rstd[:, :], var_eps[:, :], minus_half[:, 0:TT], ALU.pow).then_inc(rstd_ready, 1)
                pool.wait_ge(hi_split, 3)
                nc.gpsimd.tensor_tensor(wo_lo[:, :, :], wo_raw[:, :, :], wo_hi[:, :, :].bitcast(F32), ALU.subtract).then_inc(lo_split, 1)

            @block.tensor
            def _(pe):
                pe.wait_ge(const_loaded, 16 * CONSTS)
                with pe.Fori(0, B) as b:
                    pe.wait_ge(xn_ready, b + 1)
                    pe.wait_ge(xn_copied, b + 1)
                    for c in range(KC):
                        for t in range(TT):
                            last = nc.tensor.transpose(ps_xn[:, c, t * P:(t + 1) * P], xn[:, t, c * P:(c + 1) * P], ident[:, :])
                    last.then_inc(xn_turned, 1)
                    pe.wait_ge(xa_ready, b + 1)
                    pe.wait_ge(xa_copied, b + 1)
                    for c in range(KC):
                        for t in range(TT):
                            last = nc.tensor.transpose(ps_xa[:, c, t * P:(t + 1) * P], xa[:, t, c * P:(c + 1) * P], ident[:, :])
                    last.then_inc(xa_turned, 1)
                    pe.wait_ge(xn_copied, b + 2)
                    pe.wait_ge(logits_copied, b + 1)
                    for t in range(TT):
                        for c in range(KC):
                            last = nc.tensor.matmul(ps_logits[:, t, :], xn_stat[:, c, t * P:(t + 1) * P], wr_sb[:, c, :],
                                                    start=(c == 0), stop=(c == KC - 1))
                    last.then_inc(logits_done, 1)
                pe.wait_ge(xn_summed, B + 1)
                for c in range(KC):
                    last = nc.tensor.matmul(ps_h1[:, :], w1_sb[:, c, :], x_sum[:, c, :], start=(c == 0), stop=(c == KC - 1))
                last.then_inc(h1_done, 1)
                pe.wait_ge(h1_ready, 1)
                for b in range(B):
                    last = nc.tensor.matmul(ps_task[:, b, :], h1_rep[:, b, :], w2_sb[:, :], start=True, stop=True)
                last.then_inc(task_done, 1)
                pe.wait_ge(tri_ready, 2)
                pe.wait_ge(mask_ready, 1)
                for h in range(2):
                    tiles = slice(h * TILES // 2, (h + 1) * TILES // 2)
                    nc.tensor.matmul(ps_rank[:, tiles, :], tri_b[:, :], mask_b[:, tiles, :], start=True, stop=False)
                    nc.tensor.matmul(ps_rank[:, tiles, :], ones_b[:, :], before_b[:, tiles, :], start=False, stop=True)
                nc.tensor.matmul(ps_count[:, :], ones_b[:, :], before_b[:, TILES, :], start=True, stop=True).then_inc(ranked, 1)

            @block.vector
            def _(dve):
                for k, s in enumerate((xn_summed, xn_copied, xa_copied, logits_done, logits_copied)):
                    nc.vector.memset(spare[:, k:k + 1], 0.0).then_inc(s, 1)
                nc.vector.memset(ones_b[:, :], 1.0).then_inc(tri_ready, 1)
                nc.vector.memset(before_b[:, 0, :], 0.0)
                dve.wait_ge(x_loaded, 16 * B)
                with dve.Fori(0, B) as b:
                    links = [0]

                    def link(ins):
                        links[0] += 1
                        ins.then_inc(ln_step, 1)
                        dve.wait_ge(ln_step, b * LN_LINKS + links[0])

                    for k, (dst, ready) in enumerate(((xn, xn_ready), (xa, xa_ready))):
                        for t in range(TT):
                            src = x_sb[:, bass.ds(b * TT + t, 1), :].rearrange("p a d -> p (a d)") if k == 0 else xn[:, t, :]
                            last = nc.vector.bn_stats(stats[:, t, :], src)
                        link(last)
                        nc.vector.memset(spare[:, 7:8], 0.0)
                        for t in range(TT):
                            last = nc.vector.bn_aggr(meanvar[:, t, :], stats[:, t, :])
                        link(last)
                        nc.vector.tensor_scalar(var_eps[:, :], meanvar[:, :, 1], EPS, None, ALU.add).then_inc(var_ready, 1)
                        dve.wait_ge(rstd_ready, 2 * b + k + 1)
                        for t in range(TT):
                            src = x_sb[:, bass.ds(b * TT + t, 1), :].rearrange("p a d -> p (a d)") if k == 0 else xn[:, t, :]
                            last = nc.vector.tensor_scalar(dst[:, t, :], src, meanvar[:, t, 0:1], rstd[:, t:t + 1], ALU.subtract, ALU.mult)
                            if t == 0:
                                link(last)
                        last.then_inc(ready, 1)
                        dve.wait_ge(ready, b + 1)
                        if k == 0:
                            dve.wait_ge(xn_copied, b + 2)
                            red = nc.vector.tensor_reduce(x_sum[:, :, bass.ds(b, 1)].rearrange("p c o -> p (c o)"), xn_stat[:, :, :], AX_X, ALU.add)
                            red.then_inc(xn_summed, 1)
                            link(nc.vector.memset(spare[:, 5:6], 0.0))
                    dve.wait_ge(xa_turned, b + 1)
                    dve.wait_ge(row_kept, b + 1)
                    link(nc.vector.memset(spare[:, 6:7], 0.0))
                    assert links[0] == LN_LINKS, links

                chain = [0]
                route_step = sem("route_step")

                def then(ins):
                    chain[0] += 1
                    ins.then_inc(route_step, 1)
                    dve.wait_ge(route_step, chain[0])

                dve.wait_ge(hi_split, 2)
                then(nc.vector.tensor_tensor(wq_lo[:, :, :], wq_raw, wq_hi[:, :, :].bitcast(F32), ALU.subtract))
                nc.vector.tensor_tensor(wkv_lo[:, :, :], wkv_raw[:, :, :], wkv_hi[:, :, :].bitcast(F32), ALU.subtract)
                dve.wait_ge(task_done, 1)
                then(nc.vector.tensor_tensor(task[:, :, :], ps_task[:, :, :], bcast(b2_b[:, :].unsqueeze(1), [P, B, ND]), ALU.add))
                then(nc.vector.tensor_reduce(task_s[:, :], task[:, :, :], AX_X, ALU.max))
                nc.vector.tensor_tensor(task[:, :, :], task[:, :, :], bcast(task_s[:, :].unsqueeze(2), [P, B, ND]), ALU.subtract).then_inc(task_max, 1)
                dve.wait_ge(task_exp, 1)
                then(nc.vector.tensor_reduce(task_s[:, :], task[:, :, :], AX_X, ALU.add))
                then(nc.vector.reciprocal(task_s[:, :], task_s[:, :]))
                then(nc.vector.scalar_tensor_tensor(task[:, :, :], task[:, :, :], 0.5, bcast(task_s[:, :].unsqueeze(2), [P, B, ND]), ALU.mult, ALU.mult))
                for a in range(ND):
                    dst = dom if a == 0 else dom_part
                    then(nc.vector.tensor_tensor(dst[:, :, :], bcast(task[:, :, a].unsqueeze(2), [P, B, E]),
                                                 bcast(aff_b[:, a, :].unsqueeze(1), [P, B, E]), ALU.mult))
                    if a:
                        then(nc.vector.tensor_tensor(dom[:, :, :], dom[:, :, :], dom_part[:, :, :], ALU.add))
                dve.wait_ge(logits_copied, B + 1)
                logits4 = raw_logits[:, :, :].rearrange("p (b t) e -> p b t e", t=TT)
                for t in range(TT):
                    then(nc.vector.tensor_tensor(logits4[:, :, t, :], logits4[:, :, t, :], dom[:, :, :], ALU.add))
                then(nc.vector.tensor_tensor(choice[:, :, :], raw_logits[:, :, :], bcast(rbias_b[:, :].unsqueeze(1), [P, TILES, E]), ALU.add))
                then(nc.vector.tensor_reduce(row[:, 0, :], raw_logits[:, :, :], AX_X, ALU.max))
                nc.vector.tensor_tensor(raw_logits[:, :, :], raw_logits[:, :, :], bcast(row[:, 0, :].unsqueeze(2), [P, TILES, E]), ALU.subtract).then_inc(choice_sub, 1)
                for t in range(TILES):
                    then(nc.vector.max(top[:, t, :], choice[:, t, :]))
                    last = nc.vector.max_index(top_at[:, t, :], top[:, t, :], choice[:, t, :])
                then(last)
                then(nc.vector.tensor_copy(top_f[:, :, :], top_at[:, :, :]))
                for k in range(TOPK):
                    last = nc.vector.tensor_tensor(hit[k], bcast(iota_b[:, :].unsqueeze(1), [P, TILES, E]),
                                                   bcast(top_f[:, :, k].unsqueeze(2), [P, TILES, E]), ALU.is_equal)
                then(last)
                for k in range(2):
                    last = nc.vector.tensor_tensor(part[k][:, :, :], hit[2 * k], hit[2 * k + 1], ALU.add)
                then(last)
                then(nc.vector.tensor_tensor(mask_b[:, :, :], part[0][:, :, :], part[1][:, :, :], ALU.add))
                for t in range(TILES):
                    last = nc.vector.tensor_tensor(before_b[:, t + 1, :], before_b[:, t, :], mask_b[:, t, :], ALU.add)
                    if t < TILES - 1:
                        then(last)
                last.then_inc(mask_ready, 1)
                dve.wait_ge(choice_exp, 1)
                then(nc.vector.tensor_reduce(row[:, 1, :], raw_logits[:, :, :], AX_X, ALU.add))
                for k in range(TOPK):
                    then(nc.vector.tensor_tensor(part[k % 2][:, :, :], hit[k], raw_logits[:, :, :], ALU.mult))
                    last = nc.vector.tensor_reduce(picked[:, :, k], part[k % 2][:, :, :], AX_X, ALU.add)
                then(last)
                then(nc.vector.tensor_reduce(row[:, 0, :], picked[:, :, :], AX_X, ALU.add))
                then(nc.vector.scalar_tensor_tensor(row[:, 2, :], row[:, 1, :], 1e-8, row[:, 0, :], ALU.mult, ALU.add))
                then(nc.vector.reciprocal(row[:, 1, :], row[:, 2, :]))
                nc.vector.tensor_tensor(gates[:, :, :], picked[:, :, :], bcast(row[:, 1, :].unsqueeze(2), [P, TILES, TOPK]), ALU.mult)
                dve.wait_ge(ranked, 1)
                then(nc.vector.tensor_scalar(count_i[:, :], ps_count[:, :], float(P - 1), None, ALU.add))
                then(nc.vector.tensor_scalar(blocks_i[:, :], count_i[:, :], 7, None, ALU.arith_shift_right))
                then(nc.vector.tensor_copy(blocks[:, :], blocks_i[:, :]))
                then(nc.vector.tensor_copy(ends[0][:, :], blocks[:, :]))
                a, step = 0, 1
                while step < E:
                    nc.vector.tensor_copy(ends[1 - a][:, 0:step], ends[a][:, 0:step])
                    then(nc.vector.tensor_tensor(ends[1 - a][:, step:E], ends[a][:, step:E], ends[a][:, 0:E - step], ALU.add))
                    a, step = 1 - a, 2 * step
                last_end = ends[a]
                then(nc.vector.tensor_scalar(ends[1 - a][:, :], last_end[:, :], block_no[:, 0:1], None, ALU.is_le))
                then(nc.vector.tensor_reduce(owner[:, :], ends[1 - a][:, :], AX_X, ALU.add))
                nc.vector.tensor_scalar(owner_i[:, :], owner[:, :], float(E - 1), None, ALU.min).then_inc(owner_ready, 1)
                then(nc.vector.tensor_tensor(blocks[:, :], last_end[:, :], blocks[:, :], ALU.subtract))
                then(nc.vector.scalar_tensor_tensor(choice[:, :, :], bcast(blocks[:, :].unsqueeze(1), [P, TILES, E]), float(P),
                                                    ps_rank[:, :, :], ALU.mult, ALU.add))
                for k in range(TOPK):
                    then(nc.vector.tensor_tensor(part[k % 2][:, :, :], hit[k], choice[:, :, :], ALU.mult))
                    last = nc.vector.tensor_reduce(slot_f[:, :, k], part[k % 2][:, :, :], AX_X, ALU.add)
                then(last)
                nc.vector.tensor_copy(slots[:, :, :], slot_f[:, :, :])
        prep_ps.close()
        prep.close()

        work = ExitStack()
        xs_hi = sbuf(work, "xs_hi", [P, KC, N], F32R)
        xs_lo = sbuf(work, "xs_lo", [P, KC, N], F32R)
        kv_rows = sbuf(work, "kv_rows", [P, TT, 2 * DH])
        k_sq = sbuf(work, "k_sq", [P, TT, DH])
        k_norm = sbuf(work, "k_norm", [P, TT, DH])
        kt_hi = sbuf(work, "kt_hi", [P, N], F32R)
        kt_lo = sbuf(work, "kt_lo", [P, N], F32R)
        VW = DH + 2
        v_hi = sbuf(work, "v_hi", [P, TT, VW], F32R)
        v_lo = sbuf(work, "v_lo", [P, TT, DH], F32R)
        ones2 = sbuf(work, "ones2", [P, TT, 2])
        q_sq = sbuf(work, "q_sq", [P, 4, DH])
        q_sum = sbuf(work, "q_sum", [P, 4])
        q_var = sbuf(work, "q_var", [P, 4])
        q_scale = sbuf(work, "q_scale", [P, 4])
        k_sum = sbuf(work, "k_sum", [P, 2])
        k_var = sbuf(work, "k_var", [P, 2])
        k_scale = sbuf(work, "k_scale", [P, 2])
        q_norm = sbuf(work, "q_norm", [P, TT, 2, DH])
        qt_hi = sbuf(work, "qt_hi", [P, 2, PAIR], F32R)
        qt_lo = sbuf(work, "qt_lo", [P, 2, PAIR], F32R)
        w_f = sbuf(work, "w_f", [P, TT, PAIR])
        w_hi = sbuf(work, "w_hi", [P, 2, TT, PAIR], F32R)
        w_lo = sbuf(work, "w_lo", [P, 2, TT, PAIR], F32R)
        w_rec = sbuf(work, "w_rec", [P, 4])
        o_norm = sbuf(work, "o_norm", [P, 4, DH])
        ot_hi = sbuf(work, "ot_hi", [P, 2, PAIR], F32R)
        ot_lo = sbuf(work, "ot_lo", [P, 2, PAIR], F32R)
        rows_out = sbuf(work, "rows_out", [P, TT, D])
        o_stats = sbuf(work, "o_stats", [P, TT, 6])
        o_mv = sbuf(work, "o_mv", [P, TT, 2])
        o_var = sbuf(work, "o_var", [P, TT])
        o_rstd = sbuf(work, "o_rstd", [P, TT])

        row_stage = sbuf(work, "row_stage", [P, 2, D])
        slot_stage = sbuf(work, "slot_stage", [P, 2, TOPK], U32)

        work_ps = ExitStack()
        ps_q = psum(work_ps, "ps_q", [P, TT, 2, DH])
        ps_t = psum(work_ps, "ps_t", [P, PAIR])
        ps_s = psum(work_ps, "ps_s", [P, TT, PAIR])
        ps_o = psum(work_ps, "ps_o", [P, 2, 512])
        ps_ot = psum(work_ps, "ps_ot", [P, PAIR])
        ps_acc = psum(work_ps, "ps_acc", [P, TT, D])
        o_at = ps_o[:, :, 0:2 * VW].rearrange("p h (t w) -> p h t w", t=2)

        v_ones = sem("v_ones")
        xs_ready = sem("xs_ready")
        xs_hi_ready = sem("xs_hi_ready")
        kv_done = sem("kv_done")
        kv_copied = sem("kv_copied")
        ksq_ready = sem("ksq_ready")
        ksum_ready = sem("ksum_ready")
        kscale_ready = sem("kscale_ready")
        knorm_ready = sem("knorm_ready")
        k_turned = sem("k_turned")
        kt_hi_ready = sem("kt_hi_ready")
        kt_lo_ready = sem("kt_lo_ready")
        v_ready = sem("v_ready")
        q_done = sem("q_done")
        qsq_ready = sem("qsq_ready")
        qsum_ready = sem("qsum_ready")
        qscale_ready = sem("qscale_ready")
        qnorm_ready = sem("qnorm_ready")
        q_turned = sem("q_turned")
        qt_hi_ready = sem("qt_hi_ready")
        qt_lo_ready = sem("qt_lo_ready")
        s_done = sem("s_done")
        w_ready = sem("w_ready")
        w_hi_ready = sem("w_hi_ready")
        w_lo_ready = sem("w_lo_ready")
        av_done = sem("av_done")
        rec_ready = sem("rec_ready")
        onorm_ready = sem("onorm_ready")
        o_turned = sem("o_turned")
        ot_hi_ready = sem("ot_hi_ready")
        ot_lo_ready = sem("ot_lo_ready")
        proj_done = sem("proj_done")
        acc_copied = sem("acc_copied")
        ln_out = sem("ln_out")
        ovar_ready = sem("ovar_ready")
        orstd_ready = sem("orstd_ready")
        k_link = sem("k_link")
        q_link = sem("q_link")
        v_hi_ready = sem("v_hi_ready")

        rows_staged = sem("rows_staged")
        rows_sent = [sem(f"rows_sent{i}") for i in range(2)]
        SEND = HP // 2
        assert SEND == TOPK and B * 2 == TILES

        UNITS_A = B * HP

        def steps(eng, step):
            for hp in range(HP):
                step(0, hp)
            with eng.Fori(1, B) as b:
                for hp in range(HP):
                    step(b, hp)
            for hp in range(5):
                step(B, hp)

        def live(b, hp, lag):
            if not isinstance(b, int):
                return True
            return 0 <= HP * b + hp - lag < UNITS_A

        def started(b):
            return not isinstance(b, int) or b < B

        def first(b):
            return isinstance(b, int) and b == 0

        with nc.Block() as block:
            @block.tensor
            def _(pe):
                def mm3(dst, l_hi, l_lo, r_hi, r_lo, start, stop, **kw):
                    nc.tensor.matmul(dst, l_hi, r_hi, start=start, stop=False, **kw)
                    nc.tensor.matmul(dst, l_hi, r_lo, start=False, stop=False, **kw)
                    return nc.tensor.matmul(dst, l_lo, r_hi, start=False, stop=stop, **kw)

                def step(b, hp):
                    u = HP * b + hp
                    if hp == 0 and started(b):
                        pe.wait_ge(xs_ready, b + 1)
                        if not first(b):
                            pe.wait_ge(qnorm_ready, u)
                        for t in range(TT):
                            for c in range(KC):
                                cols = slice(t * P, (t + 1) * P)
                                last = mm3(ps_q[:, t, :, :], xs_hi[:, c, cols], xs_lo[:, c, cols],
                                           wkv_hi[:, c, :], wkv_lo[:, c, :], c == 0, c == KC - 1)
                        last.then_inc(kv_done, 1)
                    if live(b, hp, 2):
                        pe.wait_ge(qt_lo_ready, u - 1)
                        pe.wait_ge(qt_hi_ready, u - 1)
                        if hp == 2:
                            pe.wait_ge(kt_hi_ready, b + 1)
                            pe.wait_ge(kt_lo_ready, b + 1)
                        if live(b, hp, 3):
                            pe.wait_ge(w_ready, u - 2)
                        i = hp % 2
                        for t in range(TT):
                            cols = slice(t * P, (t + 1) * P)
                            last = mm3(ps_s[:, t, :], kt_hi[:, cols], kt_lo[:, cols], qt_hi[:, i, :], qt_lo[:, i, :], True, True)
                        last.then_inc(s_done, 1)
                    if hp == 1 and started(b):
                        pe.wait_ge(knorm_ready, b + 1)
                        if not first(b):
                            pe.wait_ge(qt_lo_ready, u - 1)
                            pe.wait_ge(qt_hi_ready, u - 1)
                        for t in range(TT):
                            last = nc.tensor.transpose(ps_t[:, t * P:(t + 1) * P], k_norm[:, t, :], ident[:, :])
                        last.then_inc(k_turned, 1)
                    if live(b, hp, 3):
                        pe.wait_ge(w_lo_ready, u - 2)
                        pe.wait_ge(w_hi_ready, u - 2)
                        if hp == 3:
                            pe.wait_ge(v_ready, b + 1)
                        if live(b, hp, 4):
                            pe.wait_ge(onorm_ready, u - 3)
                        i = (hp + 1) % 2
                        for h in range(2):
                            for t in range(TT):
                                cols = slice(h * N + t * P, h * N + (t + 1) * P)
                                for j in range(TT):
                                    nc.tensor.matmul(o_at[:, h, t, :], w_hi[:, i, j, cols], v_hi[:, j, :], start=(j == 0), stop=False)
                                    nc.tensor.matmul(o_at[:, h, t, 0:DH], w_hi[:, i, j, cols], v_lo[:, j, :], start=False, stop=False)
                                    last = nc.tensor.matmul(o_at[:, h, t, :], w_lo[:, i, j, cols], v_hi[:, j, :], start=False, stop=(j == TT - 1))
                        last.then_inc(av_done, 1)
                    if live(b, hp, 1):
                        pe.wait_ge(qnorm_ready, u)
                        if hp == 1 and started(b):
                            pe.wait_ge(kt_hi_ready, b + 1)
                            pe.wait_ge(kt_lo_ready, b + 1)
                        elif live(b, hp, 2):
                            pe.wait_ge(qt_hi_ready, u - 1)
                            pe.wait_ge(qt_lo_ready, u - 1)
                        for h in range(2):
                            for t in range(TT):
                                last = nc.tensor.transpose(ps_t[:, h * N + t * P:h * N + (t + 1) * P], q_norm[:, t, h, :], ident[:, :])
                        last.then_inc(q_turned, 1)
                    if started(b):
                        if hp == 0:
                            pe.wait_ge(kv_copied, b + 1)
                        else:
                            pe.wait_ge(qnorm_ready, u)
                        for t in range(TT):
                            for c in range(KC):
                                cols = slice(t * P, (t + 1) * P)
                                heads = slice(hp * 2 * DH, (hp + 1) * 2 * DH)
                                last = mm3(ps_q[:, t, :, :], xs_hi[:, c, cols], xs_lo[:, c, cols],
                                           wq_hi[:, c, heads], wq_lo[:, c, heads], c == 0, c == KC - 1)
                        last.then_inc(q_done, 1)
                    if live(b, hp, 4):
                        pe.wait_ge(onorm_ready, u - 3)
                        if live(b, hp, 5):
                            pe.wait_ge(ot_hi_ready, u - 4)
                            pe.wait_ge(ot_lo_ready, u - 4)
                        for k in range(4):
                            last = nc.tensor.transpose(ps_ot[:, k * P:(k + 1) * P], o_norm[:, k, :], ident[:, :])
                        last.then_inc(o_turned, 1)
                    if live(b, hp, 5):
                        pe.wait_ge(ot_hi_ready, u - 4)
                        pe.wait_ge(ot_lo_ready, u - 4)
                        unit = (hp - 5) % HP
                        if unit == 0 and not first(b):
                            pe.wait_ge(acc_copied, b)
                        i = unit % 2
                        for h in range(2):
                            for t in range(TT):
                                cols = slice(h * N + t * P, h * N + (t + 1) * P)
                                last = mm3(ps_acc[:, t, :], ot_hi[:, i, cols], ot_lo[:, i, cols], wo_hi[:, 2 * unit + h, :], wo_lo[:, 2 * unit + h, :],
                                           unit == 0 and h == 0 and t == 0, unit == HP - 1 and h == 1 and t == TT - 1, skip_group_check=True)
                        last.then_inc(proj_done, 1)

                steps(pe, step)

            @block.scalar
            def _(act):
                def step(b, hp):
                    u = HP * b + hp
                    if hp == 0 and started(b):
                        act.wait_ge(kv_done, b + 1)
                        if not first(b):
                            act.wait_ge(v_ready, b)
                            act.wait_ge(knorm_ready, b)
                        nc.scalar.activation(kv_rows[:, :, :], ps_q[:, :, :, :].rearrange("p t h d -> p t (h d)"), ACT.Copy).then_inc(kv_copied, 1)
                        act.wait_ge(kv_copied, b + 1)
                        nc.scalar.activation(k_sq[:, :, :], kv_rows[:, :, 0:DH], ACT.Square).then_inc(ksq_ready, 1)
                    if live(b, hp, 2):
                        act.wait_ge(s_done, u - 1)
                        if live(b, hp, 3):
                            act.wait_ge(w_lo_ready, u - 2)
                            act.wait_ge(w_hi_ready, u - 2)
                        nc.scalar.activation(w_f[:, :, :], ps_s[:, :, :], ACT.Exp).then_inc(w_ready, 1)
                        act.wait_ge(w_ready, u - 1)
                        if live(b, hp, 4):
                            act.wait_ge(av_done, u - 3)
                        nc.scalar.activation(w_hi[:, hp % 2, :, :], w_f[:, :, :], ACT.Copy).then_inc(w_hi_ready, 1)
                    if hp == 1 and started(b):
                        act.wait_ge(k_turned, b + 1)
                        nc.scalar.activation(kt_hi[:, :], ps_t[:, 0:N], ACT.Copy).then_inc(kt_hi_ready, 1)
                    if live(b, hp, 1):
                        act.wait_ge(q_turned, u)
                        if live(b, hp, 3):
                            act.wait_ge(s_done, u - 2)
                        nc.scalar.activation(qt_hi[:, (hp + 1) % 2, :], ps_t[:, :], ACT.Copy).then_inc(qt_hi_ready, 1)
                    if started(b):
                        act.wait_ge(q_done, u + 1)
                        if live(b, hp, 1):
                            act.wait_ge(qsum_ready, u)
                        nc.scalar.activation(q_sq[:, :, :], ps_q[:, :, :, :].rearrange("p t h d -> p (t h) d"), ACT.Square).then_inc(qsq_ready, 1)
                    if live(b, hp, 4):
                        act.wait_ge(o_turned, u - 3)
                        if live(b, hp, 6):
                            act.wait_ge(proj_done, u - 5)
                        nc.scalar.activation(ot_hi[:, hp % 2, :], ps_ot[:, :], ACT.Copy).then_inc(ot_hi_ready, 1)
                    if hp == 2 and started(b):
                        if not first(b):
                            act.wait_ge(av_done, HP * b)
                        nc.scalar.activation(v_hi[:, :, 0:DH], kv_rows[:, :, DH:2 * DH], ACT.Copy).then_inc(v_hi_ready, 1)
                    if hp == 4 and not first(b):
                        act.wait_ge(proj_done, HP * b)
                        act.wait_ge(ln_out, b)
                        nc.scalar.activation(rows_out[:, :, :], ps_acc[:, :, :], ACT.Copy).then_inc(acc_copied, 1)

                steps(act, step)

            @block.vector
            def _(dve):
                nc.vector.memset(ones2[:, :, :], 1.0).then_inc(v_ones, 1)
                nc.vector.memset(o_rstd[:, :], 0.0).then_inc(ln_out, 1)
                dve.wait_ge(v_ones, 1)
                nc.vector.tensor_copy(v_hi[:, :, DH:VW], ones2[:, :, :]).then_inc(v_ones, 1)

                def split_x(b):
                    cols = slice(b * N, (b + 1) * N) if isinstance(b, int) else bass.ds(b * N, N)
                    nc.vector.tensor_copy(xs_hi[:, :, :], xa_t[:, :, cols]).then_inc(xs_hi_ready, 1)
                    dve.wait_ge(xs_hi_ready, b + 1)
                    nc.vector.tensor_tensor(xs_lo[:, :, :], xa_t[:, :, cols], xs_hi[:, :, :].bitcast(F32), ALU.subtract).then_inc(xs_ready, 1)

                def step(b, hp):
                    u = HP * b + hp
                    if hp % SEND == 0 and started(b):
                        i = hp // SEND
                        t = slice(2 * b + i, 2 * b + i + 1) if isinstance(b, int) else bass.ds(2 * b + i, 1)
                        if not first(b):
                            dve.wait_ge(rows_sent[i], 16 * SEND * b)
                        nc.vector.tensor_copy(row_stage[:, i:i + 1, :], x_sb[:, t, :])
                        nc.vector.tensor_copy(slot_stage[:, i:i + 1, :], slots[:, t, :]).then_inc(rows_staged, 1)
                    if hp == 0 and started(b):
                        if not first(b):
                            dve.wait_ge(q_done, u)
                        split_x(b)
                        dve.wait_ge(ksq_ready, b + 1)
                        nc.vector.tensor_reduce(k_sum[:, :], k_sq[:, :, :], AX_X, ALU.add).then_inc(k_link, 1)
                        dve.wait_ge(k_link, b + 1)
                        nc.vector.tensor_scalar(k_var[:, :], k_sum[:, :], 1.0 / SCALE, L2_EPS / SCALE, ALU.mult, ALU.add).then_inc(ksum_ready, 1)
                    if hp == 1 and started(b):
                        dve.wait_ge(kscale_ready, b + 1)
                        if not first(b):
                            dve.wait_ge(k_turned, b)
                        nc.vector.tensor_tensor(k_norm[:, :, :], kv_rows[:, :, 0:DH], bcast(k_scale[:, :].unsqueeze(2), [P, TT, DH]),
                                                ALU.mult).then_inc(knorm_ready, 1)
                        dve.wait_ge(kt_hi_ready, b + 1)
                        nc.vector.tensor_tensor(kt_lo[:, :], ps_t[:, 0:N], kt_hi[:, :].bitcast(F32), ALU.subtract).then_inc(kt_lo_ready, 1)
                    if live(b, hp, 2):
                        dve.wait_ge(w_hi_ready, u - 1)
                        i = hp % 2
                        nc.vector.tensor_tensor(w_lo[:, i, :, :], w_f[:, :, :], w_hi[:, i, :, :].bitcast(F32), ALU.subtract).then_inc(w_lo_ready, 1)
                    if live(b, hp, 3):
                        dve.wait_ge(av_done, u - 2)
                        nc.vector.reciprocal(w_rec[:, :].rearrange("p (h t) -> p h t", h=2), o_at[:, :, :, DH]).then_inc(rec_ready, 1)
                        dve.wait_ge(rec_ready, u - 2)
                        if live(b, hp, 4):
                            dve.wait_ge(o_turned, u - 3)
                        nc.vector.tensor_tensor(o_norm[:, :, :].rearrange("p (h t) d -> p h t d", h=2), o_at[:, :, :, 0:DH],
                                                bcast(w_rec[:, :].rearrange("p (h t) -> p h t", h=2).unsqueeze(3), [P, 2, TT, DH]),
                                                ALU.mult).then_inc(onorm_ready, 1)
                    if live(b, hp, 1):
                        i = (hp + 1) % 2
                        dve.wait_ge(qt_hi_ready, u)
                        nc.vector.tensor_tensor(qt_lo[:, i, :], ps_t[:, :], qt_hi[:, i, :].bitcast(F32), ALU.subtract).then_inc(qt_lo_ready, 1)
                    if started(b):
                        dve.wait_ge(qsq_ready, u + 1)
                        nc.vector.tensor_reduce(q_sum[:, :], q_sq[:, :, :], AX_X, ALU.add).then_inc(q_link, 1)
                        dve.wait_ge(q_link, u + 1)
                        nc.vector.tensor_scalar(q_var[:, :], q_sum[:, :], 1.0 / SCALE, L2_EPS / (SCALE * SCALE * SCALE), ALU.mult, ALU.add).then_inc(qsum_ready, 1)
                    if live(b, hp, 4):
                        i = hp % 2
                        dve.wait_ge(ot_hi_ready, u - 3)
                        nc.vector.tensor_tensor(ot_lo[:, i, :], ps_ot[:, :], ot_hi[:, i, :].bitcast(F32), ALU.subtract).then_inc(ot_lo_ready, 1)
                    if started(b):
                        dve.wait_ge(qscale_ready, u + 1)
                        if live(b, hp, 1):
                            dve.wait_ge(q_turned, u)
                        nc.vector.tensor_tensor(q_norm[:, :, :, :].rearrange("p t h d -> p (t h) d"),
                                                ps_q[:, :, :, :].rearrange("p t h d -> p (t h) d"),
                                                bcast(q_scale[:, :].unsqueeze(2), [P, 4, DH]), ALU.mult).then_inc(qnorm_ready, 1)
                    if hp == 4 and not first(b):
                        dve.wait_ge(acc_copied, b)
                        for t in range(TT):
                            last = nc.vector.bn_stats(o_stats[:, t, :], rows_out[:, t, :])
                        last.then_inc(k_link2, 1)
                        dve.wait_ge(k_link2, 4 * b - 3)
                        nc.vector.memset(spare[:, 7:8], 0.0)
                        for t in range(TT):
                            last = nc.vector.bn_aggr(o_mv[:, t, :], o_stats[:, t, :])
                        last.then_inc(k_link2, 1)
                        dve.wait_ge(k_link2, 4 * b - 2)
                        nc.vector.tensor_scalar(o_var[:, :], o_mv[:, :, 1], EPS, None, ALU.add).then_inc(ovar_ready, 1)
                        dve.wait_ge(orstd_ready, b)
                        for t in range(TT):
                            last = nc.vector.tensor_scalar(rows_out[:, t, :], rows_out[:, t, :], o_mv[:, t, 0:1], o_rstd[:, t:t + 1], ALU.subtract, ALU.mult)
                            last.then_inc(k_link2, 1)
                        dve.wait_ge(k_link2, 4 * b)
                        if isinstance(b, int):
                            dst = attn_out[:, (b - 1) * TT:b * TT, :]
                        else:
                            dst = attn_out[:, bass.ds(b * TT - TT, TT), :]
                        nc.vector.tensor_tensor(dst, rows_out[:, :, :], bcast(g_out_b[:, :].unsqueeze(1), [P, TT, D]), ALU.mult).then_inc(ln_out, 1)

                k_link2 = sem("out_link")
                steps(dve, step)

            @block.gpsimd
            def _(pool):
                pool.wait_ge(v_ones, 2)

                def step(b, hp):
                    u = HP * b + hp
                    if hp == 0 and started(b):
                        pool.wait_ge(ksum_ready, b + 1)
                        nc.gpsimd.tensor_tensor(k_scale[:, :], k_var[:, :], minus_half[:, 0:2], ALU.pow).then_inc(kscale_ready, 1)
                    if started(b):
                        i, k = hp // SEND, hp % SEND
                        pool.wait_ge(rows_staged, 2 * b + i + 1)
                        pool.wait_ge(qsum_ready, u + 1)
                        nc.gpsimd.tensor_tensor(q_scale[:, :], q_var[:, :], minus_half[:, 0:4], ALU.pow).then_inc(qscale_ready, 1)
                        nc.gpsimd.indirect_dma_start(slot_x, bass.IndirectOffsetOnAxis(slot_stage[:, i, k:k + 1], 0), row_stage[:, i, :], None).then_inc(rows_sent[i], 16)
                    if hp == 2 and started(b):
                        pool.wait_ge(v_hi_ready, b + 1)
                        nc.gpsimd.tensor_tensor(v_lo[:, :, :], kv_rows[:, :, DH:2 * DH], v_hi[:, :, 0:DH].bitcast(F32), ALU.subtract).then_inc(v_ready, 1)
                    if hp == 4 and not first(b):
                        pool.wait_ge(ovar_ready, b)
                        nc.gpsimd.tensor_tensor(o_rstd[:, :], o_var[:, :], minus_half[:, 0:TT], ALU.pow).then_inc(orstd_ready, 1)

                steps(pool, step)
        work_ps.close()
        work.close()
        attention.close()

        tail = ExitStack()
        experts = ExitStack()
        NBUF = 2
        WBUF = 4
        x_in = sbuf(experts, "x_in", [P, WBUF, 2, D])
        we_raw = sbuf(experts, "we_raw", [P, WBUF, 2, WE])
        we_hi = sbuf(experts, "we_hi", [P, WBUF, 2, WE], F32R)
        we_lo = sbuf(experts, "we_lo", [P, WBUF, 2, WE], F32R)
        xe_hi = sbuf(experts, "xe_hi", [P, NBUF, KC, 2 * P], F32R)
        xe_lo = sbuf(experts, "xe_lo", [P, NBUF, KC, 2 * P], F32R)
        gate_e = sbuf(experts, "gate_e", [P, NBUF, 2 * P])
        hid_e = sbuf(experts, "hid_e", [F, NBUF, 2 * P])
        he = sbuf(experts, "he", [P, NBUF, 2 * P], F32R)
        y_out = sbuf(experts, "y_out", [P, WBUF, 2, D])
        owners = sbuf(experts, "owners", [1, NB], U32)
        DOWN = KC * 2 * F

        experts_ps = ExitStack()
        ps_x = [psum(experts_ps, f"ps_x{i}", [P, KC, 2 * P]) for i in range(NBUF)]
        ps_gu = [psum(experts_ps, f"ps_gu{i}", [P, 512]) for i in range(NBUF)]
        ps_y = [psum(experts_ps, f"ps_y{i}", [P, 2, D]) for i in range(NBUF)]

        owners_loaded = sem("owners_loaded")
        xe_loaded = [sem(f"xe_loaded{i}") for i in range(WBUF)]
        we_loaded = [sem(f"we_loaded{i}") for i in range(WBUF)]
        xe_turned = sem("xe_turned")
        xe_hi_ready = sem("xe_hi_ready")
        xe_lo_ready = sem("xe_lo_ready")
        we_hi_ready = sem("we_hi_ready")
        we_lo_ready = sem("we_lo_ready")
        gu_done = sem("gu_done")
        gate_ready = sem("gate_ready")
        hid_ready = sem("hid_ready")
        he_hi_ready = sem("he_hi_ready")
        he_lo_ready = sem("he_lo_ready")
        y_done = sem("y_done")
        y_copied = sem("y_copied")
        y_stored = [sem(f"y_stored{i}") for i in range(WBUF)]

        def duos(eng, step, late):
            for d in range(2 * WBUF):
                step(d, d % WBUF, d // WBUF)
            with eng.Fori(2, DUOS // WBUF) as j:
                for i in range(WBUF):
                    step(WBUF * j + i, i, j)
            for i in range(late):
                step(DUOS + i, i % WBUF, (DUOS + i) // WBUF)

        def on(d, lag):
            return not isinstance(d, int) or 0 <= d - lag < DUOS

        with nc.Block() as block:
            @block.sync
            def _(sp):
                sp.dma_start(owners[:, :], block_expert.rearrange("n o -> o n")).then_inc(owners_loaded, 16)
                sp.wait_ge(owners_loaded, 16)
                for i in range(2):
                    sp.wait_ge(rows_sent[i], 16 * SEND * B)
                slots_of = slot_x.rearrange("(j k p) d -> j p k d", k=2, p=P)

                def step(d, i, j):
                    if on(d, 4):
                        sp.wait_ge(xe_turned, d - 3)
                    src = slots_of[d] if isinstance(d, int) else slots_of[bass.ds(d, 1)].rearrange("j p k d -> p (j k) d")
                    sp.dma_start(x_in[:, i, :, :], src).then_inc(xe_loaded[i], 16)
                    if on(d, 4):
                        sp.wait_ge(we_lo_ready, d - 3)
                    for k in range(2):
                        at = owners[0:1, 2 * d + k:2 * d + k + 1] if isinstance(d, int) else owners[0:1, bass.ds(2 * d + k, 1)]
                        e = sp.value_load(at, min_val=0, max_val=E - 1)
                        sp.dma_start(we_raw[:, i, k, :], w_expert[bass.ds(e, 1)].rearrange("e p n -> p (e n)")).then_inc(we_loaded[i], 16)
                duos(sp, step, 0)

            @block.tensor
            def _(pe):
                def step(d, i, j):
                    n = i % 2
                    if on(d, 0):
                        pe.wait_ge(xe_loaded[i], 16 * (j + 1))
                        if on(d, 2):
                            pe.wait_ge(xe_hi_ready, d - 1)
                            pe.wait_ge(xe_lo_ready, d - 1)
                        for c in range(KC):
                            for k in range(2):
                                last = nc.tensor.transpose(ps_x[n][:, c, k * P:(k + 1) * P], x_in[:, i, k, c * P:(c + 1) * P], ident[:, :])
                        last.then_inc(xe_turned, 1)
                    if on(d, 3):
                        pe.wait_ge(he_hi_ready, d - 2)
                        pe.wait_ge(he_lo_ready, d - 2)
                        if on(d, 5):
                            pe.wait_ge(y_copied, d - 4)
                        w = (i + 1) % WBUF
                        for k in range(2):
                            cols = slice(k * P, (k + 1) * P)
                            dst = ps_y[1 - n][:, k, :]
                            nc.tensor.matmul(dst, he[:, 1 - n, cols], we_hi[:, w, k, DOWN:WE], start=True, stop=False)
                            last = nc.tensor.matmul(dst, he[0:F, 1 - n, cols], we_lo[0:F, w, k, DOWN:WE], start=False, stop=True)
                        last.then_inc(y_done, 1)
                    if on(d, 1):
                        pe.wait_ge(xe_hi_ready, d)
                        pe.wait_ge(xe_lo_ready, d)
                        pe.wait_ge(we_hi_ready, d)
                        pe.wait_ge(we_lo_ready, d)
                        if on(d, 3):
                            pe.wait_ge(gate_ready, d - 2)
                            pe.wait_ge(hid_ready, d - 2)
                        w = (i - 1) % WBUF
                        for k in range(2):
                            cols = slice(k * P, (k + 1) * P)
                            dst = ps_gu[1 - n][:, cols]
                            for c in range(KC):
                                of = slice(c * 2 * F, (c + 1) * 2 * F)
                                nc.tensor.matmul(dst, we_hi[:, w, k, of], xe_hi[:, 1 - n, c, cols], start=(c == 0), stop=False)
                                nc.tensor.matmul(dst, we_hi[:, w, k, of], xe_lo[:, 1 - n, c, cols], start=False, stop=False)
                                last = nc.tensor.matmul(dst, we_lo[:, w, k, of], xe_hi[:, 1 - n, c, cols], start=False, stop=(c == KC - 1))
                        last.then_inc(gu_done, 1)
                duos(pe, step, 3)

            @block.scalar
            def _(act):
                def step(d, i, j):
                    n = i % 2
                    if on(d, 2):
                        act.wait_ge(gu_done, d - 1)
                        if on(d, 4):
                            act.wait_ge(hid_ready, d - 3)
                        nc.scalar.activation(gate_e[F:P, n, :], ps_gu[n][0:F, 0:2 * P], ACT.Silu).then_inc(gate_ready, 1)
                    if on(d, 0):
                        act.wait_ge(xe_turned, d + 1)
                        nc.scalar.activation(xe_hi[:, n, :, :], ps_x[n][:, :, :], ACT.Copy).then_inc(xe_hi_ready, 1)
                    if on(d, 2):
                        act.wait_ge(hid_ready, d - 1)
                        if on(d, 4):
                            act.wait_ge(y_done, d - 3)
                        nc.scalar.activation(he[0:F, n, :], hid_e[:, n, :], ACT.Copy).then_inc(he_hi_ready, 1)
                    if on(d, 0):
                        act.wait_ge(we_loaded[i], 32 * (j + 1))
                        if on(d, 4):
                            act.wait_ge(y_done, d - 3)
                        nc.scalar.activation(we_hi[:, i, :, :], we_raw[:, i, :, :], ACT.Copy).then_inc(we_hi_ready, 1)
                    if on(d, 4):
                        act.wait_ge(y_copied, d - 3)
                        dst = slot_y.rearrange("(j k p) d -> j p k d", k=2, p=P)
                        dst = dst[d - 4] if isinstance(d, int) else dst[bass.ds(d - 4, 1)].rearrange("j p k d -> p (j k) d")
                        act.dma_start(dst, y_out[:, i, :, :]).then_inc(y_stored[i], 16)
                duos(act, step, 4)
                for i in range(WBUF):
                    act.wait_ge(y_stored[i], 16 * DUOS // WBUF)

            @block.gpsimd
            def _(pool):
                def step(d, i, j):
                    pool.wait_ge(we_hi_ready, d + 1)
                    nc.gpsimd.tensor_tensor(we_lo[:, i, :, :], we_raw[:, i, :, :], we_hi[:, i, :, :].bitcast(F32), ALU.subtract).then_inc(we_lo_ready, 1)
                duos(pool, step, 0)

            @block.vector
            def _(dve):
                def step(d, i, j):
                    n = i % 2
                    if on(d, 2):
                        dve.wait_ge(gate_ready, d - 1)
                        if on(d, 4):
                            dve.wait_ge(he_lo_ready, d - 3)
                            dve.wait_ge(he_hi_ready, d - 3)
                        nc.vector.tensor_tensor(hid_e[:, n, :], ps_gu[n][F:P, 0:2 * P], gate_e[F:P, n, :], ALU.mult).then_inc(hid_ready, 1)
                    if on(d, 0):
                        dve.wait_ge(xe_hi_ready, d + 1)
                        nc.vector.tensor_tensor(xe_lo[:, n, :, :], ps_x[n][:, :, :], xe_hi[:, n, :, :].bitcast(F32), ALU.subtract).then_inc(xe_lo_ready, 1)
                    if on(d, 2):
                        dve.wait_ge(he_hi_ready, d - 1)
                        nc.vector.tensor_tensor(he[F:P, n, :], hid_e[:, n, :], he[0:F, n, :].bitcast(F32), ALU.subtract).then_inc(he_lo_ready, 1)
                    if on(d, 3):
                        dve.wait_ge(y_done, d - 2)
                        if on(d, 7):
                            dve.wait_ge(y_stored[(i + 1) % WBUF], 16 * (j if i == WBUF - 1 else j - 1))
                        nc.vector.tensor_copy(y_out[:, (i + 1) % WBUF, :, :], ps_y[1 - n][:, :, :]).then_inc(y_copied, 1)
                duos(dve, step, 3)
        experts_ps.close()
        experts.close()

        WS = w_shared.shape[2]
        sh_raw = sbuf(tail, "sh_raw", [P, SH, WS])
        sh_hi = sbuf(tail, "sh_hi", [P, SH, WS], F32R)
        sh_lo = sbuf(tail, "sh_lo", [P, SH, WS], F32R)
        xh = sbuf(tail, "xh", [P, KC, TOK], F32R)
        xl = sbuf(tail, "xl", [P, KC, TOK], F32R)
        gate_s = sbuf(tail, "gate_s", [P, 2, TG])
        hid_s = sbuf(tail, "hid_s", [P, 2, TG])
        hs_hi = sbuf(tail, "hs_hi", [P, 2, TG], F32R)
        hs_lo = sbuf(tail, "hs_lo", [P, 2, TG], F32R)
        picks = sbuf(tail, "picks", [P, GT, TOPK, D])
        slot_now = sbuf(tail, "slot_now", [P, GT, TOPK], U32)
        gate_now = sbuf(tail, "gate_now", [P, GT, TOPK])
        pace = sbuf(tail, "pace", [P, GT])
        x_back = sbuf(tail, "x_back", [P, GT, D])
        total = sbuf(tail, "total", [P, GT, D])
        tail_ps = ExitStack()
        ps_sg = [psum(tail_ps, f"ps_sg{i}", [P, TG]) for i in range(2)]
        ps_su = [psum(tail_ps, f"ps_su{i}", [P, TG]) for i in range(2)]
        ps_sy = psum(tail_ps, "ps_sy", [P, GT, D])

        sh_loaded = sem("sh_loaded")
        sh_hi_ready = sem("sh_hi_ready")
        sh_lo_ready = sem("sh_lo_ready")
        xh_ready = sem("xh_ready")
        xl_ready = sem("xl_ready")
        sgu_done = sem("sgu_done")
        sgate_ready = sem("sgate_ready")
        shid_ready = sem("shid_ready")
        hs_hi_ready = sem("hs_hi_ready")
        hs_lo_ready = sem("hs_lo_ready")
        sy_done = sem("sy_done")
        slots_now = sem("slots_now")
        picked_in = [sem(f"picked_in{i}") for i in range(GT)]
        sum_step = sem("sum_step")
        paced = sem("paced")
        summed = sem("summed")
        silu_done = sem("silu_done")
        gated = sem("gated")
        x_again = sem("x_again")
        added = sem("added")
        out_stored = sem("out_stored")

        def groups(eng, body):
            body(0, True)
            with eng.Fori(1, NTG) as g:
                body(g, False)

        with nc.Block() as block:
            @block.sync
            def _(sp):
                sp.dma_start(sh_raw[:, :, :], w_shared).then_inc(sh_loaded, 16)

                def body(g, early):
                    tiles = slice(0, GT) if early else bass.ds(g * GT, GT)
                    if not early:
                        sp.wait_ge(added, GT * g)
                    sp.dma_start(x_back[:, :, :], x_rows[:, tiles, :]).then_inc(x_again, 16)
                    sp.wait_ge(added, GT * g + GT)
                    sp.dma_start(out_rows[:, tiles, :], total[:, :, :]).then_inc(out_stored, 16)
                groups(sp, body)
                sp.wait_ge(out_stored, 16 * NTG)

            @block.gpsimd
            def _(pool):
                def body(g, early):
                    pool.wait_ge(slots_now, g + 1)
                    if not early:
                        pool.wait_ge(paced, GT * g)
                    for i in range(GT):
                        if not early:
                            pool.wait_ge(summed, GT * (g - 1) + i + 1)
                        nc.gpsimd.tensor_tensor(pace[:, i:i + 1], minus_half[:, 0:1], minus_half[:, 1:2], ALU.add).then_inc(paced, 1)
                        for k in range(TOPK):
                            nc.gpsimd.indirect_dma_start(picks[:, i, k, :], None, slot_y, bass.IndirectOffsetOnAxis(slot_now[:, i, k:k + 1], 0)).then_inc(picked_in[i], 16)
                groups(pool, body)

            @block.tensor
            def _(pe):
                def mm3(dst, l_hi, l_lo, r_hi, r_lo, start, stop, **kw):
                    nc.tensor.matmul(dst, l_hi, r_hi, start=start, stop=False, **kw)
                    nc.tensor.matmul(dst, l_hi, r_lo, start=False, stop=False, **kw)
                    return nc.tensor.matmul(dst, l_lo, r_hi, start=False, stop=stop, **kw)

                def up(g, h, early):
                    n = SH * g + h
                    if not (early and h < 2):
                        pe.wait_ge(sgate_ready, n - 1)
                        pe.wait_ge(shid_ready, n - 1)
                    cols = slice(0, TG) if early else bass.ds(g * TG, TG)
                    for ps, at in ((ps_sg, 0), (ps_su, KC * P)):
                        for c in range(KC):
                            w = slice(at + c * P, at + (c + 1) * P)
                            last = mm3(ps[h % 2][:, :], sh_hi[:, h, w], sh_lo[:, h, w], xh[:, c, cols], xl[:, c, cols], c == 0, c == KC - 1)
                    last.then_inc(sgu_done, 1)

                def down(g, h, early):
                    n = SH * g + h
                    pe.wait_ge(hs_hi_ready, n + 1)
                    pe.wait_ge(hs_lo_ready, n + 1)
                    if h == 0 and not early:
                        pe.wait_ge(summed, GT * g)
                    w = slice(2 * KC * P, 2 * KC * P + D)
                    for t in range(GT):
                        cols = slice(t * P, (t + 1) * P)
                        last = mm3(ps_sy[:, t, :], hs_hi[:, h % 2, cols], hs_lo[:, h % 2, cols], sh_hi[:, h, w], sh_lo[:, h, w],
                                   h == 0 and t % 2 == 0, h == SH - 1 and t % 2 == 1, skip_group_check=True)
                    last.then_inc(sy_done, 1)

                def body(g, early):
                    for h in range(SH):
                        up(g, h, early)
                        if h:
                            down(g, h - 1, early)
                    down(g, SH - 1, early)
                pe.wait_ge(sh_lo_ready, 1)
                pe.wait_ge(xl_ready, NTG)
                groups(pe, body)

            @block.scalar
            def _(act):
                for q in range(NTG):
                    cols = slice(q * TG, (q + 1) * TG)
                    nc.scalar.activation(xh[:, :, cols], xn_t[:, :, cols], ACT.Copy).then_inc(xh_ready, 1)
                act.wait_ge(sh_loaded, 16)
                nc.scalar.activation(sh_hi[:, :, :], sh_raw[:, :, :], ACT.Copy).then_inc(sh_hi_ready, 1)

                def body(g, early):
                    for h in range(SH):
                        n = SH * g + h
                        act.wait_ge(sgu_done, n + 1)
                        if not (early and h < 2):
                            act.wait_ge(shid_ready, n - 1)
                        nc.scalar.activation(gate_s[:, h % 2, :], ps_sg[h % 2][:, :], ACT.Silu).then_inc(sgate_ready, 1)
                        act.wait_ge(shid_ready, n + 1)
                        if not (early and h < 2):
                            act.wait_ge(sy_done, n - 1)
                        nc.scalar.activation(hs_hi[:, h % 2, :], hid_s[:, h % 2, :], ACT.Copy).then_inc(hs_hi_ready, 1)
                    for i in range(GT):
                        act.wait_ge(summed, GT * g + i + 1)
                        nc.scalar.activation(total[:, i, :], total[:, i, :], ACT.Silu).then_inc(silu_done, 1)
                groups(act, body)

            @block.vector
            def _(dve):
                for q in range(NTG):
                    cols = slice(q * TG, (q + 1) * TG)
                    dve.wait_ge(xh_ready, q + 1)
                    nc.vector.tensor_tensor(xl[:, :, cols], xn_t[:, :, cols], xh[:, :, cols].bitcast(F32), ALU.subtract).then_inc(xl_ready, 1)
                dve.wait_ge(sh_hi_ready, 1)
                nc.vector.tensor_tensor(sh_lo[:, :, :], sh_raw[:, :, :], sh_hi[:, :, :].bitcast(F32), ALU.subtract).then_inc(sh_lo_ready, 1)

                def low(n, h, early):
                    dve.wait_ge(hs_hi_ready, n + 1)
                    if not (early and h < 2):
                        dve.wait_ge(sy_done, n - 1)
                    nc.vector.tensor_tensor(hs_lo[:, h % 2, :], hid_s[:, h % 2, :], hs_hi[:, h % 2, :].bitcast(F32), ALU.subtract).then_inc(hs_lo_ready, 1)

                def body(g, early):
                    tiles = slice(0, GT) if early else bass.ds(g * GT, GT)
                    if not early:
                        for i in range(GT):
                            dve.wait_ge(picked_in[i], 16 * TOPK * g)
                    nc.vector.tensor_copy(slot_now[:, :, :], slots[:, tiles, :])
                    nc.vector.tensor_copy(gate_now[:, :, :], gates[:, tiles, :]).then_inc(slots_now, 1)
                    dve.wait_ge(slots_now, g + 1)
                    for h in range(SH):
                        n = SH * g + h
                        dve.wait_ge(sgate_ready, n + 1)
                        if not (early and h < 2):
                            dve.wait_ge(hs_lo_ready, n - 1)
                            dve.wait_ge(hs_hi_ready, n - 1)
                        nc.vector.tensor_tensor(hid_s[:, h % 2, :], ps_su[h % 2][:, :], gate_s[:, h % 2, :], ALU.mult).then_inc(shid_ready, 1)
                        if h:
                            low(n - 1, h - 1, early)
                    low(SH * g + SH - 1, SH - 1, early)
                    dve.wait_ge(sy_done, SH * (g + 1))
                    if not early:
                        dve.wait_ge(out_stored, 16 * g)
                    for k in range(TOPK):
                        for i in range(GT):
                            if k == 0:
                                dve.wait_ge(picked_in[i], 16 * TOPK * (g + 1))
                            ins = nc.vector.scalar_tensor_tensor(total[:, i, :], picks[:, i, k, :], gate_now[:, i, k:k + 1],
                                                                 ps_sy[:, i, :] if k == 0 else total[:, i, :], ALU.mult, ALU.add)
                            if k == TOPK - 1:
                                ins.then_inc(summed, 1)
                        if k < TOPK - 1:
                            ins.then_inc(sum_step, 1)
                            dve.wait_ge(sum_step, (TOPK - 1) * g + k + 1)
                    dve.wait_ge(x_again, 16 * (g + 1))
                    for i in range(GT):
                        dve.wait_ge(silu_done, GT * g + i + 1)
                        rows = slice(i, i + 1) if early else bass.ds(g * GT + i, 1)
                        nc.vector.tensor_tensor(total[:, i:i + 1, :], total[:, i:i + 1, :], attn_out[:, rows, :], ALU.mult).then_inc(gated, 1)
                    for i in range(GT):
                        dve.wait_ge(gated, GT * g + i + 1)
                        nc.vector.tensor_tensor(total[:, i, :], total[:, i, :], x_back[:, i, :], ALU.add).then_inc(added, 1)
                groups(dve, body)
        tail_ps.close()
        tail.close()


def kernel(L0_attn_x, L0_attn_g_norm, L0_attn_Wq, L0_attn_Wkv, L0_attn_Wout, L0_attn_g_out, L0_ffn_Wr,
           L0_ffn_router_bias, L0_ffn_affinity, L0_ffn_te_W1, L0_ffn_te_b1, L0_ffn_te_W2, L0_ffn_te_b2,
           L0_ffn_Wg, L0_ffn_Wu, L0_ffn_Wd, L0_ffn_Sg, L0_ffn_Su, L0_ffn_Sd):
    import numpy as np
    import concourse.bacc as bacc
    from concourse import mybir as mb
    from concourse.bass_utils import run_bass_kernel_spmd as run

    E, D, F = L0_ffn_Wg.shape
    NS, _, H = L0_ffn_Sg.shape
    C = D // 128

    def by_chunk(w, n):
        return w.reshape(-1, C, 128, n).transpose(0, 2, 1, 3).reshape(-1, 128, C * n)

    def shared_up(w):
        return by_chunk(w.reshape(NS, D, H // 128, 128).transpose(0, 2, 1, 3), 128)

    shared = np.concatenate([shared_up(L0_ffn_Sg), shared_up(L0_ffn_Su), L0_ffn_Sd.reshape(-1, 128, D)], axis=2)
    arrays = {
        "x": L0_attn_x, "wq": L0_attn_Wq, "wkv": L0_attn_Wkv, "wout": L0_attn_Wout,
        "g_norm": L0_attn_g_norm.reshape(D // 128, 128).T, "g_out": L0_attn_g_out,
        "wr_t": L0_ffn_Wr.T, "r_bias": L0_ffn_router_bias, "aff_t": L0_ffn_affinity.T,
        "w1_t": L0_ffn_te_W1.T, "b1": L0_ffn_te_b1[:, None], "w2_t": L0_ffn_te_W2.T, "b2": L0_ffn_te_b2,
        "w_expert": np.concatenate([by_chunk(np.concatenate([L0_ffn_Wg, L0_ffn_Wu], axis=2), 2 * F),
                                    np.concatenate([L0_ffn_Wd, L0_ffn_Wd], axis=1)], axis=2),
        "w_shared": shared.transpose(1, 0, 2),
        "ident_in": np.eye(128, dtype=np.float32), "tri_in": np.triu(np.ones((128, 128), np.float32), 1),
        "iota_in": np.arange(128, dtype=np.float32),
    }
    arrays = {k: np.ascontiguousarray(v) for k, v in arrays.items()}
    nc = bacc.Bacc("TRN2", target_bir_lowering=False, num_devices=1)
    args = [nc.dram_tensor(k, v.shape, mb.dt.from_np(v.dtype), kind="ExternalInput").ap() for k, v in arrays.items()]
    out = nc.dram_tensor("out", L0_attn_x.shape, mb.dt.float32, kind="ExternalOutput").ap()
    build(nc, *args, out)
    r = run(nc, [arrays], core_ids=[0])
    return r.results[0]["out"]
```

```python
from contextlib import ExitStack

import concourse.bass as bass
from concourse import mybir

F32 = mybir.dt.float32
F32R = mybir.dt.float32r
U32 = mybir.dt.uint32
I32 = mybir.dt.int32
BF16 = mybir.dt.bfloat16
ALU = mybir.AluOpType
ACT = mybir.ActivationFunctionType
AX_X = mybir.AxisListType.X

P = 128
EPS = 1e-5
L2_EPS = 1e-12
SCALE = 16.0
TOPK = 4


def build(nc, x, wq, wkv, wout, g_norm, g_out, wr_t, r_bias, aff_t, w1_t, b1, w2_t, b2, w_expert, w_shared, ident_in, tri_in, iota_in, out):
    B, N, D = x.shape
    HID = wq.shape[1]
    DH = P
    HEADS = HID // DH
    E = wr_t.shape[1]
    ND = w2_t.shape[1]
    F = P // 2
    WE = w_expert.shape[2]
    WS = w_shared.shape[1]
    SHC = WS // (2 * (D // P) + D // P)
    TOK = B * N
    TT = N // P
    KC = D // P
    TILES = TOK // P
    HP = HEADS // 2
    PAIR = 2 * N
    GT = 4
    NG = TILES // GT
    NB = TOK * TOPK // P + E
    SLOTS = NB * P
    DUOS = NB // 2
    assert TT == 2 and KC == 2 and HP == 8 and PAIR == 512

    x_rows = x.rearrange("b (t p) d -> p (b t) d", p=P)
    out_rows = out.rearrange("b (t p) d -> p (b t) d", p=P)
    slot_x = nc.dram_tensor("slot_x", (SLOTS, D), F32, kind="Internal").ap()
    slot_y = nc.dram_tensor("slot_y", (SLOTS, D), F32, kind="Internal").ap()
    block_expert = nc.dram_tensor("block_expert", (NB, 1), U32, kind="Internal").ap()

    with ExitStack() as whole:
        def sem(name):
            return whole.enter_context(nc.semaphore(name))

        def sbuf(ctx, name, shape, dt=F32):
            return ctx.enter_context(nc.sbuf_tensor(name, shape, dt))

        def psum(ctx, name, shape, dt=F32):
            return ctx.enter_context(nc.psum_tensor(name, shape, dt))

        def bcast(a, shape):
            return a.to_broadcast(shape)

        x_sb = sbuf(whole, "x_sb", [P, TILES, D])
        xn_t = sbuf(whole, "xn_t", [P, KC, TOK])
        attn_out = sbuf(whole, "attn_out", [P, TILES, D])
        ident = sbuf(whole, "ident", [P, P])
        slots = sbuf(whole, "slots", [P, TILES, TOPK], U32)
        gates = sbuf(whole, "gates", [P, TILES, TOPK])
        owners = sbuf(whole, "owners", [1, NB], U32)
        minus_half = sbuf(whole, "minus_half", [P, 8])
        spare = sbuf(whole, "spare", [P, 8])

        g_out_b = sbuf(whole, "g_out_b", [P, D])
        o_stats = sbuf(whole, "o_stats", [P, TT, 6])
        o_mv = sbuf(whole, "o_mv", [P, TT, 2])
        o_var = sbuf(whole, "o_var", [P, TT])
        o_rstd = sbuf(whole, "o_rstd", [P, TT])
        sh_raw = sbuf(whole, "sh_raw", [P, WS])

        attention = ExitStack()
        xa_t = sbuf(attention, "xa_t", [P, KC, TOK])
        wq_hi = sbuf(attention, "wq_hi", [P, KC, HID], F32R)
        wq_lo = sbuf(attention, "wq_lo", [P, KC, HID], F32R)
        wkv_hi = sbuf(attention, "wkv_hi", [P, KC, 2 * DH], F32R)
        wkv_lo = sbuf(attention, "wkv_lo", [P, KC, 2 * DH], F32R)
        wo_hi = sbuf(attention, "wo_hi", [P, HEADS, D], F32R)
        wo_lo = sbuf(attention, "wo_lo", [P, HEADS, D], F32R)

        prep = ExitStack()
        wo_raw = sbuf(prep, "wo_raw", [P, HEADS, D])
        wkv_raw = sbuf(prep, "wkv_raw", [P, KC, 2 * DH])
        xn_stat = sbuf(prep, "xn_stat", [P, 2, KC, N])
        g_col = sbuf(prep, "g_col", [P, KC])
        wr_sb = sbuf(prep, "wr_sb", [P, KC, E])
        w1_sb = sbuf(prep, "w1_sb", [P, KC, P])
        b1_sb = sbuf(prep, "b1_sb", [P, 1])
        w2_sb = sbuf(prep, "w2_sb", [P, ND])
        b2_b = sbuf(prep, "b2_b", [P, ND])
        aff_b = sbuf(prep, "aff_b", [P, ND, E])
        rbias_b = sbuf(prep, "rbias_b", [P, E])
        iota_b = sbuf(prep, "iota_b", [P, E])
        stats = sbuf(prep, "stats", [P, TILES, 6])
        meanvar = sbuf(prep, "meanvar", [P, TILES, 2])
        var_eps = sbuf(prep, "var_eps", [P, TILES])
        rstd = sbuf(prep, "rstd", [P, TILES])
        half_row = sbuf(prep, "half_row", [P, TILES])
        x_sum = sbuf(prep, "x_sum", [P, KC, B])
        raw_logits = sbuf(prep, "raw_logits", [P, TILES, E])
        h1 = sbuf(prep, "h1", [P, B])
        w2_rep = sbuf(prep, "w2_rep", [P, ND, P])
        task = sbuf(prep, "task", [P, B, ND])
        task_s = sbuf(prep, "task_s", [P, B])
        dom, dom_part = (xn_stat[:, k, :, :].rearrange("p c n -> p (c n)").rearrange("p (b e) -> p b e", e=E) for k in range(2))
        assert B * E == KC * N
        choice = sbuf(prep, "choice", [P, TILES, E])
        top = sbuf(prep, "top", [P, TILES, 8])
        top_at = sbuf(prep, "top_at", [P, TILES, 8], U32)
        top_b = sbuf(prep, "top_b", [P, TILES, 8], BF16)
        iota_bf = sbuf(prep, "iota_bf", [P, E], BF16)
        parts = sbuf(prep, "parts", [P, TOPK, TILES, E])
        part = [parts[:, k, :, :] for k in range(TOPK)]
        before_b = sbuf(prep, "before_b", [P, TILES + 1, E], BF16)
        tri_sb = sbuf(prep, "tri_sb", [P, P])
        tri_b = sbuf(prep, "tri_b", [P, P], BF16)
        ones_b = sbuf(prep, "ones_b", [P, P], BF16)
        count_i = sbuf(prep, "count_i", [E, P], I32)
        blocks_i = sbuf(prep, "blocks_i", [E, P], I32)
        blocks_b = sbuf(prep, "blocks_b", [E, P], BF16)
        starts = sbuf(prep, "starts", [P, E])
        begun = sbuf(prep, "begun", [P, E])
        slot_f = sbuf(prep, "slot_f", [P, TILES, TOPK])
        picked = sbuf(prep, "picked", [P, TILES, TOPK])
        row = sbuf(prep, "row", [P, 3, TILES])
        block_no = sbuf(prep, "block_no", [P, 1])
        owner = sbuf(prep, "owner", [P, 1])
        owner_i = sbuf(prep, "owner_i", [P, 1], U32)
        zeros = sbuf(prep, "zeros", [P, D])
        wq_raw = attn_out[:, :, :].rearrange("p t d -> p (t d)").rearrange("p (c n) -> p c n", c=KC)
        picks_b = [attn_out[:, 2 * k:2 * k + 2, :].bitcast(BF16).rearrange("p a (t e) -> p (a t) e", e=E) for k in range(TOPK + 3)]
        hit, mask_part, mask_b = picks_b[:TOPK], picks_b[TOPK:TOPK + 2], picks_b[TOPK + 2]

        xa_rows = parts[:, :, :, :].rearrange("p k t e -> p (k t e)").rearrange("p (t d) -> p t d", d=D)
        assert TOPK * E == D

        prep_ps = ExitStack()
        ps_xn = [psum(prep_ps, f"ps_xn{i}", [P, KC, N]) for i in range(2)]
        ps_logits = [psum(prep_ps, f"ps_logits{i}", [P, TT, E]) for i in range(2)]
        ps_small = psum(prep_ps, "ps_small", [P, 512])
        ps_h1 = ps_small[:, 0:B]
        ps_task = ps_small[:, B:B + B * ND].rearrange("p (a b) -> p b a", a=ND)
        ps_count = ps_small[0:E, P:2 * P]
        ps_starts = ps_small[:, 2 * P:2 * P + E]
        ps_rank = psum(prep_ps, "ps_rank", [P, TILES, E])

        x_loaded = [sem(f"x_loaded{k}") for k in range(2)]
        const_loaded = sem("const_loaded")
        turn_loaded = sem("turn_loaded")
        wq_loaded = sem("wq_loaded")
        wkv_loaded = sem("wkv_loaded")
        wo_loaded = sem("wo_loaded")
        half_set = sem("half_set")
        ln_step = sem("ln_step")
        var_ready = sem("var_ready")
        rstd_ready = sem("rstd_ready")
        xn_ready = sem("xn_ready")
        xa_ready = sem("xa_ready")
        xn_turned = sem("xn_turned")
        xn_copied = sem("xn_copied")
        xn_kept = sem("xn_kept")
        xa_turned = sem("xa_turned")
        xa_kept = sem("xa_kept")
        x_summed = sem("x_summed")
        logits_done = sem("logits_done")
        logits_copied = sem("logits_copied")
        h1_done = sem("h1_done")
        h1_ready = sem("h1_ready")
        task_done = sem("task_done")
        task_max = sem("task_max")
        task_exp = sem("task_exp")
        row_max = sem("row_max")
        choice_sub = sem("choice_sub")
        choice_exp = sem("choice_exp")
        zeros_set = sem("zeros_set")
        slots_cleared = sem("slots_cleared")
        tri_ready = sem("tri_ready")
        hits_ready = sem("hits_ready")
        mask_ready = sem("mask_ready")
        ranked = sem("ranked")
        blocks_ready = sem("blocks_ready")
        starts_done = sem("starts_done")
        score_parts = sem("score_parts")
        scores_summed = sem("scores_summed")
        places_ready = sem("places_ready")
        place_parts = sem("place_parts")
        owner_ready = sem("owner_ready")
        owner_stored = sem("owner_stored")
        owners_loaded = sem("owners_loaded")
        hi_split = sem("hi_split")
        lo_split = sem("lo_split")

        CONSTS = 11

        def batches(eng, step, late):
            for b in range(4):
                step(b, b % 2)
            if eng is nc.tensor:
                for b in range(4, B):
                    step(b, b % 2)
            else:
                with eng.Fori(2, B // 2) as j:
                    for i in range(2):
                        step(2 * j + i, i)
            for i in range(late):
                step(B + i, i % 2)

        def has(b, lag):
            return not isinstance(b, int) or 0 <= b - lag < B

        def of_batch(b, n):
            return slice(b * n, (b + 1) * n) if isinstance(b, int) else bass.ds(b * n, n)

        with nc.Block() as block:
            @block.sync
            def _(sp):
                for b in range(B):
                    sp.dma_start(x_sb[:, b * TT:(b + 1) * TT, :], x_rows[:, b * TT:(b + 1) * TT, :]).then_inc(x_loaded[2 * b // B], 16)
                sp.dma_start(wq_raw, wq.rearrange("(c p) n -> p c n", p=P)).then_inc(wq_loaded, 16)
                sp.dma_start(wkv_raw[:, :, :], wkv.rearrange("(c p) n -> p c n", p=P)).then_inc(wkv_loaded, 16)
                sp.dma_start(wo_raw[:, :, :], wout.rearrange("(h p) n -> p h n", p=P)).then_inc(wo_loaded, 16)
                sp.wait_ge(zeros_set, 1)
                sp.wait_ge(const_loaded, 16 * CONSTS)
                for a in range(SLOTS // (8 * P)):
                    sp.dma_start(slot_x.rearrange("(a p r) d -> a p r d", p=P, r=8)[a], bcast(zeros[:, :].unsqueeze(1), [P, 8, D])).then_inc(slots_cleared, 16)
                sp.wait_ge(owner_ready, 1)
                sp.dma_start(block_expert, owner_i[:, :]).then_inc(owner_stored, 16)
                sp.wait_ge(owner_stored, 16)
                sp.dma_start(owners[:, :], block_expert.rearrange("n o -> o n")).then_inc(owners_loaded, 16)
                sp.wait_ge(slots_cleared, 16 * (SLOTS // (8 * P)))
                sp.wait_ge(owners_loaded, 16)

            @block.scalar
            def _(act):
                def row_b(a, n):
                    return a.unsqueeze(0).to_broadcast([P, n])
                act.dma_start(ident[:, :], ident_in).then_inc(turn_loaded, 16)
                act.dma_start(g_col[:, :], g_norm).then_inc(const_loaded, 16)
                act.dma_start(wr_sb[:, :, :], wr_t.rearrange("(c p) e -> p c e", p=P)).then_inc(turn_loaded, 16)
                act.dma_start(w1_sb[:, :, :], w1_t.rearrange("(c p) e -> p c e", p=P)).then_inc(const_loaded, 16)
                act.dma_start(b1_sb[:, :], b1).then_inc(const_loaded, 16)
                act.dma_start(w2_sb[:, :], w2_t).then_inc(const_loaded, 16)
                act.dma_start(b2_b[:, :], row_b(b2, ND)).then_inc(const_loaded, 16)
                act.dma_start(rbias_b[:, :], row_b(r_bias, E)).then_inc(const_loaded, 16)
                act.dma_start(iota_b[:, :], row_b(iota_in[0:E], E)).then_inc(const_loaded, 16)
                act.dma_start(g_out_b[:, :], row_b(g_out, D)).then_inc(const_loaded, 16)
                act.dma_start(aff_b[:, :, :].rearrange("p a e -> p (a e)"), row_b(aff_t.rearrange("a e -> (a e)"), ND * E)).then_inc(const_loaded, 16)
                act.dma_start(tri_sb[:, :], tri_in).then_inc(const_loaded, 16)
                act.dma_start(block_no[:, :], iota_in.unsqueeze(1)).then_inc(const_loaded, 16)

                def step(b, i):
                    if has(b, 0):
                        act.wait_ge(xn_turned, b + 1)
                        if has(b, 2):
                            act.wait_ge(logits_done, b - 1)
                        nc.scalar.activation(xn_stat[:, i, :, :], ps_xn[i][:, :, :], ACT.Copy).then_inc(xn_copied, 1)
                        nc.scalar.activation(xn_t[:, :, of_batch(b, N)], ps_xn[i][:, :, :], ACT.Copy).then_inc(xn_kept, 1)
                    if has(b, 1):
                        act.wait_ge(logits_done, b)
                        nc.scalar.activation(raw_logits[:, of_batch(b - 1, TT), :], ps_logits[1 - i][:, :, :], ACT.Copy).then_inc(logits_copied, 1)
                batches(act, step, 1)
                act.wait_ge(const_loaded, 16 * CONSTS)
                nc.scalar.activation(iota_bf[:, :], iota_b[:, :], ACT.Copy)
                nc.scalar.activation(w2_rep[:, :, :], bcast(w2_sb[:, :].unsqueeze(2), [P, ND, P]), ACT.Copy)
                nc.scalar.activation(tri_b[:, :], tri_sb[:, :], ACT.Copy).then_inc(tri_ready, 1)
                act.wait_ge(h1_done, 1)
                nc.scalar.activation(h1[:, :], ps_h1, ACT.Gelu, bias=b1_sb[:, 0:1], scale=1.0 / N).then_inc(h1_ready, 1)
                act.wait_ge(wq_loaded, 16)
                nc.scalar.activation(wq_hi[:, :, :], wq_raw, ACT.Copy).then_inc(hi_split, 1)
                act.wait_ge(wkv_loaded, 16)
                nc.scalar.activation(wkv_hi[:, :, :], wkv_raw[:, :, :], ACT.Copy).then_inc(hi_split, 1)
                act.wait_ge(task_max, 1)
                nc.scalar.activation(task[:, :, :], task[:, :, :], ACT.Exp).then_inc(task_exp, 1)

                def turn_step(b, i):
                    act.wait_ge(xa_turned, b + 1)
                    for c in range(KC):
                        last = nc.scalar.activation(xa_t[:, c, of_batch(b, N)], ps_xn[i][:, c, :], ACT.Copy, scale=g_col[:, c:c + 1])
                    last.then_inc(xa_kept, 1)
                batches(act, turn_step, 0)
                act.wait_ge(wo_loaded, 16)
                nc.scalar.activation(wo_hi[:, :, :], wo_raw[:, :, :], ACT.Copy).then_inc(hi_split, 1)
                act.wait_ge(choice_sub, 1)
                nc.scalar.activation(raw_logits[:, :, :], raw_logits[:, :, :], ACT.Exp).then_inc(choice_exp, 1)

            @block.gpsimd
            def _(pool):
                nc.gpsimd.memset(half_row[:, :], -0.5).then_inc(half_set, 1)
                nc.gpsimd.memset(minus_half[:, :], -0.5).then_inc(half_set, 1)
                nc.gpsimd.memset(zeros[:, :], 0.0).then_inc(zeros_set, 1)
                pool.wait_ge(half_set, 2)
                for k in range(2):
                    of = slice(k * TILES // 2, (k + 1) * TILES // 2)
                    pool.wait_ge(var_ready, k + 1)
                    nc.gpsimd.tensor_tensor(rstd[:, of], var_eps[:, of], half_row[:, of], ALU.pow).then_inc(rstd_ready, 1)
                pool.wait_ge(var_ready, 3)
                nc.gpsimd.tensor_tensor(rstd[:, :], var_eps[:, :], half_row[:, :], ALU.pow).then_inc(rstd_ready, 1)
                pool.wait_ge(hi_split, 2)
                nc.gpsimd.tensor_tensor(wq_lo[:, :, :], wq_raw, wq_hi[:, :, :].bitcast(F32), ALU.subtract).then_inc(lo_split, 1)
                pool.wait_ge(row_max, 1)
                nc.gpsimd.tensor_tensor(raw_logits[:, :, :], raw_logits[:, :, :], bcast(row[:, 0, :].unsqueeze(2), [P, TILES, E]), ALU.subtract).then_inc(choice_sub, 1)
                nc.gpsimd.tensor_tensor(wkv_lo[:, :, :], wkv_raw[:, :, :], wkv_hi[:, :, :].bitcast(F32), ALU.subtract).then_inc(lo_split, 1)
                pool.wait_ge(hi_split, 3)
                nc.gpsimd.tensor_tensor(wo_lo[:, 0:HP, :], wo_raw[:, 0:HP, :], wo_hi[:, 0:HP, :].bitcast(F32), ALU.subtract).then_inc(lo_split, 1)
                pool.wait_ge(hits_ready, 1)
                pool.wait_ge(xa_turned, B)
                pool.wait_ge(choice_exp, 1)
                for k in range(TOPK):
                    nc.gpsimd.tensor_tensor(part[k], hit[k], raw_logits[:, :, :], ALU.mult).then_inc(score_parts, 1)
                pool.wait_ge(places_ready, 1)
                pool.wait_ge(scores_summed, TOPK)
                for k in range(2, TOPK):
                    nc.gpsimd.tensor_tensor(part[k], hit[k], choice[:, :, :], ALU.mult).then_inc(place_parts, 1)
                nc.gpsimd.tensor_tensor(wo_lo[:, HP:HEADS, :], wo_raw[:, HP:HEADS, :], wo_hi[:, HP:HEADS, :].bitcast(F32), ALU.subtract).then_inc(lo_split, 1)

            @block.tensor
            def _(pe):
                def step(b, i):
                    if has(b, 0):
                        pe.wait_ge(xn_ready, b + 1)
                        if has(b, 2):
                            pe.wait_ge(xn_kept, b - 1)
                        for c in range(KC):
                            for t in range(TT):
                                at = b * TT + t
                                src = x_sb[:, at, c * P:(c + 1) * P]
                                last = nc.tensor.transpose(ps_xn[i][:, c, t * P:(t + 1) * P], src, ident[:, :])
                        last.then_inc(xn_turned, 1)
                    if has(b, 1):
                        pe.wait_ge(xn_copied, b)
                        if has(b, 3):
                            pe.wait_ge(logits_copied, b - 2)
                        for t in range(TT):
                            for c in range(KC):
                                last = nc.tensor.matmul(ps_logits[1 - i][:, t, :], xn_stat[:, 1 - i, c, t * P:(t + 1) * P], wr_sb[:, c, :],
                                                        start=(c == 0), stop=(c == KC - 1))
                        last.then_inc(logits_done, 1)
                pe.wait_ge(turn_loaded, 32)
                batches(nc.tensor, step, 1)
                pe.wait_ge(const_loaded, 16 * CONSTS)
                pe.wait_ge(x_summed, B // 2)
                for c in range(KC):
                    last = nc.tensor.matmul(ps_h1, w1_sb[:, c, :], x_sum[:, c, :], start=(c == 0), stop=(c == KC - 1))
                last.then_inc(h1_done, 1)
                pe.wait_ge(h1_ready, 1)
                pe.wait_ge(tri_ready, 2)
                for a in range(ND):
                    last = nc.tensor.matmul(ps_task[:, :, a], w2_rep[:, a, :], h1[:, :], start=True, stop=True)
                last.then_inc(task_done, 1)

                def turn_step(b, i):
                    pe.wait_ge(xa_ready, b + 1)
                    if has(b, 2):
                        pe.wait_ge(xa_kept, b - 1)
                    else:
                        pe.wait_ge(xn_kept, B)
                    for c in range(KC):
                        for t in range(TT):
                            at = b * TT + t
                            src = xa_rows[:, at, c * P:(c + 1) * P]
                            last = nc.tensor.transpose(ps_xn[i][:, c, t * P:(t + 1) * P], src, ident[:, :])
                    last.then_inc(xa_turned, 1)
                batches(nc.tensor, turn_step, 0)
                pe.wait_ge(tri_ready, 2)
                pe.wait_ge(mask_ready, 2)
                for h in range(2):
                    tiles = slice(h * TILES // 2, (h + 1) * TILES // 2)
                    nc.tensor.matmul(ps_rank[:, tiles, :], tri_b[:, :], mask_b[:, tiles, :], start=True, stop=False)
                    nc.tensor.matmul(ps_rank[:, tiles, :], ones_b[:, :], before_b[:, tiles, :], start=False, stop=True)
                nc.tensor.matmul(ps_count, before_b[:, TILES, :], ones_b[:, :], start=True, stop=True).then_inc(ranked, 1)
                pe.wait_ge(blocks_ready, 1)
                nc.tensor.matmul(ps_starts, blocks_b[:, :], tri_b[0:E, 0:E], start=True, stop=True).then_inc(starts_done, 1)

            @block.vector
            def _(dve):
                chain = [0]

                def then(ins):
                    chain[0] += 1
                    ins.then_inc(ln_step, 1)
                    dve.wait_ge(ln_step, chain[0])

                nc.vector.memset(ones_b[:, :], 1.0).then_inc(tri_ready, 1)
                nc.vector.memset(before_b[:, 0, :], 0.0)
                HALF = TILES // 2

                def moments(tiles):
                    for t in tiles:
                        last = nc.vector.bn_stats(stats[:, t, :], x_sb[:, t, :])
                    then(last)
                    for t in tiles:
                        last = nc.vector.bn_aggr(meanvar[:, t, :], stats[:, t, :])
                    then(last)
                    of = slice(tiles[0], tiles[-1] + 1)
                    nc.vector.tensor_scalar(var_eps[:, of], meanvar[:, of, 1], EPS, None, ALU.add).then_inc(var_ready, 1)

                def normed(dst, tiles, ready):
                    for t in tiles:
                        last = nc.vector.tensor_scalar(dst[:, t, :], x_sb[:, t, :], meanvar[:, t, 0:1], rstd[:, t:t + 1], ALU.subtract, ALU.mult)
                        if t % TT == TT - 1:
                            last.then_inc(ready, 1)

                halves = [range(0, HALF), range(HALF, TILES)]
                for k in range(2):
                    dve.wait_ge(x_loaded[k], 16 * B // 2)
                    moments(halves[k])
                for k in range(2):
                    dve.wait_ge(rstd_ready, k + 1)
                    normed(x_sb, halves[k], xn_ready)
                dve.wait_ge(xn_ready, B)
                moments(range(TILES))

                def batch_sums(q):
                    dve.wait_ge(xn_kept, 2 * q + 2)
                    nc.vector.tensor_reduce(x_sum[:, :, 2 * q:2 * q + 2], xn_t[:, :, 2 * q * N:(2 * q + 2) * N].rearrange("p c (b n) -> p c b n", b=2),
                                            AX_X, ALU.add).then_inc(x_summed, 1)

                for q in range(B // 2):
                    batch_sums(q)
                dve.wait_ge(rstd_ready, 3)
                normed(xa_rows, range(TILES), xa_ready)
                dve.wait_ge(const_loaded, 16 * CONSTS)
                dve.wait_ge(task_done, 1)
                then(nc.vector.tensor_tensor(task[:, :, :], ps_task, bcast(b2_b[:, :].unsqueeze(1), [P, B, ND]), ALU.add))
                then(nc.vector.tensor_reduce(task_s[:, :], task[:, :, :], AX_X, ALU.max))
                nc.vector.tensor_tensor(task[:, :, :], task[:, :, :], bcast(task_s[:, :].unsqueeze(2), [P, B, ND]), ALU.subtract).then_inc(task_max, 1)
                dve.wait_ge(task_exp, 1)
                then(nc.vector.tensor_reduce(task_s[:, :], task[:, :, :], AX_X, ALU.add))
                then(nc.vector.reciprocal(task_s[:, :], task_s[:, :]))
                then(nc.vector.scalar_tensor_tensor(task[:, :, :], task[:, :, :], 0.5, bcast(task_s[:, :].unsqueeze(2), [P, B, ND]), ALU.mult, ALU.mult))
                dve.wait_ge(logits_copied, B)
                for a in range(ND):
                    dst = dom if a == 0 else dom_part
                    then(nc.vector.tensor_tensor(dst, bcast(task[:, :, a].unsqueeze(2), [P, B, E]),
                                                 bcast(aff_b[:, a, :].unsqueeze(1), [P, B, E]), ALU.mult))
                    if a:
                        then(nc.vector.tensor_tensor(dom, dom, dom_part, ALU.add))
                logits4 = raw_logits[:, :, :].rearrange("p (b t) e -> p b t e", t=TT)
                for t in range(TT):
                    last = nc.vector.tensor_tensor(logits4[:, :, t, :], logits4[:, :, t, :], dom, ALU.add)
                then(last)
                then(nc.vector.tensor_tensor(choice[:, :, :], raw_logits[:, :, :], bcast(rbias_b[:, :].unsqueeze(1), [P, TILES, E]), ALU.add))
                nc.vector.tensor_reduce(row[:, 0, :], raw_logits[:, :, :], AX_X, ALU.max).then_inc(row_max, 1)
                for t in range(TILES):
                    last = nc.vector.max(top[:, t, :], choice[:, t, :])
                then(last)
                for t in range(TILES):
                    last = nc.vector.max_index(top_at[:, t, :], top[:, t, :], choice[:, t, :])
                then(last)
                then(nc.vector.tensor_copy(top_b[:, :, :], top_at[:, :, :]))
                dve.wait_ge(tri_ready, 2)
                dve.wait_ge(lo_split, 1)
                for k in range(TOPK):
                    last = nc.vector.tensor_tensor(hit[k], bcast(iota_bf[:, :].unsqueeze(1), [P, TILES, E]),
                                                   bcast(top_b[:, :, k].unsqueeze(2), [P, TILES, E]), ALU.is_equal)
                last.then_inc(hits_ready, 1)
                dve.wait_ge(hits_ready, 1)
                for k in range(2):
                    last = nc.vector.tensor_tensor(mask_part[k], hit[2 * k], hit[2 * k + 1], ALU.add)
                then(last)
                nc.vector.tensor_tensor(mask_b, mask_part[0], mask_part[1], ALU.add).then_inc(mask_ready, 1)
                dve.wait_ge(mask_ready, 1)
                RUN = 4
                inner = before_b[:, 1:TILES + 1, :].rearrange("p (g r) e -> p g r e", r=RUN)
                mask4 = mask_b.rearrange("p (g r) e -> p g r e", r=RUN)
                then(nc.vector.tensor_copy(inner[:, :, 0, :], mask4[:, :, 0, :]))
                for r in range(1, RUN):
                    then(nc.vector.tensor_tensor(inner[:, :, r, :], inner[:, :, r - 1, :], mask4[:, :, r, :], ALU.add))
                for g in range(1, TILES // RUN):
                    last = nc.vector.tensor_tensor(inner[:, g, :, :], inner[:, g, :, :],
                                                   bcast(inner[:, g - 1, RUN - 1, :].unsqueeze(1), [P, RUN, E]), ALU.add)
                    if g < TILES // RUN - 1:
                        then(last)
                last.then_inc(mask_ready, 1)
                dve.wait_ge(choice_exp, 1)
                nc.vector.tensor_reduce(row[:, 1, :], raw_logits[:, :, :], AX_X, ALU.add)

                def pick_scores(ks):
                    for k in ks:
                        dve.wait_ge(score_parts, k + 1)
                        nc.vector.tensor_reduce(picked[:, :, k], part[k], AX_X, ALU.add).then_inc(scores_summed, 1)
                pick_scores(range(2))
                dve.wait_ge(ranked, 1)
                then(nc.vector.tensor_scalar(count_i[:, :], ps_count, float(P - 1), None, ALU.add))
                then(nc.vector.tensor_scalar(blocks_i[:, :], count_i[:, :], 7, None, ALU.arith_shift_right))
                nc.vector.tensor_copy(blocks_b[:, :], blocks_i[:, :]).then_inc(blocks_ready, 1)
                dve.wait_ge(starts_done, 1)
                then(nc.vector.tensor_copy(starts[:, :], ps_starts))
                nc.vector.scalar_tensor_tensor(choice[:, :, :], bcast(starts[:, :].unsqueeze(1), [P, TILES, E]), float(P),
                                               ps_rank[:, :, :], ALU.mult, ALU.add).then_inc(places_ready, 1)
                then(nc.vector.tensor_scalar(begun[:, :], starts[:, :], block_no[:, 0:1], None, ALU.is_le))
                then(nc.vector.tensor_reduce(owner[:, :], begun[:, 1:E], AX_X, ALU.add))
                nc.vector.tensor_copy(owner_i[:, :], owner[:, :]).then_inc(owner_ready, 1)
                pick_scores(range(2, TOPK))
                dve.wait_ge(scores_summed, TOPK)
                dve.wait_ge(places_ready, 1)
                for k in range(2):
                    last = nc.vector.tensor_tensor(part[k], hit[k], choice[:, :, :], ALU.mult)
                then(last)
                for k in range(2):
                    last = nc.vector.tensor_reduce(slot_f[:, :, k], part[k], AX_X, ALU.add)
                then(nc.vector.tensor_reduce(row[:, 0, :], picked[:, :, :], AX_X, ALU.add))
                then(nc.vector.scalar_tensor_tensor(row[:, 2, :], row[:, 1, :], 1e-8, row[:, 0, :], ALU.mult, ALU.add))
                then(nc.vector.reciprocal(row[:, 1, :], row[:, 2, :]))
                nc.vector.tensor_tensor(gates[:, :, :], picked[:, :, :], bcast(row[:, 1, :].unsqueeze(2), [P, TILES, TOPK]), ALU.mult)
                for k in range(2, TOPK):
                    dve.wait_ge(place_parts, k - 1)
                    last = nc.vector.tensor_reduce(slot_f[:, :, k], part[k], AX_X, ALU.add)
                then(last)
                nc.vector.tensor_copy(slots[:, :, :], slot_f[:, :, :])
        prep_ps.close()
        prep.close()

        work = ExitStack()
        xs_hi = sbuf(work, "xs_hi", [P, KC, N], F32R)
        xs_lo = sbuf(work, "xs_lo", [P, KC, N], F32R)
        kv_rows = sbuf(work, "kv_rows", [P, TT, 2 * DH])
        k_sq = sbuf(work, "k_sq", [P, TT, DH])
        k_norm = sbuf(work, "k_norm", [P, TT, DH])
        kt_hi = sbuf(work, "kt_hi", [P, N], F32R)
        kt_lo = sbuf(work, "kt_lo", [P, N], F32R)
        v_hi = sbuf(work, "v_hi", [P, TT, DH], F32R)
        v_lo = sbuf(work, "v_lo", [P, TT, DH], F32R)
        QT = 2 * TT
        pick_f = sbuf(work, "pick_f", [P, QT, QT])
        pick_row = sbuf(work, "pick_row", [P, QT, QT], F32R)
        q_sq = sbuf(work, "q_sq", [P, 4, DH])
        q_sum = sbuf(work, "q_sum", [P, 4])
        q_var = sbuf(work, "q_var", [P, 4])
        q_scale = sbuf(work, "q_scale", [P, 4])
        k_sum = sbuf(work, "k_sum", [P, 2])
        k_var = sbuf(work, "k_var", [P, 2])
        k_scale = sbuf(work, "k_scale", [P, 2])
        q_norm = sbuf(work, "q_norm", [P, TT, 2, DH])
        qt_hi = sbuf(work, "qt_hi", [P, 2, PAIR], F32R)
        qt_lo = sbuf(work, "qt_lo", [P, 2, PAIR], F32R)
        w_f = sbuf(work, "w_f", [P, TT, PAIR])
        w_hi = sbuf(work, "w_hi", [P, 2, TT, PAIR], F32R)
        w_lo = sbuf(work, "w_lo", [P, 2, TT, PAIR], F32R)
        pair_f = sbuf(work, "pair_f", [P, PAIR])
        pair_hi = sbuf(work, "pair_hi", [P, PAIR], F32R)
        pair_lo = sbuf(work, "pair_lo", [P, PAIR], F32R)
        w_sums = sbuf(work, "w_sums", [P, P])
        w_rec = sbuf(work, "w_rec", [P, 2, QT])
        ot_hi = sbuf(work, "ot_hi", [P, 2, PAIR], F32R)
        ot_lo = sbuf(work, "ot_lo", [P, 2, PAIR], F32R)

        row_stage = sbuf(work, "row_stage", [P, 2, D])
        slot_stage = sbuf(work, "slot_stage", [P, 2, TOPK], U32)

        work_ps = ExitStack()
        ps_q = psum(work_ps, "ps_q", [P, TT, 2, DH])
        ps_t = psum(work_ps, "ps_t", [P, PAIR])
        ps_s = psum(work_ps, "ps_s", [P, TT, PAIR])
        ps_av = psum(work_ps, "ps_av", [P, PAIR])
        ps_sum = psum(work_ps, "ps_sum", [P, 512])
        ps_acc = psum(work_ps, "ps_acc", [P, 2, TT, D])
        sum_rows = ps_sum[0:QT, 0:P]
        sum_turned = ps_sum[:, P:2 * P]
        sum_cols = ps_sum[:, P:P + QT]

        pick_set = sem("pick_set")
        xs_ready = sem("xs_ready")
        xs_hi_ready = sem("xs_hi_ready")
        kv_done = sem("kv_done")
        kv_copied = sem("kv_copied")
        ksq_ready = sem("ksq_ready")
        k_link = sem("k_link")
        ksum_ready = sem("ksum_ready")
        kscale_ready = sem("kscale_ready")
        knorm_ready = sem("knorm_ready")
        k_turned = sem("k_turned")
        kt_hi_ready = sem("kt_hi_ready")
        kt_lo_ready = sem("kt_lo_ready")
        v_hi_ready = sem("v_hi_ready")
        v_ready = sem("v_ready")
        q_done = sem("q_done")
        qsq_ready = sem("qsq_ready")
        q_link = sem("q_link")
        qsum_ready = sem("qsum_ready")
        qscale_ready = sem("qscale_ready")
        qnorm_ready = sem("qnorm_ready")
        q_turned = sem("q_turned")
        qt_hi_ready = sem("qt_hi_ready")
        qt_lo_ready = sem("qt_lo_ready")
        s_done = sem("s_done")
        w_ready = sem("w_ready")
        w_hi_ready = sem("w_hi_ready")
        w_lo_ready = sem("w_lo_ready")
        pair_ready = sem("pair_ready")
        pair_hi_ready = sem("pair_hi_ready")
        pair_lo_ready = sem("pair_lo_ready")
        av_done = sem("av_done")
        sums_done = sem("sums_done")
        sums_copied = sem("sums_copied")
        sums_cleared = sem("sums_cleared")
        sums_turned = sem("sums_turned")
        rec_ready = sem("rec_ready")
        ot_hi_ready = sem("ot_hi_ready")
        ot_lo_ready = sem("ot_lo_ready")
        proj_done = sem("proj_done")
        head_added = sem("head_added")
        unit_added = sem("unit_added")
        norm_link = sem("norm_link")
        ovar_ready = sem("ovar_ready")
        orstd_ready = sem("orstd_ready")
        out_normed = sem("out_normed")
        sh_loaded = sem("sh_loaded")
        rows_staged = sem("rows_staged")
        rows_sent = [sem(f"rows_sent{i}") for i in range(2)]
        SEND = HP // 2
        assert SEND == TOPK and B * 2 == TILES

        UNITS_A = B * HP
        LATE = 4

        def steps(eng, step):
            for hp in range(HP):
                step(0, hp)
            with eng.Fori(1, B) as b:
                for hp in range(HP):
                    step(b, hp)
            for hp in range(LATE):
                step(B, hp)

        def live(b, hp, lag):
            if not isinstance(b, int):
                return True
            return 0 <= HP * b + hp - lag < UNITS_A

        def started(b):
            return not isinstance(b, int) or b < B

        def first(b):
            return isinstance(b, int) and b == 0

        def batch_rows(b, t, count):
            at = b * TT + t
            return attn_out[:, at:at + count, :] if isinstance(at, int) else attn_out[:, bass.ds(at, count), :]

        def out_moments(dve, b):
            dve.wait_ge(unit_added, TT * HP * b)
            dve.wait_ge(out_normed, b)
            nc.vector.memset(spare[:, 6:7], 0.0)
            for t in range(TT):
                last = nc.vector.bn_stats(o_stats[:, t, :], batch_rows(b - 1, t, 1).rearrange("p t d -> p (t d)"))
            last.then_inc(norm_link, 1)
            dve.wait_ge(norm_link, 3 * b - 1)
            nc.vector.memset(spare[:, 7:8], 0.0)
            for t in range(TT):
                last = nc.vector.bn_aggr(o_mv[:, t, :], o_stats[:, t, :])
            last.then_inc(norm_link, 1)
            dve.wait_ge(norm_link, 3 * b)
            nc.vector.tensor_scalar(o_var[:, :], o_mv[:, :, 1], EPS, None, ALU.add).then_inc(ovar_ready, 1)

        def out_rstd(pool, b):
            pool.wait_ge(ovar_ready, b)
            nc.gpsimd.tensor_tensor(o_rstd[:, :], o_var[:, :], minus_half[:, 0:TT], ALU.pow).then_inc(orstd_ready, 1)

        def norm_out(dve, b):
            dve.wait_ge(orstd_ready, b)
            for t in range(TT):
                rows = batch_rows(b - 1, t, 1).rearrange("p t d -> p (t d)")
                last = nc.vector.tensor_scalar(rows, rows, o_mv[:, t, 0:1], o_rstd[:, t:t + 1], ALU.subtract, ALU.mult)
            last.then_inc(norm_link, 1)

        def scale_out(dve, b):
            dve.wait_ge(norm_link, 3 * b + 1)
            rows = batch_rows(b - 1, 0, TT)
            nc.vector.tensor_tensor(rows, rows, bcast(g_out_b[:, :].unsqueeze(1), [P, TT, D]), ALU.mult).then_inc(out_normed, 1)

        with nc.Block() as block:
            @block.sync
            def _(sp):
                sp.dma_start(sh_raw[:, :], w_shared).then_inc(sh_loaded, 16)

            @block.tensor
            def _(pe):
                def mm3(dst, l_hi, l_lo, r_hi, r_lo, start, stop):
                    nc.tensor.matmul(dst, l_hi, r_hi, start=start, stop=False)
                    nc.tensor.matmul(dst, l_hi, r_lo, start=False, stop=False)
                    return nc.tensor.matmul(dst, l_lo, r_hi, start=False, stop=stop)

                def step(b, hp):
                    u = HP * b + hp
                    if live(b, hp, 2):
                        pe.wait_ge(qt_lo_ready, u - 1)
                        pe.wait_ge(qt_hi_ready, u - 1)
                        if hp == 2:
                            pe.wait_ge(kt_hi_ready, b + 1)
                            pe.wait_ge(kt_lo_ready, b + 1)
                        if live(b, hp, 3):
                            pe.wait_ge(w_ready, u - 2)
                        i = hp % 2
                        for t in range(TT):
                            cols = slice(t * P, (t + 1) * P)
                            last = mm3(ps_s[:, t, :], kt_hi[:, cols], kt_lo[:, cols], qt_hi[:, i, :], qt_lo[:, i, :], True, True)
                        last.then_inc(s_done, 1)
                    if hp == 1 and started(b):
                        pe.wait_ge(knorm_ready, b + 1)
                        if not first(b):
                            pe.wait_ge(qt_lo_ready, u - 1)
                            pe.wait_ge(qt_hi_ready, u - 1)
                        for t in range(TT):
                            last = nc.tensor.transpose(ps_t[:, t * P:(t + 1) * P], k_norm[:, t, :], ident[:, :])
                        last.then_inc(k_turned, 1)
                    if live(b, hp, 3):
                        pe.wait_ge(w_lo_ready, u - 2)
                        pe.wait_ge(w_hi_ready, u - 2)
                        if hp == 3:
                            pe.wait_ge(v_hi_ready, b + 1)
                            pe.wait_ge(v_ready, b + 1)
                        if live(b, hp, 4):
                            pe.wait_ge(ot_hi_ready, u - 3)
                            pe.wait_ge(ot_lo_ready, u - 3)
                        i = (hp + 1) % 2
                        for j in range(TT):
                            last = mm3(ps_av[:, :], v_hi[:, j, :], v_lo[:, j, :], w_hi[:, i, j, :], w_lo[:, i, j, :], j == 0, j == TT - 1)
                        last.then_inc(av_done, 1)
                        if live(b, hp, 4):
                            pe.wait_ge(rec_ready, u - 3)
                        elif hp == 3:
                            pe.wait_ge(pick_set, 2)
                        pe.wait_ge(pair_hi_ready, u - 2)
                        pe.wait_ge(pair_lo_ready, u - 2)
                        for c in range(QT):
                            for w in (pair_hi, pair_lo):
                                last = nc.tensor.matmul(sum_rows, pick_row[:, c, :], w[:, c * P:(c + 1) * P],
                                                        start=(c == 0 and w is pair_hi), stop=(c == QT - 1 and w is pair_lo))
                        last.then_inc(sums_done, 1)
                    if live(b, hp, 1):
                        pe.wait_ge(qnorm_ready, u)
                        if hp == 1 and started(b):
                            pe.wait_ge(kt_hi_ready, b + 1)
                            pe.wait_ge(kt_lo_ready, b + 1)
                        elif live(b, hp, 2):
                            pe.wait_ge(qt_hi_ready, u - 1)
                            pe.wait_ge(qt_lo_ready, u - 1)
                        for h in range(2):
                            for t in range(TT):
                                last = nc.tensor.transpose(ps_t[:, h * N + t * P:h * N + (t + 1) * P], q_norm[:, t, h, :], ident[:, :])
                        last.then_inc(q_turned, 1)
                    if hp == 0 and started(b):
                        pe.wait_ge(xs_hi_ready, b + 1)
                        pe.wait_ge(xs_ready, b + 1)
                        if not first(b):
                            pe.wait_ge(unit_added, TT * (u - 4))
                        for t in range(TT):
                            for c in range(KC):
                                cols = slice(t * P, (t + 1) * P)
                                last = mm3(ps_acc[:, 0, t, :], xs_hi[:, c, cols], xs_lo[:, c, cols],
                                           wkv_hi[:, c, :], wkv_lo[:, c, :], c == 0, c == KC - 1)
                        last.then_inc(kv_done, 1)
                    if started(b):
                        if live(b, hp, 1):
                            pe.wait_ge(qnorm_ready, u)
                        for t in range(TT):
                            for c in range(KC):
                                cols = slice(t * P, (t + 1) * P)
                                heads = slice(hp * 2 * DH, (hp + 1) * 2 * DH)
                                last = mm3(ps_q[:, t, :, :], xs_hi[:, c, cols], xs_lo[:, c, cols],
                                           wq_hi[:, c, heads], wq_lo[:, c, heads], c == 0, c == KC - 1)
                        last.then_inc(q_done, 1)
                    if live(b, hp, 3):
                        pe.wait_ge(sums_copied, u - 2)
                        nc.tensor.transpose(sum_turned, w_sums[:, :], ident[:, :]).then_inc(sums_turned, 1)
                    if live(b, hp, 4):
                        pe.wait_ge(ot_hi_ready, u - 3)
                        pe.wait_ge(ot_lo_ready, u - 3)
                        if live(b, hp, 5):
                            pe.wait_ge(unit_added, TT * (u - 4))
                        if hp == 0 and started(b):
                            pe.wait_ge(kv_copied, b + 1)
                        unit = (hp - 4) % HP
                        i = unit % 2
                        for h in range(2):
                            for t in range(TT):
                                cols = slice(h * N + t * P, h * N + (t + 1) * P)
                                last = mm3(ps_acc[:, h, t, :], ot_hi[:, i, cols], ot_lo[:, i, cols], wo_hi[:, 2 * unit + h, :], wo_lo[:, 2 * unit + h, :], True, True)
                        last.then_inc(proj_done, 1)

                steps(pe, step)

            @block.scalar
            def _(act):
                def step(b, hp):
                    u = HP * b + hp
                    if hp == 0 and started(b):
                        if not first(b):
                            act.wait_ge(q_done, u)
                        cols = slice(b * N, (b + 1) * N) if isinstance(b, int) else bass.ds(b * N, N)
                        nc.scalar.activation(xs_hi[:, :, :], xa_t[:, :, cols], ACT.Copy).then_inc(xs_hi_ready, 1)
                    if live(b, hp, 2):
                        act.wait_ge(s_done, u - 1)
                        if live(b, hp, 3):
                            act.wait_ge(w_lo_ready, u - 2)
                            act.wait_ge(w_hi_ready, u - 2)
                            act.wait_ge(pair_ready, u - 2)
                        nc.scalar.activation(w_f[:, :, :], ps_s[:, :, :], ACT.Exp).then_inc(w_ready, 1)
                    if hp == 1 and started(b):
                        act.wait_ge(k_turned, b + 1)
                        nc.scalar.activation(kt_hi[:, :], ps_t[:, 0:N], ACT.Copy).then_inc(kt_hi_ready, 1)
                    if live(b, hp, 2):
                        act.wait_ge(w_ready, u - 1)
                        if live(b, hp, 4):
                            act.wait_ge(av_done, u - 3)
                        nc.scalar.activation(w_hi[:, hp % 2, :, :], w_f[:, :, :], ACT.Copy).then_inc(w_hi_ready, 1)
                    if live(b, hp, 3):
                        act.wait_ge(av_done, u - 2)
                        if live(b, hp, 5):
                            act.wait_ge(proj_done, u - 4)
                        nc.scalar.activation(ot_hi[:, (hp + 1) % 2, :], ps_av[:, :], ACT.Copy).then_inc(ot_hi_ready, 1)
                    if hp == 2 and started(b):
                        if not first(b):
                            act.wait_ge(av_done, HP * b)
                        nc.scalar.activation(v_hi[:, :, :], kv_rows[:, :, DH:2 * DH], ACT.Copy).then_inc(v_hi_ready, 1)
                    if live(b, hp, 3):
                        act.wait_ge(sums_done, u - 2)
                        if not live(b, hp, 4):
                            act.wait_ge(sums_cleared, 1)
                        nc.scalar.activation(w_sums[0:QT, :], sum_rows, ACT.Copy).then_inc(sums_copied, 1)
                    if live(b, hp, 2):
                        act.wait_ge(pair_ready, u - 1)
                        nc.scalar.activation(pair_hi[:, :], pair_f[:, :], ACT.Copy).then_inc(pair_hi_ready, 1)
                    if live(b, hp, 1):
                        act.wait_ge(q_turned, u)
                        if live(b, hp, 3):
                            act.wait_ge(s_done, u - 2)
                        nc.scalar.activation(qt_hi[:, (hp + 1) % 2, :], ps_t[:, :], ACT.Copy).then_inc(qt_hi_ready, 1)
                    if hp == 0 and started(b):
                        act.wait_ge(kv_done, b + 1)
                        if not first(b):
                            act.wait_ge(v_ready, b)
                            act.wait_ge(knorm_ready, b)
                        nc.scalar.activation(kv_rows[:, :, :], ps_acc[:, 0, :, :], ACT.Copy).then_inc(kv_copied, 1)
                        act.wait_ge(kv_copied, b + 1)
                        nc.scalar.activation(k_sq[:, :, :], kv_rows[:, :, 0:DH], ACT.Square).then_inc(ksq_ready, 1)
                    if started(b):
                        act.wait_ge(q_done, u + 1)
                        if live(b, hp, 1):
                            act.wait_ge(qsum_ready, u)
                        nc.scalar.activation(q_sq[:, :, :], ps_q[:, :, :, :].rearrange("p t h d -> p (t h) d"), ACT.Square).then_inc(qsq_ready, 1)

                steps(act, step)

            @block.vector
            def _(dve):
                nc.vector.memset(spare[:, 5:6], 0.0).then_inc(out_normed, 1)
                nc.vector.memset(w_sums[:, :], 0.0).then_inc(sums_cleared, 1)
                nc.vector.memset(pick_f[:, :, :], 0.0).then_inc(pick_set, 1)
                dve.wait_ge(pick_set, 1)
                for c in range(QT):
                    last = nc.vector.memset(pick_f[:, c, c:c + 1], 1.0)
                last.then_inc(norm_link, 1)
                dve.wait_ge(norm_link, 1)
                nc.vector.tensor_copy(pick_row[:, :, :], pick_f[:, :, :]).then_inc(pick_set, 1)

                def step(b, hp):
                    u = HP * b + hp
                    if hp == 0 and started(b):
                        dve.wait_ge(xs_hi_ready, b + 1)
                        cols = slice(b * N, (b + 1) * N) if isinstance(b, int) else bass.ds(b * N, N)
                        nc.vector.tensor_tensor(xs_lo[:, :, :], xa_t[:, :, cols], xs_hi[:, :, :].bitcast(F32), ALU.subtract).then_inc(xs_ready, 1)
                    if hp % SEND == 0 and started(b):
                        i = hp // SEND
                        t = slice(2 * b + i, 2 * b + i + 1) if isinstance(b, int) else bass.ds(2 * b + i, 1)
                        if not first(b):
                            dve.wait_ge(rows_sent[i], 16 * SEND * b)
                        nc.vector.tensor_copy(row_stage[:, i:i + 1, :], x_sb[:, t, :])
                        nc.vector.tensor_copy(slot_stage[:, i:i + 1, :], slots[:, t, :]).then_inc(rows_staged, 1)
                    if hp == 1 and started(b):
                        dve.wait_ge(kt_hi_ready, b + 1)
                        nc.vector.tensor_tensor(kt_lo[:, :], ps_t[:, 0:N], kt_hi[:, :].bitcast(F32), ALU.subtract).then_inc(kt_lo_ready, 1)
                    if live(b, hp, 2):
                        dve.wait_ge(w_hi_ready, u - 1)
                        i = hp % 2
                        nc.vector.tensor_tensor(w_lo[:, i, :, :], w_f[:, :, :], w_hi[:, i, :, :].bitcast(F32), ALU.subtract).then_inc(w_lo_ready, 1)
                    if live(b, hp, 3):
                        i = (hp + 1) % 2
                        dve.wait_ge(ot_hi_ready, u - 2)
                        nc.vector.tensor_tensor(ot_lo[:, i, :], ps_av[:, :], ot_hi[:, i, :].bitcast(F32), ALU.subtract).then_inc(ot_lo_ready, 1)
                    if live(b, hp, 1):
                        i = (hp + 1) % 2
                        dve.wait_ge(qt_hi_ready, u)
                        nc.vector.tensor_tensor(qt_lo[:, i, :], ps_t[:, :], qt_hi[:, i, :].bitcast(F32), ALU.subtract).then_inc(qt_lo_ready, 1)
                    if hp == 0 and started(b):
                        dve.wait_ge(ksq_ready, b + 1)
                        nc.vector.tensor_reduce(k_sum[:, :], k_sq[:, :, :], AX_X, ALU.add).then_inc(k_link, 1)
                        dve.wait_ge(k_link, b + 1)
                        nc.vector.tensor_scalar(k_var[:, :], k_sum[:, :], 1.0 / SCALE, L2_EPS / SCALE, ALU.mult, ALU.add).then_inc(ksum_ready, 1)
                    if started(b):
                        dve.wait_ge(qsq_ready, u + 1)
                        nc.vector.tensor_reduce(q_sum[:, :], q_sq[:, :, :], AX_X, ALU.add).then_inc(q_link, 1)
                        dve.wait_ge(q_link, u + 1)
                        nc.vector.tensor_scalar(q_var[:, :], q_sum[:, :], 1.0 / SCALE, L2_EPS / (SCALE * SCALE * SCALE), ALU.mult, ALU.add).then_inc(qsum_ready, 1)
                    if live(b, hp, 3):
                        dve.wait_ge(sums_turned, u - 2)
                        if live(b, hp, 5):
                            dve.wait_ge(unit_added, TT * (u - 4))
                        nc.vector.reciprocal(w_rec[:, (hp + 1) % 2, :], sum_cols).then_inc(rec_ready, 1)
                    if hp == 0 and started(b):
                        dve.wait_ge(kscale_ready, b + 1)
                        if not first(b):
                            dve.wait_ge(k_turned, b)
                        nc.vector.tensor_tensor(k_norm[:, :, :], kv_rows[:, :, 0:DH], bcast(k_scale[:, :].unsqueeze(2), [P, TT, DH]),
                                                ALU.mult).then_inc(knorm_ready, 1)
                    if live(b, hp, 4):
                        unit = (hp - 4) % HP
                        of = b if hp >= 4 else b - 1
                        v = u - 4
                        dve.wait_ge(proj_done, v + 1)
                        dve.wait_ge(rec_ready, v + 1)
                        for h in range(2):
                            for t in range(TT):
                                rows = batch_rows(of, t, 1).rearrange("p t d -> p (t d)")
                                scale = w_rec[:, hp % 2, h * TT + t:h * TT + t + 1]
                                if h == 0 and unit == 0:
                                    nc.vector.tensor_scalar(rows, ps_acc[:, h, t, :], scale, None, ALU.mult).then_inc(head_added, 1)
                                elif h == 0:
                                    if t == 0:
                                        dve.wait_ge(unit_added, TT * v)
                                    nc.vector.scalar_tensor_tensor(rows, ps_acc[:, h, t, :], scale, rows, ALU.mult, ALU.add).then_inc(head_added, 1)
                                else:
                                    dve.wait_ge(head_added, TT * v + t + 1)
                                    nc.vector.scalar_tensor_tensor(rows, ps_acc[:, h, t, :], scale, rows, ALU.mult, ALU.add).then_inc(unit_added, 1)
                    if started(b):
                        dve.wait_ge(qscale_ready, u + 1)
                        if live(b, hp, 1):
                            dve.wait_ge(q_turned, u)
                        nc.vector.tensor_tensor(q_norm[:, :, :, :].rearrange("p t h d -> p (t h) d"),
                                                ps_q[:, :, :, :].rearrange("p t h d -> p (t h) d"),
                                                bcast(q_scale[:, :].unsqueeze(2), [P, 4, DH]), ALU.mult).then_inc(qnorm_ready, 1)
                    if hp == 4 and started(b) and not first(b):
                        out_moments(dve, b)
                    if hp == 5 and started(b) and not first(b):
                        norm_out(dve, b)
                    if hp == 6 and started(b) and not first(b):
                        scale_out(dve, b)

                steps(dve, step)

            @block.gpsimd
            def _(pool):
                def step(b, hp):
                    u = HP * b + hp
                    if live(b, hp, 2):
                        pool.wait_ge(w_ready, u - 1)
                        if live(b, hp, 3):
                            pool.wait_ge(pair_hi_ready, u - 2)
                            pool.wait_ge(pair_lo_ready, u - 2)
                        nc.gpsimd.tensor_tensor(pair_f[:, :], w_f[:, 0, :], w_f[:, 1, :], ALU.add).then_inc(pair_ready, 1)
                    if live(b, hp, 2):
                        pool.wait_ge(pair_hi_ready, u - 1)
                        nc.gpsimd.tensor_tensor(pair_lo[:, :], pair_f[:, :], pair_hi[:, :].bitcast(F32), ALU.subtract).then_inc(pair_lo_ready, 1)
                    if hp == 5 and started(b) and not first(b):
                        out_rstd(pool, b)
                    if hp == 0 and started(b):
                        pool.wait_ge(ksum_ready, b + 1)
                        nc.gpsimd.tensor_tensor(k_scale[:, :], k_var[:, :], minus_half[:, 0:2], ALU.pow).then_inc(kscale_ready, 1)
                    if hp == 2 and started(b):
                        pool.wait_ge(v_hi_ready, b + 1)
                        nc.gpsimd.tensor_tensor(v_lo[:, :, :], kv_rows[:, :, DH:2 * DH], v_hi[:, :, :].bitcast(F32), ALU.subtract).then_inc(v_ready, 1)
                    if started(b):
                        i, k = hp // SEND, hp % SEND
                        pool.wait_ge(rows_staged, 2 * b + i + 1)
                        pool.wait_ge(qsum_ready, u + 1)
                        nc.gpsimd.tensor_tensor(q_scale[:, :], q_var[:, :], minus_half[:, 0:4], ALU.pow).then_inc(qscale_ready, 1)
                        nc.gpsimd.indirect_dma_start(slot_x, bass.IndirectOffsetOnAxis(slot_stage[:, i, k:k + 1], 0), row_stage[:, i, :], None).then_inc(rows_sent[i], 16)

                steps(pool, step)
        work_ps.close()
        work.close()
        attention.close()

        tail = ExitStack()
        x_back = sbuf(tail, "x_back", [P, TILES, D])
        shared_y = x_sb
        experts = ExitStack()
        SH = SHC // P
        sh_hi = sbuf(experts, "sh_hi", [P, WS], F32R)
        sh_lo = sbuf(experts, "sh_lo", [P, WS], F32R)
        xh = sbuf(experts, "xh", [P, KC, P], F32R)
        xl = sbuf(experts, "xl", [P, KC, P], F32R)
        gate_s = sbuf(experts, "gate_s", [P, SHC])
        hid_s = sbuf(experts, "hid_s", [P, SHC])
        hs_hi = sbuf(experts, "hs_hi", [P, SH, P], F32R)
        hs_lo = sbuf(experts, "hs_lo", [P, SH, P], F32R)
        NBUF = 2
        WBUF = 4
        x_in = sbuf(experts, "x_in", [P, WBUF, 2, D])
        we_raw = sbuf(experts, "we_raw", [P, WBUF, 2, WE])
        we_hi = sbuf(experts, "we_hi", [P, WBUF, 2, WE], F32R)
        we_lo = sbuf(experts, "we_lo", [P, WBUF, 2, WE], F32R)
        xe = sbuf(experts, "xe", [P, NBUF, KC, 2, 2 * P], F32R)
        gu_low = sbuf(experts, "gu_low", [P, NBUF, 2, P])
        gu_sum = sbuf(experts, "gu_sum", [P, NBUF, 2, P])
        gate_e = sbuf(experts, "gate_e", [P, NBUF, 2 * P])
        hid_e = sbuf(experts, "hid_e", [F, NBUF, 2 * P])
        he = sbuf(experts, "he", [P, NBUF, 2 * P], F32R)
        y_out = sbuf(experts, "y_out", [P, WBUF, 2, D])
        DOWN = KC * 2 * F

        experts_ps = ExitStack()
        ps_x = [psum(experts_ps, f"ps_x{i}", [P, KC, 2 * P]) for i in range(NBUF)]
        ps_gu = [psum(experts_ps, f"ps_gu{i}", [P, 2, 2, P]) for i in range(NBUF)]
        ps_y = [psum(experts_ps, f"ps_y{i}", [P, 2, D]) for i in range(NBUF)]

        ps_sg = psum(experts_ps, "ps_sg", [P, SHC])
        ps_su = psum(experts_ps, "ps_su", [P, SHC])

        SH_PARTS = [slice(0, KC * SHC), slice(KC * SHC, 2 * KC * SHC), slice(2 * KC * SHC, WS)]
        sh_hi_ready = sem("sh_hi_ready")
        sh_lo_ready = sem("sh_lo_ready")
        xh_ready = sem("xh_ready")
        xl_ready = sem("xl_ready")
        sg_done = sem("sg_done")
        su_done = sem("su_done")
        sgate_ready = sem("sgate_ready")
        shid_ready = sem("shid_ready")
        shid_turned = sem("shid_turned")
        hs_hi_ready = sem("hs_hi_ready")
        hs_lo_ready = sem("hs_lo_ready")
        sy_done = sem("sy_done")
        sy_copied = sem("sy_copied")
        x_again = sem("x_again")
        xe_loaded = [sem(f"xe_loaded{i}") for i in range(WBUF)]
        we_loaded = [sem(f"we_loaded{i}") for i in range(WBUF)]
        xe_turned = sem("xe_turned")
        xe_hi_ready = sem("xe_hi_ready")
        xe_lo_ready = sem("xe_lo_ready")
        we_hi_ready = sem("we_hi_ready")
        we_lo_ready = sem("we_lo_ready")
        gu_done = sem("gu_done")
        gu_low_ready = sem("gu_low_ready")
        gu_summed = sem("gu_summed")
        gate_ready = sem("gate_ready")
        hid_ready = sem("hid_ready")
        he_hi_ready = sem("he_hi_ready")
        he_lo_ready = sem("he_lo_ready")
        y_done = sem("y_done")
        y_copied = sem("y_copied")
        y_stored = [sem(f"y_stored{i}") for i in range(WBUF)]

        def duos(eng, step, late):
            for d in range(2 * WBUF):
                step(d, d % WBUF, d // WBUF)
            with eng.Fori(2, DUOS // WBUF - 1) as j:
                for i in range(WBUF):
                    step(WBUF * j + i, i, j)
            for d in range(DUOS - WBUF, DUOS + late):
                step(d, d % WBUF, d // WBUF)

        def on(d, lag):
            return not isinstance(d, int) or 0 <= d - lag < DUOS

        assert DUOS // WBUF == TILES

        with nc.Block() as block:
            @block.sync
            def _(sp):
                for i in range(2):
                    sp.wait_ge(rows_sent[i], 16 * SEND * B)
                slots_of = slot_x.rearrange("(j k p) d -> j p k d", k=2, p=P)

                def step(d, i, j):
                    if on(d, 4):
                        sp.wait_ge(xe_turned, d - 3)
                    src = slots_of[d] if isinstance(d, int) else slots_of[bass.ds(d, 1)].rearrange("j p k d -> p (j k) d")
                    sp.dma_start(x_in[:, i, :, :], src).then_inc(xe_loaded[i], 16)
                    if isinstance(d, int) and d == 2 * WBUF - 1:
                        sp.dma_start(x_back[:, :, :], x_rows).then_inc(x_again, 16)
                    if on(d, 4):
                        sp.wait_ge(we_lo_ready, d - 3)
                    pair = owners[0:1, 2 * d:2 * d + 2] if isinstance(d, int) else owners[0:1, bass.ds(2 * d, 2)]
                    _, experts_of = nc.values_load_multi_w_load_instructions(pair, engines=(mybir.EngineType.SP,), min_val=0, max_val=E - 1)
                    for k, e in enumerate(experts_of):
                        sp.dma_start(we_raw[:, i, k, :], w_expert[bass.ds(e, 1)].rearrange("e p n -> p (e n)")).then_inc(we_loaded[i], 16)
                duos(sp, step, 0)

            @block.tensor
            def _(pe):
                def shared_up(dst, at, done):
                    for c in range(KC):
                        w = slice(at + c * SHC, at + (c + 1) * SHC)
                        nc.tensor.matmul(dst[:, :], xh[:, c, :], sh_hi[:, w], start=(c == 0), stop=False)
                        nc.tensor.matmul(dst[:, :], xh[:, c, :], sh_lo[:, w], start=False, stop=False)
                        last = nc.tensor.matmul(dst[:, :], xl[:, c, :], sh_hi[:, w], start=False, stop=(c == KC - 1))
                    last.then_inc(done, 1)

                def shared_part(i, j, early):
                    if i == 0:
                        pe.wait_ge(xh_ready, j + 1)
                        pe.wait_ge(xl_ready, j + 1)
                        if early:
                            pe.wait_ge(sh_lo_ready, 1)
                        else:
                            pe.wait_ge(hs_hi_ready, j)
                            pe.wait_ge(hs_lo_ready, j)
                        shared_up(ps_sg, 0, sg_done)
                    if i == 1:
                        if early:
                            pe.wait_ge(sh_lo_ready, 2)
                        else:
                            pe.wait_ge(sy_copied, j)
                        shared_up(ps_su, KC * SHC, su_done)
                    if i == 2:
                        pe.wait_ge(sgate_ready, j + 1)
                        pe.wait_ge(shid_ready, j + 1)
                        for h in range(SH):
                            last = nc.tensor.transpose(ps_sg[:, h * P:(h + 1) * P], hid_s[:, h * P:(h + 1) * P], ident[:, :])
                        last.then_inc(shid_turned, 1)
                    if i == 3:
                        if early:
                            pe.wait_ge(sh_lo_ready, 3)
                        pe.wait_ge(hs_hi_ready, j + 1)
                        pe.wait_ge(hs_lo_ready, j + 1)
                        for h in range(SH):
                            w = slice(2 * KC * SHC + h * D, 2 * KC * SHC + (h + 1) * D)
                            nc.tensor.matmul(ps_su[:, 0:D], hs_hi[:, h, :], sh_hi[:, w], start=(h == 0), stop=False)
                            nc.tensor.matmul(ps_su[:, 0:D], hs_hi[:, h, :], sh_lo[:, w], start=False, stop=False)
                            last = nc.tensor.matmul(ps_su[:, 0:D], hs_lo[:, h, :], sh_hi[:, w], start=False, stop=(h == SH - 1))
                        last.then_inc(sy_done, 1)

                def step(d, i, j):
                    n = i % 2
                    if on(d, 0):
                        pe.wait_ge(xe_loaded[i], 16 * (j + 1))
                        if on(d, 2):
                            pe.wait_ge(xe_hi_ready, d - 1)
                            pe.wait_ge(xe_lo_ready, d - 1)
                        for c in range(KC):
                            for k in range(2):
                                last = nc.tensor.transpose(ps_x[n][:, c, k * P:(k + 1) * P], x_in[:, i, k, c * P:(c + 1) * P], ident[:, :])
                        last.then_inc(xe_turned, 1)
                    if on(d, 3):
                        pe.wait_ge(he_hi_ready, d - 2)
                        pe.wait_ge(he_lo_ready, d - 2)
                        if on(d, 5):
                            pe.wait_ge(y_copied, d - 4)
                        w = (i + 1) % WBUF
                        for k in range(2):
                            cols = slice(k * P, (k + 1) * P)
                            dst = ps_y[1 - n][:, k, :]
                            nc.tensor.matmul(dst, he[:, 1 - n, cols], we_hi[:, w, k, DOWN:WE], start=True, stop=False)
                            last = nc.tensor.matmul(dst, he[0:F, 1 - n, cols], we_lo[0:F, w, k, DOWN:WE], start=False, stop=True)
                        last.then_inc(y_done, 1)
                    if on(d, 1):
                        pe.wait_ge(xe_hi_ready, d)
                        pe.wait_ge(xe_lo_ready, d)
                        pe.wait_ge(we_hi_ready, d)
                        pe.wait_ge(we_lo_ready, d)
                        if on(d, 3):
                            pe.wait_ge(gu_summed, d - 2)
                        w = (i - 1) % WBUF
                        for k in range(2):
                            cols = slice(k * P, (k + 1) * P)
                            dst = ps_gu[1 - n]
                            for c in range(KC):
                                of = slice(c * 2 * F, (c + 1) * 2 * F)
                                nc.tensor.matmul(dst[:, k, :, :], we_hi[:, w, k, of], xe[:, 1 - n, c, :, cols], start=(c == 0), stop=False)
                                last = nc.tensor.matmul(dst[:, k, 0, :], we_lo[:, w, k, of], xe[:, 1 - n, c, 0, cols], start=False, stop=(c == KC - 1))
                        last.then_inc(gu_done, 1)
                    if on(d, 0):
                        shared_part(i, j, isinstance(j, int) and j == 0)
                duos(pe, step, 3)

            @block.scalar
            def _(act):
                act.wait_ge(sh_loaded, 16)
                for w in SH_PARTS:
                    nc.scalar.activation(sh_hi[:, w], sh_raw[:, w], ACT.Copy).then_inc(sh_hi_ready, 1)

                def split_weights(d, i, j):
                    act.wait_ge(we_loaded[i], 32 * (j + 1))
                    if on(d, 4):
                        act.wait_ge(y_done, d - 3)
                    nc.scalar.activation(we_hi[:, i, :, :], we_raw[:, i, :, :], ACT.Copy).then_inc(we_hi_ready, 1)

                split_weights(0, 0, 0)

                def step(d, i, j):
                    n = i % 2
                    early = isinstance(j, int) and j == 0
                    if i == 0 and on(d, 0):
                        if not early:
                            act.wait_ge(su_done, j)
                        cols = slice(j * P, (j + 1) * P) if isinstance(j, int) else bass.ds(j * P, P)
                        nc.scalar.activation(xh[:, :, :], xn_t[:, :, cols], ACT.Copy).then_inc(xh_ready, 1)
                    if i == 1 and on(d, 0):
                        act.wait_ge(sg_done, j + 1)
                        if not early:
                            act.wait_ge(shid_ready, j)
                        nc.scalar.activation(gate_s[:, :], ps_sg[:, :], ACT.Silu).then_inc(sgate_ready, 1)
                    if i == 3 and on(d, 0):
                        act.wait_ge(shid_turned, j + 1)
                        if not early:
                            act.wait_ge(sy_done, j)
                        nc.scalar.activation(hs_hi[:, :, :].rearrange("p h t -> p (h t)"), ps_sg[:, :], ACT.Copy).then_inc(hs_hi_ready, 1)
                    if on(d, 2):
                        act.wait_ge(gu_summed, d - 1)
                        if on(d, 4):
                            act.wait_ge(hid_ready, d - 3)
                        nc.scalar.activation(gate_e[F:P, n, :], gu_sum[0:F, n, :, :].rearrange("p k t -> p (k t)"), ACT.Silu).then_inc(gate_ready, 1)
                    if on(d, 0):
                        act.wait_ge(xe_turned, d + 1)
                        nc.scalar.activation(xe[:, n, :, 0, :], ps_x[n][:, :, :], ACT.Copy).then_inc(xe_hi_ready, 1)
                    if on(d, 2):
                        act.wait_ge(hid_ready, d - 1)
                        if on(d, 4):
                            act.wait_ge(y_done, d - 3)
                        nc.scalar.activation(he[0:F, n, :], hid_e[:, n, :], ACT.Copy).then_inc(he_hi_ready, 1)
                    if on(d, 1):
                        act.wait_ge(gu_done, d)
                        nc.scalar.activation(gu_low[:, 1 - n, :, :], ps_gu[1 - n][:, :, 1, :], ACT.Copy).then_inc(gu_low_ready, 1)
                    if on(d, -1):
                        split_weights(d + 1, (i + 1) % WBUF, j + (i + 1) // WBUF)
                    if on(d, 4):
                        act.wait_ge(y_copied, d - 3)
                        dst = slot_y.rearrange("(j k p) d -> j p k d", k=2, p=P)
                        dst = dst[d - 4] if isinstance(d, int) else dst[bass.ds(d - 4, 1)].rearrange("j p k d -> p (j k) d")
                        act.dma_start(dst, y_out[:, i, :, :]).then_inc(y_stored[i], 16)
                duos(act, step, 4)
                for i in range(WBUF):
                    act.wait_ge(y_stored[i], 16 * DUOS // WBUF)

            @block.gpsimd
            def _(pool):
                def step(d, i, j):
                    pool.wait_ge(we_hi_ready, d + 1)
                    nc.gpsimd.tensor_tensor(we_lo[:, i, :, :], we_raw[:, i, :, :], we_hi[:, i, :, :].bitcast(F32), ALU.subtract).then_inc(we_lo_ready, 1)
                out_rstd(pool, B)
                duos(pool, step, 0)

            @block.vector
            def _(dve):
                out_moments(dve, B)
                for k, w in enumerate(SH_PARTS):
                    dve.wait_ge(sh_hi_ready, k + 1)
                    nc.vector.tensor_tensor(sh_lo[:, w], sh_raw[:, w], sh_hi[:, w].bitcast(F32), ALU.subtract).then_inc(sh_lo_ready, 1)

                def step(d, i, j):
                    n = i % 2
                    early = isinstance(j, int) and j == 0
                    if i == 0 and on(d, 0):
                        dve.wait_ge(xh_ready, j + 1)
                        cols = slice(j * P, (j + 1) * P) if isinstance(j, int) else bass.ds(j * P, P)
                        nc.vector.tensor_tensor(xl[:, :, :], xn_t[:, :, cols], xh[:, :, :].bitcast(F32), ALU.subtract).then_inc(xl_ready, 1)
                    if i == 2 and on(d, 0):
                        dve.wait_ge(su_done, j + 1)
                        dve.wait_ge(sgate_ready, j + 1)
                        if not early:
                            dve.wait_ge(shid_turned, j)
                        nc.vector.tensor_tensor(hid_s[:, :], ps_su[:, :], gate_s[:, :], ALU.mult).then_inc(shid_ready, 1)
                    if i == 3 and on(d, 0):
                        dve.wait_ge(hs_hi_ready, j + 1)
                        nc.vector.tensor_tensor(hs_lo[:, :, :].rearrange("p h t -> p (h t)"), ps_sg[:, :],
                                                hs_hi[:, :, :].rearrange("p h t -> p (h t)").bitcast(F32), ALU.subtract).then_inc(hs_lo_ready, 1)
                    if on(d, 2):
                        dve.wait_ge(gate_ready, d - 1)
                        if on(d, 4):
                            dve.wait_ge(he_lo_ready, d - 3)
                            dve.wait_ge(he_hi_ready, d - 3)
                        nc.vector.tensor_tensor(hid_e[:, n, :], gu_sum[F:P, n, :, :].rearrange("p k t -> p (k t)"), gate_e[F:P, n, :], ALU.mult).then_inc(hid_ready, 1)
                    if on(d, 0):
                        dve.wait_ge(xe_hi_ready, d + 1)
                        nc.vector.tensor_tensor(xe[:, n, :, 1, :], ps_x[n][:, :, :], xe[:, n, :, 0, :].bitcast(F32), ALU.subtract).then_inc(xe_lo_ready, 1)
                    if on(d, 2):
                        dve.wait_ge(he_hi_ready, d - 1)
                        nc.vector.tensor_tensor(he[F:P, n, :], hid_e[:, n, :], he[0:F, n, :].bitcast(F32), ALU.subtract).then_inc(he_lo_ready, 1)
                    if on(d, 1):
                        dve.wait_ge(gu_low_ready, d)
                        if on(d, 3):
                            dve.wait_ge(gate_ready, d - 2)
                            dve.wait_ge(hid_ready, d - 2)
                        nc.vector.tensor_tensor(gu_sum[:, 1 - n, :, :], ps_gu[1 - n][:, :, 0, :], gu_low[:, 1 - n, :, :], ALU.add).then_inc(gu_summed, 1)
                    if on(d, 3):
                        dve.wait_ge(y_done, d - 2)
                        if on(d, 7):
                            dve.wait_ge(y_stored[(i + 1) % WBUF], 16 * (j if i == WBUF - 1 else j - 1))
                        nc.vector.tensor_copy(y_out[:, (i + 1) % WBUF, :, :], ps_y[1 - n][:, :, :]).then_inc(y_copied, 1)
                    if i == 0 and not early:
                        dve.wait_ge(sy_done, j)
                        rows = slice(j - 1, j) if isinstance(j, int) else bass.ds(j - 1, 1)
                        nc.vector.tensor_copy(shared_y[:, rows, :].rearrange("p t d -> p (t d)"), ps_su[:, 0:D]).then_inc(sy_copied, 1)
                    if isinstance(d, int) and d == WBUF:
                        norm_out(dve, B)
                        scale_out(dve, B)
                duos(dve, step, 3)
        experts_ps.close()
        experts.close()

        picks = sbuf(tail, "picks", [P, GT, TOPK, D])
        slot_now = sbuf(tail, "slot_now", [P, GT, TOPK], U32)
        gate_now = sbuf(tail, "gate_now", [P, GT, TOPK])
        pace = sbuf(tail, "pace", [P, GT])
        total = sbuf(tail, "total", [P, GT, D])

        slots_now = sem("slots_now")
        gates_now = sem("gates_now")
        picked_in = [sem(f"picked_in{i}") for i in range(GT)]
        sum_step = sem("sum_step")
        paced = sem("paced")
        summed = sem("summed")
        silu_done = sem("silu_done")
        gated = sem("gated")
        added = sem("added")
        out_stored = [sem(f"out_stored{i}") for i in range(GT)]

        def groups(eng, body):
            for i in range(GT):
                body(0, i, True, False)
            with eng.Fori(1, NG - 1) as g:
                for i in range(GT):
                    body(g, i, False, False)
            for i in range(GT):
                body(NG - 1, i, False, True)

        with nc.Block() as block:
            @block.sync
            def _(sp):
                def body(g, i, first_g, last_g):
                    sp.wait_ge(added, GT * g + i + 1)
                    tile = bass.ds(GT * g + i, 1) if not isinstance(g, int) else slice(GT * g + i, GT * g + i + 1)
                    sp.dma_start(out_rows[:, tile, :], total[:, i:i + 1, :]).then_inc(out_stored[i], 16)
                groups(sp, body)
                for i in range(GT):
                    sp.wait_ge(out_stored[i], 16 * NG)

            @block.gpsimd
            def _(pool):
                def body(g, i, first_g, last_g):
                    pool.wait_ge(slots_now, GT * g + i + 1)
                    if not first_g:
                        pool.wait_ge(summed, GT * (g - 1) + i + 1)
                    if not last_g:
                        if not isinstance(g, int):
                            pool.wait_ge(paced, GT * (g - 1) + i + 1)
                        nc.gpsimd.tensor_tensor(pace[:, i:i + 1], minus_half[:, 0:1], minus_half[:, 1:2], ALU.add).then_inc(paced, 1)
                    for k in range(TOPK):
                        nc.gpsimd.indirect_dma_start(picks[:, i, k, :], None, slot_y, bass.IndirectOffsetOnAxis(slot_now[:, i, k:k + 1], 0)).then_inc(picked_in[i], 16)
                groups(pool, body)

            @block.scalar
            def _(act):
                def body(g, i, first_g, last_g):
                    act.wait_ge(summed, GT * g + i + 1)
                    nc.scalar.activation(total[:, i, :], total[:, i, :], ACT.Silu).then_inc(silu_done, 1)
                groups(act, body)

            @block.vector
            def _(dve):
                for i in range(GT):
                    nc.vector.tensor_copy(slot_now[:, i, :], slots[:, i, :]).then_inc(slots_now, 1)
                    nc.vector.tensor_copy(gate_now[:, i, :], gates[:, i, :]).then_inc(gates_now, 1)
                dve.wait_ge(x_again, 16)

                def tile_of(g, i):
                    t = GT * g + i
                    return slice(t, t + 1) if isinstance(g, int) else bass.ds(t, 1)

                def body(g, i, first_g, last_g):
                    dve.wait_ge(picked_in[i], 16 * TOPK * (g + 1))
                    if not last_g:
                        nc.vector.tensor_copy(slot_now[:, i:i + 1, :], slots[:, tile_of(g + 1, i), :]).then_inc(slots_now, 1)
                    dve.wait_ge(gates_now, GT * g + i + 1)
                    if not first_g:
                        dve.wait_ge(out_stored[i], 16 * g)
                    for k in range(TOPK):
                        base = shared_y[:, tile_of(g, i), :].rearrange("p t d -> p (t d)") if k == 0 else total[:, i, :]
                        ins = nc.vector.scalar_tensor_tensor(total[:, i, :], picks[:, i, k, :], gate_now[:, i, k:k + 1], base, ALU.mult, ALU.add)
                        if k < TOPK - 1:
                            ins.then_inc(sum_step, 1)
                            dve.wait_ge(sum_step, (TOPK - 1) * (GT * g + i) + k + 1)
                    ins.then_inc(summed, 1)
                    if not last_g:
                        dve.wait_ge(summed, GT * g + i + 1)
                        nc.vector.tensor_copy(gate_now[:, i:i + 1, :], gates[:, tile_of(g + 1, i), :]).then_inc(gates_now, 1)
                    dve.wait_ge(silu_done, GT * g + i + 1)
                    nc.vector.tensor_tensor(total[:, i:i + 1, :], total[:, i:i + 1, :], attn_out[:, tile_of(g, i), :], ALU.mult).then_inc(gated, 1)
                    dve.wait_ge(gated, GT * g + i + 1)
                    nc.vector.tensor_tensor(total[:, i:i + 1, :], total[:, i:i + 1, :], x_back[:, tile_of(g, i), :], ALU.add).then_inc(added, 1)
                groups(dve, body)
        tail.close()


def kernel(L0_attn_x, L0_attn_g_norm, L0_attn_Wq, L0_attn_Wkv, L0_attn_Wout, L0_attn_g_out, L0_ffn_Wr,
           L0_ffn_router_bias, L0_ffn_affinity, L0_ffn_te_W1, L0_ffn_te_b1, L0_ffn_te_W2, L0_ffn_te_b2,
           L0_ffn_Wg, L0_ffn_Wu, L0_ffn_Wd, L0_ffn_Sg, L0_ffn_Su, L0_ffn_Sd):
    import numpy as np
    import concourse.bacc as bacc
    from concourse import mybir as mb
    from concourse.bass_utils import run_bass_kernel_spmd as run

    E, D, F = L0_ffn_Wg.shape
    NS, _, H = L0_ffn_Sg.shape
    C = D // 128

    def by_chunk(w, n):
        return w.reshape(-1, C, 128, n).transpose(0, 2, 1, 3).reshape(-1, 128, C * n)

    def side_by_side(w):
        return w.transpose(1, 0, 2).reshape(D, NS * H)

    shared = np.concatenate([by_chunk(side_by_side(L0_ffn_Sg), NS * H)[0], by_chunk(side_by_side(L0_ffn_Su), NS * H)[0],
                             L0_ffn_Sd.reshape(-1, 128, D).transpose(1, 0, 2).reshape(128, -1)], axis=1)
    arrays = {
        "x": L0_attn_x, "wq": L0_attn_Wq, "wkv": L0_attn_Wkv, "wout": L0_attn_Wout,
        "g_norm": L0_attn_g_norm.reshape(D // 128, 128).T, "g_out": L0_attn_g_out,
        "wr_t": L0_ffn_Wr.T, "r_bias": L0_ffn_router_bias, "aff_t": L0_ffn_affinity.T,
        "w1_t": L0_ffn_te_W1.T, "b1": L0_ffn_te_b1[:, None], "w2_t": L0_ffn_te_W2.T, "b2": L0_ffn_te_b2,
        "w_expert": np.concatenate([by_chunk(np.concatenate([L0_ffn_Wg, L0_ffn_Wu], axis=2), 2 * F),
                                    np.concatenate([L0_ffn_Wd, L0_ffn_Wd], axis=1)], axis=2),
        "w_shared": shared,
        "ident_in": np.eye(128, dtype=np.float32), "tri_in": np.triu(np.ones((128, 128), np.float32), 1),
        "iota_in": np.arange(128, dtype=np.float32),
    }
    arrays = {k: np.ascontiguousarray(v) for k, v in arrays.items()}
    nc = bacc.Bacc("TRN2", target_bir_lowering=False, num_devices=1)
    args = [nc.dram_tensor(k, v.shape, mb.dt.from_np(v.dtype), kind="ExternalInput").ap() for k, v in arrays.items()]
    out = nc.dram_tensor("out", L0_attn_x.shape, mb.dt.float32, kind="ExternalOutput").ap()
    build(nc, *args, out)
    r = run(nc, [arrays], core_ids=[0])
    return r.results[0]["out"]
```
